# Optimizing a Trainium2 kernel written in Bass

```python
import numpy as np
import jax
import jax.numpy as jnp

def _softmax(x, axis=-1):
    return jax.nn.softmax(x, axis=axis)

def _gelu(x):
    return jax.nn.gelu(x, approximate=True)

def _silu(x):
    return jax.nn.silu(x)

def _sigmoid(x):
    return jax.nn.sigmoid(x)

def _layernorm(x, axis=-1, eps=1e-05):
    m = jnp.mean(x, axis=axis, keepdims=True)
    v = jnp.var(x, axis=axis, keepdims=True)
    return (x - m) / jnp.sqrt(v + eps)

def _scatter_add(tgt, idx, src, axis=0):
    return tgt.at[idx].add(src)

def _segment_sum(src, seg, n):
    return jax.ops.segment_sum(src, seg, n)
kernel_name = 'mk_gnn_preln_d2_gnn_r8_274ebe'

def setup_inputs(seed: int=0):
    np.random.seed(seed)
    _w = jnp.asarray

    def _rec_inputs():
        import jax
        import jax.numpy as jnp
        _gk = jax.random.key(seed)
        x = -0.000202 + 1 * jax.random.normal(jax.random.fold_in(_gk, 1), (6250, 128), jnp.float32)
        _s = jax.random.randint(jax.random.fold_in(_gk, 2), (100000,), 0, 6250, jnp.int32)
        _d = jax.random.randint(jax.random.fold_in(_gk, 3), (100000,), 0, 6250, jnp.int32)
        _loop = jnp.arange(6250, dtype=jnp.int32)
        src = jnp.concatenate([_s, _d, _loop])
        dst = jnp.concatenate([_d, _s, _loop])
        _o = jnp.argsort(dst, stable=True)
        src = src[_o]
        dst = dst[_o]
        edge_attr_128 = -5.16925e-05 + 1.00005 * jax.random.normal(jax.random.fold_in(_gk, 13), (206250, 128), jnp.float32)
        edge_attr_64 = -8.16379e-05 + 0.999858 * jax.random.normal(jax.random.fold_in(_gk, 14), (206250, 64), jnp.float32)
        return (x, src, dst, edge_attr_128, edge_attr_64)
    x, src, dst, edge_attr_128, edge_attr_64 = _rec_inputs()

    def _L0_gnn_setup():
        import jax, jax.numpy as jnp
        import numpy as np
        N_NODES = 6250
        N_EDGES = 100000
        D = 128
        L = 3
        BN_EPS = 1e-05

        def _bn(h, gamma, beta):
            m = h.mean(axis=0)
            v = h.var(axis=0)
            return gamma * (h - m) * jax.lax.rsqrt(v + BN_EPS) + beta
        key = jax.random.key(seed)
        ks = jax.random.split(key, 12)
        x = jax.random.normal(ks[0], (N_NODES, D), dtype=jnp.float32)
        edge_index = jax.random.randint(ks[1], (2, N_EDGES), 0, N_NODES, dtype=jnp.int64)
        edge_attr = jax.random.normal(ks[2], (N_EDGES, D), dtype=jnp.float32)
        batch = jnp.zeros((N_NODES,), dtype=jnp.int64)
        s = 1.0 / np.sqrt(D)
        W1 = jax.random.uniform(ks[3], (L, D, D), jnp.float32, -s, s)
        b1 = jax.random.uniform(ks[4], (L, D), jnp.float32, -s, s)
        g_mlp = jnp.ones((L, D), jnp.float32)
        be_mlp = jnp.zeros((L, D), jnp.float32)
        W2 = jax.random.uniform(ks[5], (L, D, D), jnp.float32, -s, s)
        b2 = jax.random.uniform(ks[6], (L, D), jnp.float32, -s, s)
        g_out = jnp.ones((L, D), jnp.float32)
        be_out = jnp.zeros((L, D), jnp.float32)
        return {'x': x, 'edge_index': edge_index, 'edge_attr': edge_attr, 'batch': batch, 'W1': W1, 'b1': b1, 'g_mlp': g_mlp, 'be_mlp': be_mlp, 'W2': W2, 'b2': b2, 'g_out': g_out, 'be_out': be_out}
    _L0_gnn_all = _L0_gnn_setup()
    _L0_gnn_in = {k: v for k, v in _L0_gnn_all.items() if k in ('W1', 'b1', 'g_mlp', 'be_mlp', 'W2', 'b2', 'g_out', 'be_out')}
    del _L0_gnn_all

    def _L1_gnn_setup():
        import jax, jax.numpy as jnp
        import numpy as np
        N_NODES = 12500
        N_EDGES = 200000
        NDIM_IN = 128
        EDIMS = 64
        NDIM_OUT = 128
        NUM_HEADS = 4
        HEAD_DIM = NDIM_OUT // NUM_HEADS
        key = jax.random.key(seed)
        ks = jax.random.split(key, 10)
        in_dim = NDIM_IN + EDIMS
        b1 = float(np.sqrt(6.0 / (in_dim + NDIM_OUT)))
        b2 = float(np.sqrt(6.0 / (NDIM_OUT + NDIM_OUT)))
        bav = float(np.sqrt(6.0 / (NUM_HEADS + HEAD_DIM)))
        return {'nfeats': jax.random.normal(ks[0], (N_NODES, NDIM_IN), dtype=jnp.float32), 'efeats': jax.random.normal(ks[1], (N_EDGES, EDIMS), dtype=jnp.float32), 'src': jax.random.randint(ks[2], (N_EDGES,), 0, N_NODES, dtype=jnp.int32), 'dst': jax.random.randint(ks[3], (N_EDGES,), 0, N_NODES, dtype=jnp.int32), 'W_proj_w': jax.random.uniform(ks[4], (NDIM_OUT, in_dim), jnp.float32, -b1, b1), 'W_proj_b': jnp.zeros((NDIM_OUT,), jnp.float32), 'attn_vec': jax.random.uniform(ks[5], (NUM_HEADS, HEAD_DIM), jnp.float32, -bav, bav), 'W_out_w': jax.random.uniform(ks[6], (NDIM_OUT, NDIM_OUT), jnp.float32, -b2, b2), 'W_out_b': jnp.zeros((NDIM_OUT,), jnp.float32), 'ln_gamma': jnp.ones((NDIM_OUT,), jnp.float32), 'ln_beta': jnp.zeros((NDIM_OUT,), jnp.float32)}
    _L1_gnn_all = _L1_gnn_setup()
    _L1_gnn_in = {k: v for k, v in _L1_gnn_all.items() if k in ('W_proj_w', 'W_proj_b', 'attn_vec', 'W_out_w', 'W_out_b', 'ln_gamma', 'ln_beta')}
    del _L1_gnn_all
    return {'x': x, 'src': src, 'dst': dst, 'edge_attr_128': edge_attr_128, 'edge_attr_64': edge_attr_64, 'L0_gnn_W1': _L0_gnn_in['W1'], 'L0_gnn_b1': _L0_gnn_in['b1'], 'L0_gnn_g_mlp': _L0_gnn_in['g_mlp'], 'L0_gnn_be_mlp': _L0_gnn_in['be_mlp'], 'L0_gnn_W2': _L0_gnn_in['W2'], 'L0_gnn_b2': _L0_gnn_in['b2'], 'L0_gnn_g_out': _L0_gnn_in['g_out'], 'L0_gnn_be_out': _L0_gnn_in['be_out'], 'L1_gnn_W_proj_w': _L1_gnn_in['W_proj_w'], 'L1_gnn_W_proj_b': _L1_gnn_in['W_proj_b'], 'L1_gnn_attn_vec': _L1_gnn_in['attn_vec'], 'L1_gnn_W_out_w': _L1_gnn_in['W_out_w'], 'L1_gnn_W_out_b': _L1_gnn_in['W_out_b'], 'L1_gnn_ln_gamma': _L1_gnn_in['ln_gamma'], 'L1_gnn_ln_beta': _L1_gnn_in['ln_beta']}

def reference(x, src, dst, edge_attr_128, edge_attr_64, L0_gnn_W1, L0_gnn_b1, L0_gnn_g_mlp, L0_gnn_be_mlp, L0_gnn_W2, L0_gnn_b2, L0_gnn_g_out, L0_gnn_be_out, L1_gnn_W_proj_w, L1_gnn_W_proj_b, L1_gnn_attn_vec, L1_gnn_W_out_w, L1_gnn_W_out_b, L1_gnn_ln_gamma, L1_gnn_ln_beta):
    import jax
    import jax.numpy as jnp

    def _L0_gnn_ref(x, edge_index, edge_attr, batch, W1, b1, g_mlp, be_mlp, W2, b2, g_out, be_out):
        import jax, jax.numpy as jnp
        import numpy as np
        N_NODES = 6250
        N_EDGES = 100000
        D = 128
        L = 3
        BN_EPS = 1e-05

        def _bn(h, gamma, beta):
            m = h.mean(axis=0)
            v = h.var(axis=0)
            return gamma * (h - m) * jax.lax.rsqrt(v + BN_EPS) + beta
        src, dst = (edge_index[0], edge_index[1])
        for i in range(L):
            msg = jax.nn.relu(x[src] + edge_attr)
            aggr = jax.ops.segment_sum(msg, dst, num_segments=N_NODES)
            h = x + aggr
            h = h @ W1[i] + b1[i]
            h = jax.nn.relu(_bn(h, g_mlp[i], be_mlp[i]))
            h = h @ W2[i] + b2[i]
            h = _bn(h, g_out[i], be_out[i])
            if i != L - 1:
                h = jax.nn.relu(h)
            x = h
        return x

    def _L1_gnn_ref(nfeats, efeats, src, dst, W_proj_w, W_proj_b, attn_vec, W_out_w, W_out_b, ln_gamma, ln_beta):
        import jax, jax.numpy as jnp
        import numpy as np
        N_NODES = 12500
        N_EDGES = 200000
        NDIM_IN = 128
        EDIMS = 64
        NDIM_OUT = 128
        NUM_HEADS = 4
        HEAD_DIM = NDIM_OUT // NUM_HEADS
        N = nfeats.shape[0]
        H, D = attn_vec.shape
        x = jnp.concatenate([nfeats[src], efeats], axis=1)
        x_proj = (x @ W_proj_w.T + W_proj_b).reshape(-1, H, D)
        e = jnp.sum(x_proj * attn_vec, axis=-1)
        emax = jax.ops.segment_max(e, dst, num_segments=N)
        ex = jnp.exp(e - emax[dst])
        denom = jax.ops.segment_sum(ex, dst, num_segments=N)
        alpha = ex / denom[dst]
        m = (x_proj * alpha[:, :, None]).reshape(-1, H * D)
        h_neigh = jax.ops.segment_sum(m, dst, num_segments=N)
        h = jax.nn.relu((h_neigh + nfeats) @ W_out_w.T + W_out_b)
        mu = jnp.mean(h, axis=-1, keepdims=True)
        var = jnp.mean((h - mu) ** 2, axis=-1, keepdims=True)
        return (h - mu) * jax.lax.rsqrt(var + 1e-05) * ln_gamma + ln_beta
    edge_index = jnp.stack([src, dst])
    batch0 = jnp.zeros((6250,), jnp.int32)
    h = jnp.maximum(_layernorm(x, axis=-1), 0.0)
    x = x + _L0_gnn_ref(h, edge_index, edge_attr_128, batch0, L0_gnn_W1, L0_gnn_b1, L0_gnn_g_mlp, L0_gnn_be_mlp, L0_gnn_W2, L0_gnn_b2, L0_gnn_g_out, L0_gnn_be_out)
    h = jnp.maximum(_layernorm(x, axis=-1), 0.0)
    x = x + _L1_gnn_ref(h, edge_attr_64, src, dst, L1_gnn_W_proj_w, L1_gnn_W_proj_b, L1_gnn_attn_vec, L1_gnn_W_out_w, L1_gnn_W_out_b, L1_gnn_ln_gamma, L1_gnn_ln_beta)
    return x

_drawn_inputs = setup_inputs


def setup_inputs(seed=0):
    import zlib

    import numpy as np

    out = dict(_drawn_inputs(seed))
    spreads = {'L0_gnn_g_mlp': (1.0, 0.2),
     'L0_gnn_be_mlp': (0.0, 0.1),
     'L0_gnn_g_out': (1.0, 0.2),
     'L0_gnn_be_out': (0.0, 0.1),
     'L1_gnn_W_proj_b': (0.0, 0.1),
     'L1_gnn_W_out_b': (0.0, 0.1),
     'L1_gnn_ln_gamma': (1.0, 0.2),
     'L1_gnn_ln_beta': (0.0, 0.1)}
    factors = {}
    for name, (base, spread) in spreads.items():
        noise = np.random.default_rng([zlib.crc32(name.encode()), seed]).standard_normal(out[name].shape)
        drawn = base * np.exp(spread * noise) if base else spread * noise
        out[name] = jnp.asarray(drawn.astype(out[name].dtype))
    for name, factor in factors.items():
        out[name] = (out[name] * factor).astype(out[name].dtype)
    return out
```

```python
import numpy as np
import concourse.bass as bass
from concourse import mybir
from contextlib import ExitStack

F32 = mybir.dt.float32
I32 = mybir.dt.int32
ALU = mybir.AluOpType
ACT = mybir.ActivationFunctionType
AX = mybir.AxisListType

P = 128
EPS = 1e-5
BIG = 1.0e38


class Link:

    def __init__(self, engine, sem, start=0):
        self.engine, self.sem, self.start, self.n = engine, sem, start, 0

    def step(self, instruction):
        instruction.then_inc(self.sem, 1)
        self.n += 1
        self.engine.wait_ge(self.sem, self.start + self.n)


def gnn_program(nc, x, src, dst, ea128, ea64, W1, b1, g_mlp, be_mlp, W2, b2, g_out, be_out,
                Wproj, bproj, attn, Wout, bout, gamma, beta, out):
    N, D = x.shape
    E = ea128.shape[0]
    EF = ea64.shape[1]
    L = W1.shape[0]
    H, HD = attn.shape
    assert D == P and H * HD == P and EF * 2 == P

    J = 8
    GE = J * P
    G = -(-E // GE)
    G += G % 2
    PAIRS = G // 2
    DUP = G * GE - E
    assert 0 <= DUP < GE
    DP, DJ = DUP // J, DUP % J
    WIN = 64
    NT = -(-N // P)
    NP = NT * P
    NLAST = N - (NT - 1) * P
    chunks = [(c, min(512, NP - c)) for c in range(0, NP, 512)]
    CH = len(chunks)
    real = [min(w, N - c) for c, w in chunks]
    NB = 4
    SP_ = max(d for d in range(1, P + 1) if E % d == 0)
    SF = E // SP_
    SA = SP_ // 16 * 16
    AW = max(NP + WIN, SF * H)

    def dram(name, shape):
        return nc.dram_tensor(name, shape, F32).ap()

    table = dram("table", (N, D))
    table2 = dram("table2", (N, D))
    xp_d = dram("xp_d", (G * P, J * D))
    lg_d = dram("lg_d", (E, H))
    ex_d = dram("ex_d", (E, H))

    ctx = ExitStack()
    with ctx:
        def sb(name, shape, dt=F32):
            return ctx.enter_context(nc.sbuf_tensor(name, shape, dt))

        def pb(name, shape):
            return ctx.enter_context(nc.psum_tensor(name, shape, F32))

        def sem(name):
            return ctx.enter_context(nc.semaphore(name))

        acc = sb("acc", [P, AW])
        zbuf = sb("zbuf", [P, AW])
        bbuf = sb("bbuf", [P, AW])
        xres = sb("xres", [P, NT, D])
        srci = sb("srci", [P, (G + 2) * J], I32)
        dsti = sb("dsti", [P, G * J], I32)
        dloc = sb("dloc", [P, G * J])
        idx = sb("idx", [P, 2, J], I32)
        gx = sb("gx", [P, 2, GE])
        ea = sb("ea", [P, 2, GE])
        msg = sb("msg", [P, 2, GE])
        hot = sb("hot", [P, 2, J, WIN])
        prod = sb("prod", [P, GE])
        lg = sb("lg", [P, 2, J, H])
        eft = sb("eft", [P, 2, GE // 2])
        win = sb("win", [P, WIN])
        rampi = sb("rampi", [P, P], I32)
        ident = sb("ident", [P, P])
        ones = sb("ones", [1, P])
        tailpos = sb("tailpos", [P, J])
        params = sb("params", [6 * L, D])
        pcols = sb("pcols", [P, 6 * L])
        pl = sb("pl", [P, 6])
        w1 = sb("w1", [P, D])
        w2 = sb("w2", [P, D])
        stats = sb("stats", [P, CH, 6])
        mv = sb("mv", [P, 2])
        std = sb("std", [P, 1])
        scl = sb("scl", [P, 1])
        shf = sb("shf", [P, 1])
        mean = sb("mean", [P, NT])
        var = sb("var", [P, NT])
        wp = sb("wp", [P, D + 2 * EF])
        wo = sb("wo", [P, D])
        wnT = sb("wnT", [P, D])
        we2 = sb("we2", [P, 2, D])
        woT = sb("woT", [P, D])
        bp = sb("bp", [1, D])
        bo = sb("bo", [1, D])
        attnb = sb("attnb", [P, D])
        gamb = sb("gamb", [P, D])
        betb = sb("betb", [P, D])
        dedge = sb("dedge", [SP_, SF + 2], I32)
        cap = sb("cap", [SP_, SF + 1])
        pair = sb("pair", [SP_, 2, H])
        rows = sb("rows", [H, 2, SP_])
        carry = sb("carry", [H, SP_ + 2])
        carried = sb("carried", [SP_, H])
        selh = sb("selh", [H, D])

        wps = [pb(f"wps{i}", [P, 512]) for i in range(2)]
        nps = pb("nps", [P, NB, 512])
        tps = [pb(f"tps{i}", [P, 512]) for i in range(2)]

        accT = acc[:, 0:NP]
        zN = zbuf[:, 0:NP].rearrange("p (t d) -> p t d", d=D)
        bN = bbuf[:, 0:NP].rearrange("p (t d) -> p t d", d=D)
        aN = acc[:, 0:NP].rearrange("p (t d) -> p t d", d=D)

        def edges(g):
            return E - GE if isinstance(g, int) and g == G - 1 else g * GE

        def by_group(t, g, inner):
            return t[bass.ds(edges(g), GE), :].rearrange("(p j) f -> p (j f)", j=inner)

        def node_rows(t, c):
            o, w = chunks[c]
            whole = min(w, N - o) // P
            parts = []
            if whole:
                parts.append((o // P, whole, P, t[o:o + whole * P, :].rearrange("(t p) d -> p t d", p=P)))
            if whole * P < min(w, N - o):
                o += whole * P
                parts.append((o // P, 1, N - o, t[o:N, :].rearrange("(t p) d -> p t d", t=1)))
            return parts

        ROWS = sum(len(node_rows(table, c)) for c in range(CH))

        def layer_norm(v, act, link, s_v, s_a, a0, src3, dst3, tmp3):
            link.step(nc.vector.tensor_reduce(mean[:, :], src3, AX.X, ALU.add))
            link.step(nc.vector.tensor_scalar(mean[:, :], mean[:, :], 1.0 / D, None, ALU.mult))
            link.step(nc.vector.tensor_tensor(dst3, src3, mean[:, :].unsqueeze(2).to_broadcast([P, NT, D]),
                                              ALU.subtract))
            link.step(nc.vector.tensor_tensor(tmp3, dst3, dst3, ALU.mult))
            link.step(nc.vector.tensor_reduce(var[:, :], tmp3, AX.X, ALU.add))
            nc.vector.tensor_scalar(var[:, :], var[:, :], 1.0 / D, EPS, ALU.mult, ALU.add).then_inc(s_v, 1)
            v.wait_ge(s_a, a0 + 1)
            link.step(nc.vector.reciprocal(var[:, :], var[:, :]))
            nc.vector.tensor_tensor(dst3, dst3, var[:, :].unsqueeze(2).to_broadcast([P, NT, D]),
                                    ALU.mult).then_inc(s_v, 1)

        s_x = sem("s_x")
        s_ld = sem("s_ld")
        s_io = sem("s_io")
        s_l0 = sem("s_l0")
        s_v0 = sem("s_v0")
        s_a0 = sem("s_a0")
        s_t0 = sem("s_t0")
        s_e0 = sem("s_e0")
        s_c0 = sem("s_c0")
        LOADS = 19
        s_de = sem("s_de")
        with nc.Block() as block:
            @block.sync
            def _(sp):
                for c in range(CH):
                    for t, k, n, v in node_rows(x, c):
                        if n < P:
                            sp.wait_ge(s_io, 1)
                        sp.dma_start(xres[0:n, t:t + k, :], v).then_inc(s_x, 16)
                for tab, arr in ((srci, src), (dsti, dst)):
                    sp.dma_start(tab[:, 0:(G - 1) * J].rearrange("p (g j) -> p g j", j=J),
                                 arr[0:(G - 1) * GE].rearrange("(g p j) -> p g j", p=P, j=J)).then_inc(s_ld, 16)
                    sp.dma_start(tab[:, (G - 1) * J:G * J],
                                 arr[E - GE:E].rearrange("(p j) -> p j", j=J)).then_inc(s_ld, 16)
                sp.dma_start(srci[:, G * J:(G + 2) * J].rearrange("p (g j) -> p g j", j=J),
                             src[0:2 * GE].rearrange("(g p j) -> p g j", p=P, j=J)).then_inc(s_ld, 16)
                for k, w in enumerate((b1, g_mlp, be_mlp, b2, g_out, be_out)):
                    sp.dma_start(params[k * L:(k + 1) * L, :], w).then_inc(s_ld, 16)
                sp.dma_start(wp[:, 0:D + EF], Wproj).then_inc(s_ld, 16)
                sp.dma_start(wp[:, D + EF:D + 2 * EF], Wproj[:, D:D + EF]).then_inc(s_ld, 16)
                sp.dma_start(wo[:, :], Wout).then_inc(s_ld, 16)
                sp.dma_start(bp[:, :], bproj.unsqueeze(0)).then_inc(s_ld, 16)
                sp.dma_start(bo[:, :], bout.unsqueeze(0)).then_inc(s_ld, 16)
                sp.dma_start(attnb[:, :], attn.rearrange("h d -> (h d)").partition_broadcast(P)).then_inc(s_ld, 16)
                sp.dma_start(gamb[:, :], gamma.partition_broadcast(P)).then_inc(s_ld, 16)
                sp.dma_start(betb[:, :], beta.partition_broadcast(P)).then_inc(s_ld, 16)
                sp.wait_ge(s_io, 2)
                sp.dma_start(dedge[:, 1:SF + 1], dst.rearrange("(p f) -> p f", f=SF)).then_inc(s_de, 16)
                with nc.allow_non_contiguous_dma(reason="one word of each partition"):
                    ends = dst.rearrange("(p f) -> p f", f=SF)
                    sp.dma_start(dedge[1:SP_, 0:1], ends[0:SP_ - 1, SF - 1:SF]).then_inc(s_de, 16)
                    sp.dma_start(dedge[0:SP_ - 1, SF + 1:SF + 2], ends[1:SP_, 0:1]).then_inc(s_de, 16)
                sp.wait_ge(s_ld, 16 * LOADS)
                sp.wait_ge(s_de, 48)
                sp.wait_ge(s_x, 16 * ROWS)

            @block.gpsimd
            def _(p):
                nc.gpsimd.memset(xres[:, NT - 1, :], 0.0).then_inc(s_io, 1)
                nc.gpsimd.memset(dedge[:, :], -1).then_inc(s_io, 1)
                nc.gpsimd.iota(rampi[:, :], [[1, P]], base=0, channel_multiplier=-1).then_inc(s_io, 1)
                nc.gpsimd.iota(win[:, :], [[1, WIN]], base=0, channel_multiplier=0,
                               allow_small_or_imprecise_dtypes=True).then_inc(s_io, 1)
                nc.gpsimd.iota(tailpos[:, :], [[1, J]], base=0, channel_multiplier=J,
                               allow_small_or_imprecise_dtypes=True).then_inc(s_io, 1)
                nc.gpsimd.memset(ones[:, :], 1.0).then_inc(s_io, 1)
                nc.gpsimd.memset(selh[:, :], 1.0).then_inc(s_io, 1)
                p.wait_ge(s_io, 7)
                nc.gpsimd.affine_select(out=selh[:, :], in_=selh[:, :], compare_op=ALU.is_ge, fill=0.0, base=0,
                                        pattern=[[1, D]], channel_multiplier=-HD).then_inc(s_io, 1)
                p.wait_ge(s_io, 8)
                nc.gpsimd.affine_select(out=selh[:, :], in_=selh[:, :], compare_op=ALU.is_ge, fill=0.0,
                                        base=HD - 1, pattern=[[-1, D]], channel_multiplier=HD).then_inc(s_io, 1)

            @block.vector
            def _(v):
                link = Link(v, s_l0)
                v.wait_ge(s_io, 9)
                nc.vector.tensor_scalar(ident[:, :], rampi[:, :], 0.0, None, ALU.is_equal).then_inc(s_c0, 1)
                nc.vector.memset(acc[:, NP:AW], 0.0)
                link.step(nc.vector.memset(we2[:, :, :], 0.0))
                v.wait_ge(s_ld, 16 * LOADS)
                link.step(nc.vector.tensor_copy(dloc[:, :], dsti[:, :]))
                v.wait_ge(s_c0, 1)
                nc.vector.tensor_scalar(tailpos[:, :], tailpos[:, :], float(DUP), 1.0e6,
                                        ALU.is_lt, ALU.mult).then_inc(s_c0, 1)
                v.wait_ge(s_t0, 1)
                link.step(nc.vector.tensor_tensor(
                    dloc[:, :].rearrange("p (g j) -> p g j", j=J), dloc[:, :].rearrange("p (g j) -> p g j", j=J),
                    wps[0][:, 0:G].unsqueeze(2).to_broadcast([P, G, J]), ALU.subtract))
                v.wait_ge(s_c0, 2)
                nc.vector.tensor_tensor(dloc[:, (G - 1) * J:G * J], dloc[:, (G - 1) * J:G * J],
                                        tailpos[:, :], ALU.subtract).then_inc(s_c0, 1)
                v.wait_ge(s_t0, 2)
                nc.vector.tensor_copy(pcols[:, :], wps[1][:, 0:6 * L])
                nc.vector.tensor_copy(wnT[:, :], tps[0][:, 0:P])
                nc.vector.tensor_copy(we2[0:EF, 0, :], tps[0][0:EF, P:2 * P])
                nc.vector.tensor_copy(we2[EF:P, 1, :], tps[0][EF:P, P:2 * P])
                nc.vector.tensor_copy(woT[:, :], tps[0][:, 2 * P:3 * P]).then_inc(s_c0, 1)
                v.wait_ge(s_x, 16 * ROWS)
                layer_norm(v, None, link, s_v0, s_a0, 0, xres[:, :, :], bN, zN)
                for c, (o, w) in enumerate(chunks):
                    v.wait_ge(s_t0, 3 + c)
                    nc.vector.tensor_copy(acc[:, o:o + w], nps[:, c % NB, 0:w]).then_inc(s_e0, 1)

            @block.scalar
            def _(a):
                a.wait_ge(s_v0, 1)
                nc.scalar.activation(var[:, :], var[:, :], ACT.Sqrt).then_inc(s_a0, 1)

            @block.tensor
            def _(pe):
                pe.wait_ge(s_io, 9)
                pe.wait_ge(s_l0, 2)
                firsts = dloc[0:1, :].rearrange("p (g j) -> p g j", j=J)[:, :, 0]
                nc.tensor.matmul(wps[0][:, 0:G], ones[0:1, :], firsts, start=True, stop=True).then_inc(s_t0, 1)
                pe.wait_ge(s_c0, 1)
                pe.wait_ge(s_ld, 16 * LOADS)
                nc.tensor.transpose(wps[1][:, 0:6 * L], params[:, :], ident[0:6 * L, 0:6 * L])
                nc.tensor.transpose(tps[0][:, 0:P], wp[:, 0:D], ident[:, :])
                nc.tensor.transpose(tps[0][:, P:2 * P], wp[:, D:D + 2 * EF], ident[:, :])
                nc.tensor.transpose(tps[0][:, 2 * P:3 * P], wo[:, :], ident[:, :]).then_inc(s_t0, 1)
                pe.wait_ge(s_v0, 2)
                for c, (o, w) in enumerate(chunks):
                    if c >= NB:
                        pe.wait_ge(s_e0, c - NB + 1)
                    for t in range(w // P):
                        last = nc.tensor.transpose(nps[:, c % NB, t * P:(t + 1) * P], bN[:, o // P + t, :],
                                                   ident[:, :])
                    last.then_inc(s_t0, 1)

        s_w = sem("s_w")
        s_rl = sem("s_rl")
        s_tp = sem("s_tp")
        s_st = sem("s_st")
        s_tab = sem("s_tab")
        s_idx = [sem(f"s_idx{i}") for i in range(2)]
        s_gx = [[sem(f"s_gx{i}{h}") for h in range(2)] for i in range(2)]
        s_ea = [sem(f"s_ea{i}") for i in range(2)]
        s_hot = [sem(f"s_hot{i}") for i in range(2)]
        s_add = [sem(f"s_add{i}") for i in range(2)]
        s_msg = [sem(f"s_msg{i}") for i in range(2)]
        s_win = [sem(f"s_win{i}") for i in range(2)]
        s_acc = [sem(f"s_acc{i}") for i in range(2)]
        s_z1 = sem("s_z1")
        s_z1e = sem("s_z1e")
        s_h1 = sem("s_h1")
        s_z2 = sem("s_z2")
        s_z2e = sem("s_z2e")
        s_y = sem("s_y")
        s_bv = sem("s_bv")
        s_ba = sem("s_ba")
        s_l1 = sem("s_l1")
        s_pl = sem("s_pl")
        LINKS = 8
        with nc.Block() as block:
            @block.sync
            def _(sp):
                with sp.Fori(0, L) as l:
                    sp.wait_ge(s_y, l * CH)
                    sp.dma_start(w1[:, :], W1[bass.ds(l, 1), :, :].rearrange("l i o -> (l i) o")).then_inc(s_w, 16)
                    sp.dma_start(w2[:, :], W2[bass.ds(l, 1), :, :].rearrange("l i o -> (l i) o")).then_inc(s_w, 16)
                    for c in range(CH):
                        sp.wait_ge(s_st, l * CH + c + 1)
                        for t, k, n, rows_ in node_rows(table, c):
                            sp.dma_start(rows_, zN[0:n, t:t + k, :]).then_inc(s_tab, 16)

                    def load(k, s):
                        sp.wait_ge(s_add[s], l * PAIRS + k)
                        sp.dma_start(ea[:, s, :], by_group(ea128, 2 * k + s, J)).then_inc(s_ea[s], 16)

                    with sp.Fori(0, PAIRS - 1) as k:
                        load(k, 0)
                        load(k, 1)
                    load(PAIRS - 1, 0)
                    load(PAIRS - 1, 1)
                sp.wait_ge(s_tab, L * ROWS * 16)

            @block.gpsimd
            def _(p):
                with p.Fori(0, L) as l:
                    p.wait_ge(s_tab, (l + 1) * (ROWS * 16))
                    p.nop(nofuse=True)
                    with p.Fori(0, PAIRS) as k:
                        for s in range(2):
                            p.wait_ge(s_idx[s], l * PAIRS + k + 1)
                            p.nop(nofuse=True)
                            for j in range(J):
                                nc.gpsimd.indirect_dma_start(
                                    gx[:, s, j * D:(j + 1) * D], None, table,
                                    bass.IndirectOffsetOnAxis(ap=idx[:, s, j:j + 1], axis=0),
                                ).then_inc(s_gx[s][j // (J // 2)], 16)

            @block.vector
            def _(v):
                for s in range(2):
                    nc.vector.tensor_copy(idx[:, s, :], srci[:, s * J:(s + 1) * J]).then_inc(s_idx[s], 1)
                with v.Fori(0, L) as l:
                    link = Link(v, s_l1, l * LINKS)
                    v.wait_ge(s_y, l * CH)
                    nc.vector.tensor_copy(pl[:, :].unsqueeze(1),
                                          pcols[:, :].rearrange("p (k l) -> p l k", l=L)[:, bass.ds(l, 1), :]
                                          ).then_inc(s_pl, 1)
                    for c, (o, w) in enumerate(chunks):
                        v.wait_ge(s_tp, l * CH + c + 1)
                        nc.vector.tensor_copy(zbuf[:, o:o + w], nps[:, c % NB, 0:w]).then_inc(s_st, 1)
                    with v.Fori(0, PAIRS) as k:
                        for s in range(2):
                            g = k * 2 + s
                            n = l * PAIRS + k
                            v.wait_ge(s_win[s], n)
                            nc.vector.tensor_tensor(
                                hot[:, s, :, :], win[:, :].unsqueeze(1).to_broadcast([P, J, WIN]),
                                dloc[:, bass.ds(g * J, J)].unsqueeze(2).to_broadcast([P, J, WIN]),
                                ALU.is_equal).then_inc(s_hot[s], 1)
                            v.wait_ge(s_ea[s], (n + 1) * 16)
                            for h in range(2):
                                v.wait_ge(s_gx[s][h], (n + 1) * (8 * J))
                                i = nc.vector.tensor_tensor(
                                    msg[:, s, h * GE // 2:(h + 1) * GE // 2], gx[:, s, h * GE // 2:(h + 1) * GE // 2],
                                    ea[:, s, h * GE // 2:(h + 1) * GE // 2], ALU.add)
                            i.then_inc(s_add[s], 1)
                            v.wait_ge(s_add[s], n + 1)
                            nc.vector.tensor_copy(idx[:, s, :], srci[:, bass.ds((g + 2) * J, J)]
                                                  ).then_inc(s_idx[s], 1)
                            first = v.value_load(dsti[0:1, bass.ds(g * J, 1)], min_val=0, max_val=N - 1)
                            v.wait_ge(s_win[s], n + 1)
                            v.wait_ge(s_acc[1 - s], n + s)
                            nc.vector.tensor_tensor(acc[:, bass.ds(first, WIN)], wps[s][:, 0:WIN],
                                                    acc[:, bass.ds(first, WIN)], ALU.add).then_inc(s_acc[s], 1)
                    for half, (s_e, buf) in enumerate(((s_z1e, zbuf), (s_z2e, acc))):
                        for c, (o, w) in enumerate(chunks):
                            v.wait_ge(s_e, l * CH + c + 1)
                            i = nc.vector.bn_stats(stats[:, c, :], buf[:, o:o + real[c]])
                        link.step(i)
                        v.nop(nofuse=True)
                        link.step(nc.vector.bn_aggr(mv[:, :], stats[:, :, :].rearrange("p c s -> p (c s)")))
                        nc.vector.tensor_scalar(std[:, :], mv[:, 1:2], EPS, None, ALU.add).then_inc(s_bv, 1)
                        v.wait_ge(s_ba, l * 2 + half + 1)
                        link.step(nc.vector.reciprocal(std[:, :], std[:, :]))
                        nc.vector.tensor_tensor(scl[:, :], std[:, :], pl[:, 3 * half + 1:3 * half + 2],
                                                ALU.mult).then_inc(s_bv, 1)
                        v.wait_ge(s_bv, l * 6 + half * 3 + 2)
                        link.step(nc.vector.scalar_tensor_tensor(shf[:, :], mv[:, 0:1], -1.0, scl[:, :],
                                                                 ALU.mult, ALU.mult))
                        nc.vector.tensor_tensor(shf[:, :], shf[:, :], pl[:, 3 * half + 2:3 * half + 3],
                                                ALU.add).then_inc(s_bv, 1)
                    assert link.n == LINKS

            def evacuate2(a, l, c):
                o, w = chunks[c]
                a.wait_ge(s_z2, l * CH + c + 1)
                nc.scalar.activation(acc[:, o:o + real[c]], nps[:, c % NB, 0:real[c]], ACT.Identity,
                                     bias=pl[:, 3:4]).then_inc(s_z2e, 1)

            @block.scalar
            def _(a):
                with a.Fori(0, L) as l:
                    for c, (o, w) in enumerate(chunks):
                        nc.scalar.activation(acc[:, o:o + w], acc[:, o:o + w], ACT.Relu).then_inc(s_rl, 1)
                    with a.Fori(0, PAIRS) as k:
                        for s in range(2):
                            a.wait_ge(s_add[s], l * PAIRS + k + 1)
                            nc.scalar.activation(msg[:, s, :], msg[:, s, :], ACT.Relu).then_inc(s_msg[s], 1)
                    a.wait_ge(s_pl, l + 1)
                    for c, (o, w) in enumerate(chunks):
                        a.wait_ge(s_z1, l * CH + c + 1)
                        nc.scalar.activation(zbuf[:, o:o + w], nps[:, c % NB, 0:w], ACT.Identity,
                                             bias=pl[:, 0:1]).then_inc(s_z1e, 1)
                    a.wait_ge(s_bv, l * 6 + 1)
                    nc.scalar.activation(std[:, :], std[:, :], ACT.Sqrt).then_inc(s_ba, 1)
                    a.wait_ge(s_bv, l * 6 + 3)
                    for c, (o, w) in enumerate(chunks):
                        nc.scalar.activation(zbuf[:, o:o + real[c]], zbuf[:, o:o + real[c]], ACT.Relu,
                                             bias=shf[:, 0:1], scale=scl[:, 0:1]).then_inc(s_h1, 1)
                        if c >= 1:
                            evacuate2(a, l, c - 1)
                    evacuate2(a, l, CH - 1)
                    a.wait_ge(s_bv, l * 6 + 4)
                    nc.scalar.activation(std[:, :], std[:, :], ACT.Sqrt).then_inc(s_ba, 1)
                    a.wait_ge(s_bv, l * 6 + 6)
                    for c, (o, w) in enumerate(chunks):
                        nc.scalar.activation(acc[:, o:o + real[c]], acc[:, o:o + real[c]], ACT.Identity,
                                             bias=shf[:, 0:1], scale=scl[:, 0:1]).then_inc(s_y, 1)
                    a.wait_ge(s_y, (l + 1) * CH)

            @block.tensor
            def _(pe):
                with pe.Fori(0, L) as l:
                    for c, (o, w) in enumerate(chunks):
                        pe.wait_ge(s_rl, l * CH + c + 1)
                        if c >= NB:
                            pe.wait_ge(s_st, l * CH + c - NB + 1)
                        for t in range(w // P):
                            last = nc.tensor.transpose(nps[:, c % NB, t * P:(t + 1) * P],
                                                       acc[:, o + t * P:o + (t + 1) * P], ident[:, :])
                        last.then_inc(s_tp, 1)
                    with pe.Fori(0, PAIRS) as k:
                        for s in range(2):
                            n = l * PAIRS + k
                            pe.wait_ge(s_hot[s], n + 1)
                            pe.wait_ge(s_msg[s], n + 1)
                            pe.wait_ge(s_acc[s], n)
                            for j in range(J):
                                last = nc.tensor.matmul(wps[s][:, 0:WIN], msg[:, s, j * D:(j + 1) * D],
                                                        hot[:, s, j, :], start=(j == 0), stop=(j == J - 1))
                            last.then_inc(s_win[s], 1)
                    for s in range(2):
                        pe.wait_ge(s_acc[s], (l + 1) * PAIRS)
                    pe.wait_ge(s_st, (l + 1) * CH)
                    pe.wait_ge(s_w, (l + 1) * 32)
                    for c, (o, w) in enumerate(chunks):
                        if c >= NB:
                            pe.wait_ge(s_z1e, l * CH + c - NB + 1)
                        nc.tensor.matmul(nps[:, c % NB, 0:w], w1[:, :], acc[:, o:o + w],
                                         start=True, stop=True).then_inc(s_z1, 1)
                    pe.wait_ge(s_z1e, (l + 1) * CH)
                    for c, (o, w) in enumerate(chunks):
                        pe.wait_ge(s_h1, l * CH + c + 1)
                        if c >= NB:
                            pe.wait_ge(s_z2e, l * CH + c - NB + 1)
                        nc.tensor.matmul(nps[:, c % NB, 0:real[c]], w2[:, :], zbuf[:, o:o + real[c]],
                                         start=True, stop=True).then_inc(s_z2, 1)
                    pe.wait_ge(s_z2e, (l + 1) * CH)

        s_t2 = sem("s_t2")
        s_r2 = sem("s_r2")
        s_l2 = sem("s_l2")
        s_v2 = sem("s_v2")
        s_a2 = sem("s_a2")
        s_u2 = sem("s_u2")
        s_e2 = sem("s_e2")
        s_p2 = sem("s_p2")
        s_q2 = sem("s_q2")
        s_d2 = sem("s_d2")
        with nc.Block() as block:
            @block.tensor
            def _(pe):
                for c, (o, w) in enumerate(chunks):
                    if c >= NB:
                        pe.wait_ge(s_r2, c - NB + 1)
                    for t in range(w // P):
                        last = nc.tensor.transpose(nps[:, c % NB, t * P:(t + 1) * P],
                                                   acc[:, o + t * P:o + (t + 1) * P], ident[:, :])
                    last.then_inc(s_t2, 1)
                pe.wait_ge(s_r2, CH)
                for c, (o, w) in enumerate(chunks):
                    pe.wait_ge(s_a2, 2 + c)
                    if c >= NB:
                        pe.wait_ge(s_e2, c - NB + 1)
                    for t in range(w // P):
                        last = nc.tensor.transpose(nps[:, c % NB, t * P:(t + 1) * P], bN[:, o // P + t, :],
                                                   ident[:, :])
                    last.then_inc(s_u2, 1)
                for c, (o, w) in enumerate(chunks):
                    pe.wait_ge(s_e2, CH)
                    if c >= NB:
                        pe.wait_ge(s_q2, c - NB + 1)
                    for t in range(w // P):
                        nc.tensor.matmul(nps[:, c % NB, t * P:(t + 1) * P], acc[:, o + t * P:o + (t + 1) * P],
                                         wnT[:, :], start=True, stop=False)
                        last = nc.tensor.matmul(nps[:, c % NB, t * P:(t + 1) * P], ones[:, :], bp[:, :],
                                                start=False, stop=True)
                    last.then_inc(s_p2, 1)

            @block.vector
            def _(v):
                link = Link(v, s_l2)
                for c, (o, w) in enumerate(chunks):
                    v.wait_ge(s_t2, c + 1)
                    nc.vector.tensor_tensor(xres[:, o // P:(o + w) // P, :],
                                            nps[:, c % NB, 0:w].rearrange("p (t d) -> p t d", d=D),
                                            xres[:, o // P:(o + w) // P, :], ALU.add).then_inc(s_r2, 1)
                v.wait_ge(s_r2, CH)
                layer_norm(v, None, link, s_v2, s_a2, 0, xres[:, :, :], bN, zN)
                for c, (o, w) in enumerate(chunks):
                    v.wait_ge(s_u2, c + 1)
                    nc.vector.tensor_copy(acc[:, o:o + w], nps[:, c % NB, 0:w]).then_inc(s_e2, 1)
                for c, (o, w) in enumerate(chunks):
                    v.wait_ge(s_p2, c + 1)
                    nc.vector.tensor_copy(zbuf[:, o:o + w], nps[:, c % NB, 0:w]).then_inc(s_q2, 1)

            @block.scalar
            def _(a):
                a.wait_ge(s_v2, 1)
                nc.scalar.activation(var[:, :], var[:, :], ACT.Sqrt).then_inc(s_a2, 1)
                a.wait_ge(s_v2, 2)
                for c, (o, w) in enumerate(chunks):
                    nc.scalar.activation(bbuf[:, o:o + w], bbuf[:, o:o + w], ACT.Relu).then_inc(s_a2, 1)

            @block.sync
            def _(sp):
                for c in range(CH):
                    sp.wait_ge(s_q2, c + 1)
                    for t, k, n, rows_ in node_rows(table2, c):
                        sp.dma_start(rows_, zN[0:n, t:t + k, :]).then_inc(s_d2, 16)
                sp.wait_ge(s_d2, 16 * ROWS)

        s_ef = [sem(f"s_ef{i}") for i in range(2)]
        s_ft = [sem(f"s_ft{i}") for i in range(2)]
        s_fs = [sem(f"s_fs{i}") for i in range(2)]
        s_pe = [sem(f"s_pe{i}") for i in range(2)]
        s_xp = [sem(f"s_xp{i}") for i in range(2)]
        s_lg = [sem(f"s_lg{i}") for i in range(2)]
        s_pr = sem("s_pr")
        s_id3 = [sem(f"s_id3{i}") for i in range(2)]
        s_g3 = [sem(f"s_g3{i}") for i in range(2)]
        s_ox = [sem(f"s_ox{i}") for i in range(2)]
        s_ol = [sem(f"s_ol{i}") for i in range(2)]
        XSTORES = (1 if DP + 1 < P else 0) + 1
        with nc.Block() as block:
            @block.sync
            def _(sp):
                def load(k, s):
                    sp.wait_ge(s_ft[s], k)
                    sp.dma_start(ea[:, s, 0:J * EF], by_group(ea64, 2 * k + s, J)).then_inc(s_ef[s], 16)

                with sp.Fori(0, PAIRS - 1) as k:
                    load(k, 0)
                    load(k, 1)
                load(PAIRS - 1, 0)
                load(PAIRS - 1, 1)

            @block.gpsimd
            def _(p):
                with p.Fori(0, PAIRS) as k:
                    for s in range(2):
                        p.wait_ge(s_id3[s], k + 1)
                        p.nop(nofuse=True)
                        for j in range(J):
                            nc.gpsimd.indirect_dma_start(
                                gx[:, s, j * D:(j + 1) * D], None, table2,
                                bass.IndirectOffsetOnAxis(ap=idx[:, s, j:j + 1], axis=0)).then_inc(s_g3[s], 16)

            @block.tensor
            def _(pe):
                with pe.Fori(0, PAIRS) as k:
                    for s in range(2):
                        pe.wait_ge(s_ef[s], (k + 1) * 16)
                        pe.wait_ge(s_fs[s], k)
                        for q in range(J // 2):
                            last = nc.tensor.transpose(tps[s][:, q * P:(q + 1) * P],
                                                       ea[:, s, q * P:(q + 1) * P], ident[:, :])
                        last.then_inc(s_ft[s], 1)
                        pe.wait_ge(s_fs[s], k + 1)
                        pe.wait_ge(s_xp[s], k)
                        for q in range(J // 2):
                            last = nc.tensor.matmul(
                                nps[:, 2 * s + q // 2, (q % 2) * 2 * D:(q % 2 + 1) * 2 * D],
                                eft[:, s, q * P:(q + 1) * P], we2[:, :, :].rearrange("p a d -> p (a d)"),
                                start=True, stop=True)
                        last.then_inc(s_pe[s], 1)

            @block.vector
            def _(v):
                for s in range(2):
                    nc.vector.tensor_copy(idx[:, s, :], srci[:, s * J:(s + 1) * J]).then_inc(s_id3[s], 1)
                with v.Fori(0, PAIRS) as k:
                    for s in range(2):
                        g = k * 2 + s
                        v.wait_ge(s_pe[s], k + 1)
                        v.wait_ge(s_g3[s], (k + 1) * (16 * J))
                        v.wait_ge(s_ox[s], k * 16)
                        nc.vector.tensor_tensor(msg[:, s, :].rearrange("p (b c) -> p b c", b=2),
                                                nps[:, 2 * s:2 * s + 2, :],
                                                gx[:, s, :].rearrange("p (b c) -> p b c", b=2),
                                                ALU.add).then_inc(s_xp[s], 1)
                        v.wait_ge(s_xp[s], k + 1)
                        nc.vector.tensor_copy(idx[:, s, :], srci[:, bass.ds((g + 2) * J, J)]).then_inc(s_id3[s], 1)
                        v.wait_ge(s_lg[1 - s], k + s)
                        nc.vector.tensor_tensor(prod[:, :].rearrange("p (j d) -> p j d", d=D),
                                                msg[:, s, :].rearrange("p (j d) -> p j d", d=D),
                                                attnb[:, :].unsqueeze(1).to_broadcast([P, J, D]),
                                                ALU.mult).then_inc(s_pr, 1)
                        v.wait_ge(s_pr, 2 * k + s + 1)
                        v.wait_ge(s_ol[s], k * 16)
                        nc.vector.tensor_reduce(lg[:, s, :, :].rearrange("p j h -> p (j h)"),
                                                prod[:, :].rearrange("p (q d) -> p q d", d=HD), AX.X,
                                                ALU.add).then_inc(s_lg[s], 1)

            @block.scalar
            def _(a):
                def copy_out(k, s):
                    a.wait_ge(s_ft[s], k + 1)
                    a.wait_ge(s_pe[s], k)
                    nc.scalar.copy(eft[:, s, :], tps[s][:, :]).then_inc(s_fs[s], 1)

                def store(k, s):
                    g = 2 * k + s
                    a.wait_ge(s_xp[s], k + 1)
                    a.dma_start(xp_d[bass.ds(g * P, P), :], msg[:, s, :]).then_inc(s_ox[s], 16)
                    a.wait_ge(s_lg[s], k + 1)
                    if isinstance(k, int) and g == G - 1:
                        rest = lg_d[E - GE + DUP:E, :]
                        if DJ:
                            a.dma_start(rest[0:J - DJ, :].rearrange("(p j) h -> p (j h)", p=1),
                                        lg[DP:DP + 1, s, DJ:J, :].rearrange("p j h -> p (j h)")).then_inc(s_ol[s], 16)
                        else:
                            a.dma_start(rest[0:J, :].rearrange("(p j) h -> p (j h)", p=1),
                                        lg[DP:DP + 1, s, :, :].rearrange("p j h -> p (j h)")).then_inc(s_ol[s], 16)
                        if DP + 1 < P:
                            a.dma_start(rest[J - DJ:, :].rearrange("(p j) h -> p (j h)", j=J),
                                        lg[DP + 1:P, s, :, :].rearrange("p j h -> p (j h)")).then_inc(s_ol[s], 16)
                    else:
                        a.dma_start(by_group(lg_d, g, J),
                                    lg[:, s, :, :].rearrange("p j h -> p (j h)")).then_inc(s_ol[s], 16)

                with a.Fori(0, PAIRS - 1) as k:
                    for s in range(2):
                        copy_out(k, s)
                        store(k, s)
                for s in range(2):
                    copy_out(PAIRS - 1, s)
                    store(PAIRS - 1, s)
                for s in range(2):
                    a.wait_ge(s_ox[s], PAIRS * 16)
                a.wait_ge(s_ol[0], PAIRS * 16)
                a.wait_ge(s_ol[1], (PAIRS - 1 + XSTORES) * 16)

        s_la = sem("s_la")
        s_l4 = sem("s_l4")
        s_t4 = sem("s_t4")
        s_v4 = sem("s_v4")
        s_a4 = sem("s_a4")
        s_o4 = sem("s_o4")
        lgE = bbuf[0:SP_, 0:SF * H].rearrange("p (f h) -> p f h", h=H)
        mxE = zbuf[0:SP_, 0:SF * H].rearrange("p (f h) -> p f h", h=H)
        halves = [(0, SA), (SA, SP_)] if 0 < SA < SP_ else [(0, SP_)]
        with nc.Block() as block:
            @block.sync
            def _(sp):
                for a0, a1 in halves:
                    sp.dma_start(bbuf[a0:a1, 0:SF * H],
                                 lg_d.rearrange("(p f) h -> p (f h)", f=SF)[a0:a1, :]).then_inc(s_la, 16)
                sp.wait_ge(s_a4, 1)
                for a0, a1 in halves:
                    sp.dma_start(ex_d.rearrange("(p f) h -> p (f h)", f=SF)[a0:a1, :],
                                 zbuf[a0:a1, 0:SF * H]).then_inc(s_o4, 16)
                sp.wait_ge(s_o4, 16 * len(halves))

            @block.vector
            def _(v):
                link = Link(v, s_l4)
                link.step(nc.vector.tensor_tensor(cap[:, :], dedge[:, 1:SF + 2], dedge[:, 0:SF + 1], ALU.not_equal))
                link.step(nc.vector.tensor_scalar(cap[:, :], cap[:, :], -2.0 * BIG, BIG, ALU.mult, ALU.add))
                v.wait_ge(s_la, 16 * len(halves))
                for turn in range(2):
                    back = turn == 1
                    caps = cap[:, 1:SF + 1][:, ::-1] if back else cap[:, 0:SF]
                    data = mxE if back else lgE

                    def scans(initial):
                        for h in range(H):
                            i, o = data[:, :, h], mxE[:, :, h]
                            if back:
                                i, o = i[:, ::-1], o[:, ::-1]
                            last = nc.vector.tensor_tensor_scan(o, caps, i, initial(h), ALU.min, ALU.max)
                        link.step(last)

                    scans(lambda h: -BIG)
                    end = 0 if back else SF - 1
                    nc.vector.tensor_copy(pair[:, 0, :], mxE[:, end, :])
                    link.step(nc.vector.tensor_reduce(pair[:, 1, 0:1], caps, AX.X, ALU.min))
                    for h in range(1, H):
                        last = nc.vector.tensor_copy(pair[:, 1, h:h + 1], pair[:, 1, 0:1])
                    last.then_inc(s_v4, 1)
                    v.wait_ge(s_t4, 2 * turn + 1)
                    link.step(nc.vector.tensor_copy(rows[:, :, :],
                                                    tps[0][0:H, 0:2 * SP_].rearrange("h (a p) -> h a p", a=2)))
                    link.step(nc.vector.memset(carry[:, :], -BIG))
                    d0, d1, o = rows[:, 1, :], rows[:, 0, :], carry[:, 1:SP_ + 1]
                    if back:
                        d0, d1, o = d0[:, ::-1], d1[:, ::-1], o[:, ::-1]
                    nc.vector.tensor_tensor_scan(o, d0, d1, -BIG, ALU.min, ALU.max).then_inc(s_v4, 1)
                    v.wait_ge(s_t4, 2 * turn + 2)
                    link.step(nc.vector.tensor_copy(carried[:, :], tps[1][0:SP_, 0:H]))
                    scans(lambda h: carried[:, h:h + 1])
                nc.vector.tensor_tensor(mxE, lgE, mxE, ALU.subtract).then_inc(s_v4, 1)

            @block.tensor
            def _(pe):
                for turn in range(2):
                    pe.wait_ge(s_v4, 2 * turn + 1)
                    nc.tensor.transpose(tps[0][0:H, 0:SP_], pair[:, 0, :], ident[0:SP_, 0:SP_])
                    nc.tensor.transpose(tps[0][0:H, SP_:2 * SP_], pair[:, 1, :],
                                        ident[0:SP_, 0:SP_]).then_inc(s_t4, 1)
                    pe.wait_ge(s_v4, 2 * turn + 2)
                    o = 2 if turn == 1 else 0
                    nc.tensor.transpose(tps[1][0:SP_, 0:H], carry[:, o:o + SP_], ident[0:H, 0:H]).then_inc(s_t4, 1)

            @block.scalar
            def _(a):
                a.wait_ge(s_v4, 5)
                nc.scalar.activation(mxE, mxE, ACT.Exp).then_inc(s_a4, 1)

        s_x5 = [sem(f"s_x5{i}") for i in range(2)]
        s_e5 = [sem(f"s_e5{i}") for i in range(2)]
        s_h5 = [sem(f"s_h5{i}") for i in range(2)]
        s_m5 = [sem(f"s_m5{i}") for i in range(2)]
        s_w5 = [sem(f"s_w5{i}") for i in range(2)]
        s_s5 = [sem(f"s_s5{i}") for i in range(2)]
        num = zbuf
        den = bbuf
        with nc.Block() as block:
            @block.sync
            def _(sp):
                def load(k, s):
                    g = 2 * k + s
                    sp.wait_ge(s_m5[s], k)
                    sp.dma_start(gx[:, s, :], xp_d[bass.ds(g * P, P), :]).then_inc(s_x5[s], 16)
                    sp.wait_ge(s_w5[s], k)
                    sp.dma_start(lg[:, s, :, :].rearrange("p j h -> p (j h)"), by_group(ex_d, g, J)
                                 ).then_inc(s_e5[s], 16)

                with sp.Fori(0, PAIRS - 1) as k:
                    load(k, 0)
                    load(k, 1)
                load(PAIRS - 1, 0)
                load(PAIRS - 1, 1)

            @block.vector
            def _(v):
                nc.vector.memset(num[:, 0:NP + WIN], 0.0)
                nc.vector.memset(den[0:H, 0:NP + WIN], 0.0).then_inc(s_s5[1], 1)
                with v.Fori(0, PAIRS) as k:
                    for s in range(2):
                        g = k * 2 + s
                        v.wait_ge(s_w5[s], k)
                        nc.vector.tensor_tensor(
                            hot[:, s, :, :], win[:, :].unsqueeze(1).to_broadcast([P, J, WIN]),
                            dloc[:, bass.ds(g * J, J)].unsqueeze(2).to_broadcast([P, J, WIN]),
                            ALU.is_equal).then_inc(s_h5[s], 1)
                        v.wait_ge(s_x5[s], (k + 1) * 16)
                        v.wait_ge(s_e5[s], (k + 1) * 16)
                        nc.vector.tensor_tensor(
                            msg[:, s, :].rearrange("p (q d) -> p q d", d=HD),
                            gx[:, s, :].rearrange("p (q d) -> p q d", d=HD),
                            lg[:, s, :, :].rearrange("p j h -> p (j h)").unsqueeze(2).to_broadcast([P, J * H, HD]),
                            ALU.mult).then_inc(s_m5[s], 1)
                        first = v.value_load(dsti[0:1, bass.ds(g * J, 1)], min_val=0, max_val=N - 1)
                        v.wait_ge(s_w5[s], k + 1)
                        v.wait_ge(s_s5[1 - s], k + 1)
                        nc.vector.tensor_tensor(num[:, bass.ds(first, WIN)], wps[s][:, 0:WIN],
                                                num[:, bass.ds(first, WIN)], ALU.add)
                        nc.vector.tensor_tensor(den[0:H, bass.ds(first, WIN)], tps[s][0:H, 0:WIN],
                                                den[0:H, bass.ds(first, WIN)], ALU.add).then_inc(s_s5[s], 1)

            @block.tensor
            def _(pe):
                with pe.Fori(0, PAIRS) as k:
                    for s in range(2):
                        pe.wait_ge(s_h5[s], k + 1)
                        pe.wait_ge(s_m5[s], k + 1)
                        pe.wait_ge(s_s5[s], k + s)
                        for j in range(J):
                            nc.tensor.matmul(wps[s][:, 0:WIN], msg[:, s, j * D:(j + 1) * D], hot[:, s, j, :],
                                             start=(j == 0), stop=(j == J - 1))
                        for j in range(J):
                            last = nc.tensor.matmul(tps[s][0:H, 0:WIN], lg[:, s, j, :], hot[:, s, j, :],
                                                    start=(j == 0), stop=(j == J - 1))
                        last.then_inc(s_w5[s], 1)

        s_d6 = sem("s_d6")
        s_r6 = sem("s_r6")
        s_n6 = sem("s_n6")
        s_v6 = sem("s_v6")
        s_p6 = sem("s_p6")
        s_h6 = sem("s_h6")
        s_l6 = sem("s_l6")
        s_y6 = sem("s_y6")
        s_a6 = sem("s_a6")
        s_f6 = sem("s_f6")
        s_out = sem("s_out")
        with nc.Block() as block:
            def project(pe, c):
                o, w = chunks[c]
                pe.wait_ge(s_v6, c + 1)
                if c >= 2:
                    pe.wait_ge(s_h6, c - 1)
                for t in range(w // P):
                    nc.tensor.matmul(nps[:, 2 + c % 2, t * P:(t + 1) * P], num[:, o + t * P:o + (t + 1) * P],
                                     woT[:, :], start=True, stop=False)
                    last = nc.tensor.matmul(nps[:, 2 + c % 2, t * P:(t + 1) * P], ones[:, :], bo[:, :],
                                            start=False, stop=True)
                last.then_inc(s_p6, 1)

            @block.tensor
            def _(pe):
                for c, (o, w) in enumerate(chunks):
                    if c >= 2:
                        pe.wait_ge(s_r6, c - 1)
                    nc.tensor.matmul(nps[:, c % 2, 0:w], selh[:, :], den[0:H, o:o + w],
                                     start=True, stop=True).then_inc(s_d6, 1)
                    if c >= 1:
                        project(pe, c - 1)
                project(pe, CH - 1)

            @block.vector
            def _(v):
                for c, (o, w) in enumerate(chunks):
                    s = c % 2
                    v.wait_ge(s_d6, c + 1)
                    if c >= 2:
                        v.wait_ge(s_n6, c - 1)
                    nc.vector.tensor_scalar(gx[:, s, 0:w], nps[:, s, 0:w], 1.0e-30, None, ALU.max).then_inc(s_r6, 1)
                    v.wait_ge(s_r6, c + 1)
                    nc.vector.reciprocal(msg[:, s, 0:w], gx[:, s, 0:w]).then_inc(s_n6, 1)
                    v.wait_ge(s_n6, c + 1)
                    nc.vector.tensor_tensor(ea[:, s, 0:w], num[:, o:o + w], msg[:, s, 0:w], ALU.mult
                                            ).then_inc(s_f6, 1)
                    v.wait_ge(s_f6, c + 1)
                    nc.vector.tensor_tensor(num[:, o:o + w], ea[:, s, 0:w], acc[:, o:o + w], ALU.add
                                            ).then_inc(s_v6, 1)
                v.wait_ge(s_h6, CH)
                link = Link(v, s_l6)
                layer_norm(v, None, link, s_y6, s_a6, 0, aN, bN, zN)
                v.wait_ge(s_y6, 2)
                for c, (o, w) in enumerate(chunks):
                    t0, t1 = o // P, (o + w) // P
                    k = t1 - t0
                    link.step(nc.vector.tensor_tensor(bN[:, t0:t1, :], bN[:, t0:t1, :],
                                                      gamb[:, :].unsqueeze(1).to_broadcast([P, k, D]), ALU.mult))
                    link.step(nc.vector.tensor_tensor(bN[:, t0:t1, :], bN[:, t0:t1, :],
                                                      betb[:, :].unsqueeze(1).to_broadcast([P, k, D]), ALU.add))
                    nc.vector.tensor_tensor(bN[:, t0:t1, :], bN[:, t0:t1, :], xres[:, t0:t1, :],
                                            ALU.add).then_inc(s_y6, 1)

            @block.scalar
            def _(a):
                for c, (o, w) in enumerate(chunks):
                    a.wait_ge(s_p6, c + 1)
                    nc.scalar.activation(acc[:, o:o + w], nps[:, 2 + c % 2, 0:w], ACT.Relu).then_inc(s_h6, 1)
                a.wait_ge(s_y6, 1)
                nc.scalar.activation(var[:, :], var[:, :], ACT.Sqrt).then_inc(s_a6, 1)

            @block.sync
            def _(sp):
                for c in range(CH):
                    sp.wait_ge(s_y6, 3 + c)
                    for t, k, n, rows_ in node_rows(out, c):
                        sp.dma_start(rows_, bN[0:n, t:t + k, :]).then_inc(s_out, 16)
                sp.wait_ge(s_out, 16 * ROWS)


_INS = ["x", "src", "dst", "edge_attr_128", "edge_attr_64", "L0_gnn_W1", "L0_gnn_b1", "L0_gnn_g_mlp",
        "L0_gnn_be_mlp", "L0_gnn_W2", "L0_gnn_b2", "L0_gnn_g_out", "L0_gnn_be_out", "L1_gnn_W_proj_w",
        "L1_gnn_W_proj_b", "L1_gnn_attn_vec", "L1_gnn_W_out_w", "L1_gnn_W_out_b", "L1_gnn_ln_gamma",
        "L1_gnn_ln_beta"]


def kernel(**inputs):
    import concourse.bacc as bacc
    from concourse.bass_utils import run_bass_kernel_spmd

    nc = bacc.Bacc("TRN2", target_bir_lowering=False, num_devices=1)
    arrays, args = {}, []
    for name in _INS:
        a = np.ascontiguousarray(inputs[name])
        arrays[f"in_{name}"] = a
        args.append(nc.dram_tensor(f"in_{name}", a.shape, mybir.dt.from_np(a.dtype), kind="ExternalInput").ap())
    shape = inputs["x"].shape
    args.append(nc.dram_tensor("out_0", shape, F32, kind="ExternalOutput").ap())
    gnn_program(nc, *args)
    r = run_bass_kernel_spmd(nc, [arrays], core_ids=[0])
    return r.results[0]["out_0"]
```

```python
import numpy as np
import concourse.bass as bass
from concourse import mybir
from contextlib import ExitStack

F32 = mybir.dt.float32
I32 = mybir.dt.int32
ALU = mybir.AluOpType
ACT = mybir.ActivationFunctionType
AX = mybir.AxisListType

P = 128
EPS = 1e-5
BIG = 1.0e38


class Link:

    def __init__(self, engine, sem, start=0):
        self.engine, self.sem, self.start, self.n = engine, sem, start, 0

    def step(self, instruction):
        instruction.then_inc(self.sem, 1)
        self.n += 1
        self.engine.wait_ge(self.sem, self.start + self.n)


def gnn_program(nc, x, src, dst, ea128, ea64, W1, b1, g_mlp, be_mlp, W2, b2, g_out, be_out,
                Wproj, bproj, attn, Wout, bout, gamma, beta, out):
    N, D = x.shape
    E = ea128.shape[0]
    EF = ea64.shape[1]
    L = W1.shape[0]
    H, HD = attn.shape
    assert D == P and H * HD == P and EF * 2 == P

    J = 8
    GE = J * P
    G = -(-E // GE)
    assert G % 2 == 0
    PAIRS = G // 2
    REM = E - (G - 1) * GE
    RP, RJ = REM // J, REM % J
    assert RP > 0
    EP = G * GE
    NOWHERE = -1000000
    WIN = 64
    NT = -(-N // P)
    NP = NT * P
    NLAST = N - (NT - 1) * P
    chunks = [(c, min(512, NP - c)) for c in range(0, NP, 512)]
    CH = len(chunks)
    real = [min(w, N - c) for c, w in chunks]
    NB = 4
    SF = EP // P
    SLAST = E - (P - 1) * SF
    assert 0 < SLAST
    AW = max(NP + WIN, SF * H)
    NW = -(-NP // WIN)
    UN = max(d for d in range(1, 9) if NT % d == 0)
    CB = max(d for d in range(1, 257) if E % d == 0)

    def dram(name, shape):
        return nc.dram_tensor(name, shape, F32).ap()

    table = dram("table", (N, D))
    table2 = dram("table2", (N, D))
    xp_d = dram("xp_d", (G * P, J * D))
    lg_d = dram("lg_d", (EP, H))
    ex_d = dram("ex_d", (EP, H))

    nm_d = dram("nm_d", (NP, H))
    mx_d = dram("mx_d", (EP, H))

    ctx = ExitStack()
    with ctx:
        def sb(name, shape, dt=F32):
            return ctx.enter_context(nc.sbuf_tensor(name, shape, dt))

        def pb(name, shape):
            return ctx.enter_context(nc.psum_tensor(name, shape, F32))

        def sem(name):
            return ctx.enter_context(nc.semaphore(name))

        acc = sb("acc", [P, AW])
        zbuf = sb("zbuf", [P, AW])
        bbuf = sb("bbuf", [P, AW])
        xres = sb("xres", [P, NT, D])
        srci = sb("srci", [P, (G + 2) * J], I32)
        dsti = sb("dsti", [P, G * J], I32)
        dloc = sb("dloc", [P, G * J])
        idx = sb("idx", [P, 2, J], I32)
        gx = sb("gx", [P, 2, GE])
        ea = sb("ea", [P, 2, GE])
        msg = sb("msg", [P, 2, GE])
        hot = sb("hot", [P, 2, J, WIN])
        prod = sb("prod", [P, GE])
        lg = sb("lg", [P, 4, J, H])
        eft = sb("eft", [P, 2, GE // 2])
        win = sb("win", [P, WIN])
        rampi = sb("rampi", [P, P], I32)
        ident = sb("ident", [P, P])
        ones = sb("ones", [1, P])
        dmiss = sb("dmiss", [P, G * J])
        dcur = sb("dcur", [P, J])
        idg = sb("idg", [P, J], I32)
        onec = sb("onec", [P, 1])
        nodeid = sb("nodeid", [P, 1])
        blockmax = sb("blockmax", [P, H])
        bad = sb("bad", [P, 2])
        flagi = sb("flagi", [1, 1], I32)
        params = sb("params", [6 * L, D])
        pcols = sb("pcols", [P, 6 * L])
        pl = sb("pl", [P, 6])
        w1 = sb("w1", [P, D])
        w2 = sb("w2", [P, D])
        stats = sb("stats", [P, CH, 6])
        mv = sb("mv", [P, 2])
        std = sb("std", [P, 1])
        scl = sb("scl", [P, 1])
        shf = sb("shf", [P, 1])
        lnst = sb("lnst", [P, NT, 6])
        dif = sb("dif", [P, NT])
        var = sb("var", [P, NT])
        nmr = sb("nmr", [P, NT])
        ev = sb("ev", [P, 2, 2, WIN])
        rec = sb("rec", [P, NT * H])
        wp = sb("wp", [P, D + 2 * EF])
        wo = sb("wo", [P, D])
        wnT = sb("wnT", [P, D])
        we2 = sb("we2", [P, 2, D])
        woT = sb("woT", [P, D])
        bp = sb("bp", [1, D])
        bo = sb("bo", [1, D])
        attnb = sb("attnb", [P, D])
        gamb = sb("gamb", [P, D])
        betb = sb("betb", [P, D])
        dedge = sb("dedge", [P, SF + 2], I32)
        cap = sb("cap", [P, SF + 1])
        pair = sb("pair", [P, 2, H])
        rows = sb("rows", [H, 2, P])
        carry = sb("carry", [H, P + 2])
        carried = sb("carried", [P, H])
        selh = sb("selh", [H, D])

        wps = [pb(f"wps{i}", [P, 512]) for i in range(2)]
        nps = pb("nps", [P, NB, 512])
        tps = [pb(f"tps{i}", [P, 512]) for i in range(2)]

        accT = acc[:, 0:NP]
        zN = zbuf[:, 0:NP].rearrange("p (t d) -> p t d", d=D)
        bN = bbuf[:, 0:NP].rearrange("p (t d) -> p t d", d=D)
        aN = acc[:, 0:NP].rearrange("p (t d) -> p t d", d=D)

        def by_group(t, g):
            return t[bass.ds(g * GE, GE), :].rearrange("(p j) f -> p (j f)", j=J)

        def load_edges(sp, tile, t, g, s_done, s_rest, rest):
            F = t.shape[1]
            if isinstance(g, int) and g == G - 1:
                if RJ:
                    sp.dma_start(tile[RP:RP + 1, 0:RJ * F],
                                 t[E - RJ:E, :].rearrange("(p j) f -> p (j f)", p=1)).then_inc(s_rest, 16)
                    sp.wait_ge(s_rest, rest)
                sp.dma_start(tile[0:RP, :],
                             t[g * GE:g * GE + RP * J, :].rearrange("(p j) f -> p (j f)", j=J)).then_inc(s_done, 16)
            else:
                sp.dma_start(tile, by_group(t, g)).then_inc(s_done, 16)

        def node_rows(t, c):
            o, w = chunks[c]
            whole = min(w, N - o) // P
            parts = []
            if whole:
                parts.append((o // P, whole, P, t[o:o + whole * P, :].rearrange("(t p) d -> p t d", p=P)))
            if whole * P < min(w, N - o):
                o += whole * P
                parts.append((o // P, 1, N - o, t[o:N, :].rearrange("(t p) d -> p t d", t=1)))
            return parts

        ROWS = sum(len(node_rows(table, c)) for c in range(CH))

        def layer_norm(v, link, s_v, s_a, s_n, src3, dst3):
            with v.Fori(0, NT // UN) as b:
                for u in range(UN):
                    last = nc.vector.bn_stats(lnst[:, bass.ds(b * UN + u, 1), :].rearrange("p t s -> p (t s)"),
                                              src3[:, bass.ds(b * UN + u, 1), :].rearrange("p t d -> p (t d)"))
            link.step(v.drain())
            me, ve, mo, vo = (lnst[:, :, i] for i in (1, 2, 4, 5))
            link.step(nc.vector.tensor_tensor(dif[:, :], me, mo, ALU.subtract))
            link.step(nc.vector.tensor_tensor(dif[:, :], dif[:, :], dif[:, :], ALU.mult))
            link.step(nc.vector.tensor_tensor(var[:, :], ve, vo, ALU.add))
            link.step(nc.vector.tensor_scalar(var[:, :], var[:, :], 1.0 / D, EPS, ALU.mult, ALU.add))
            nc.vector.scalar_tensor_tensor(var[:, :], dif[:, :], 0.25, var[:, :], ALU.mult, ALU.add).then_inc(s_v, 1)
            link.step(nc.vector.tensor_tensor(nmr[:, :], me, mo, ALU.add))
            v.wait_ge(s_a, 1)
            link.step(nc.vector.reciprocal(var[:, :], var[:, :]))
            link.step(nc.vector.scalar_tensor_tensor(nmr[:, :], nmr[:, :], -0.5, var[:, :], ALU.mult, ALU.mult))
            with v.Fori(0, NT // UN) as b:
                for u in range(UN):
                    t = b * UN + u
                    nc.vector.tensor_scalar(dst3[:, bass.ds(t, 1), :].rearrange("p t d -> p (t d)"),
                                            src3[:, bass.ds(t, 1), :].rearrange("p t d -> p (t d)"),
                                            var[:, bass.ds(t, 1)], nmr[:, bass.ds(t, 1)],
                                            ALU.mult, ALU.add).then_inc(s_n, 1)

        def flag_on(engine):
            return engine.value_load(flagi[0:1, 0:1], min_val=0, max_val=1)

        s_x = sem("s_x")
        s_ld = sem("s_ld")
        s_io = sem("s_io")
        s_l0 = sem("s_l0")
        s_v0 = sem("s_v0")
        s_a0 = sem("s_a0")
        s_t0 = sem("s_t0")
        s_e0 = sem("s_e0")
        s_c0 = sem("s_c0")
        LOADS = 19 + 2 * (RJ > 0)
        LN0 = 8
        s_nt0 = sem("s_nt0")
        s_de = sem("s_de")
        with nc.Block() as block:
            @block.sync
            def _(sp):
                for c in range(CH):
                    for t, k, n, v in node_rows(x, c):
                        if n < P:
                            sp.wait_ge(s_io, 1)
                        sp.dma_start(xres[0:n, t:t + k, :], v).then_inc(s_x, 16)
                sp.wait_ge(s_io, 4)
                for tab, arr in ((srci, src), (dsti, dst)):
                    sp.dma_start(tab[:, 0:(G - 1) * J].rearrange("p (g j) -> p g j", j=J),
                                 arr[0:(G - 1) * GE].rearrange("(g p j) -> p g j", p=P, j=J)).then_inc(s_ld, 16)
                    last = tab[:, (G - 1) * J:G * J]
                    sp.dma_start(last[0:RP, :], arr[(G - 1) * GE:(G - 1) * GE + RP * J
                                                    ].rearrange("(p j) -> p j", j=J)).then_inc(s_ld, 16)
                    if RJ:
                        sp.dma_start(last[RP:RP + 1, 0:RJ], arr[E - RJ:E].unsqueeze(0)).then_inc(s_ld, 16)
                sp.dma_start(srci[:, G * J:(G + 2) * J].rearrange("p (g j) -> p g j", j=J),
                             src[0:2 * GE].rearrange("(g p j) -> p g j", p=P, j=J)).then_inc(s_ld, 16)
                for k, w in enumerate((b1, g_mlp, be_mlp, b2, g_out, be_out)):
                    sp.dma_start(params[k * L:(k + 1) * L, :], w).then_inc(s_ld, 16)
                sp.dma_start(wp[:, 0:D + EF], Wproj).then_inc(s_ld, 16)
                sp.dma_start(wp[:, D + EF:D + 2 * EF], Wproj[:, D:D + EF]).then_inc(s_ld, 16)
                sp.dma_start(wo[:, :], Wout).then_inc(s_ld, 16)
                sp.dma_start(bp[:, :], bproj.unsqueeze(0)).then_inc(s_ld, 16)
                sp.dma_start(bo[:, :], bout.unsqueeze(0)).then_inc(s_ld, 16)
                sp.dma_start(attnb[:, :], attn.rearrange("h d -> (h d)").partition_broadcast(P)).then_inc(s_ld, 16)
                sp.dma_start(gamb[:, :], gamma.partition_broadcast(P)).then_inc(s_ld, 16)
                sp.dma_start(betb[:, :], beta.partition_broadcast(P)).then_inc(s_ld, 16)
                sp.dma_start(dedge[0:P - 1, 1:SF + 1],
                             dst[0:(P - 1) * SF].rearrange("(p f) -> p f", f=SF)).then_inc(s_de, 16)
                sp.dma_start(dedge[P - 1:P, 1:SLAST + 1], dst[(P - 1) * SF:E].unsqueeze(0)).then_inc(s_de, 16)
                with nc.allow_non_contiguous_dma(reason="one word of each partition"):
                    sp.dma_start(dedge[1:P, 0:1], dst[0:(P - 1) * SF].rearrange("(p f) -> p f", f=SF)
                                 [:, SF - 1:SF]).then_inc(s_de, 16)
                    sp.dma_start(dedge[0:P - 2, SF + 1:SF + 2], dst[SF:(P - 1) * SF].rearrange("(p f) -> p f", f=SF)
                                 [:, 0:1]).then_inc(s_de, 16)
                    sp.dma_start(dedge[P - 2:P - 1, SF + 1:SF + 2],
                                 dst[(P - 1) * SF:(P - 1) * SF + 1].unsqueeze(0)).then_inc(s_de, 16)
                sp.wait_ge(s_ld, 16 * LOADS)
                sp.wait_ge(s_x, 16 * ROWS)
                sp.wait_ge(s_de, 16 * 5)

            @block.gpsimd
            def _(p):
                nc.gpsimd.memset(xres[:, NT - 1, :], 0.0).then_inc(s_io, 1)
                nc.gpsimd.memset(srci[:, (G - 1) * J:G * J], 0).then_inc(s_io, 1)
                nc.gpsimd.memset(dsti[:, (G - 1) * J:G * J], NOWHERE).then_inc(s_io, 1)
                nc.gpsimd.memset(dedge[:, :], N).then_inc(s_io, 1)
                nc.gpsimd.iota(rampi[:, :], [[1, P]], base=0, channel_multiplier=-1).then_inc(s_io, 1)
                nc.gpsimd.iota(win[:, :], [[1, WIN]], base=0, channel_multiplier=0,
                               allow_small_or_imprecise_dtypes=True).then_inc(s_io, 1)
                nc.gpsimd.memset(ones[:, :], 1.0).then_inc(s_io, 1)
                nc.gpsimd.memset(selh[:, :], 1.0).then_inc(s_io, 1)
                nc.gpsimd.memset(onec[:, :], 1.0).then_inc(s_io, 1)
                nc.gpsimd.iota(nodeid[:, :], [[0, 1]], base=0, channel_multiplier=1,
                               allow_small_or_imprecise_dtypes=True).then_inc(s_io, 1)
                p.wait_ge(s_io, 10)
                nc.gpsimd.affine_select(out=selh[:, :], in_=selh[:, :], compare_op=ALU.is_ge, fill=0.0, base=0,
                                        pattern=[[1, D]], channel_multiplier=-HD).then_inc(s_io, 1)
                p.wait_ge(s_io, 11)
                nc.gpsimd.affine_select(out=selh[:, :], in_=selh[:, :], compare_op=ALU.is_ge, fill=0.0,
                                        base=HD - 1, pattern=[[-1, D]], channel_multiplier=HD).then_inc(s_io, 1)

            @block.vector
            def _(v):
                link = Link(v, s_l0)
                v.wait_ge(s_io, 12)
                nc.vector.tensor_scalar(ident[:, :], rampi[:, :], 0.0, None, ALU.is_equal).then_inc(s_c0, 1)
                nc.vector.memset(acc[:, NP:AW], 0.0)
                nc.vector.memset(scl[:, :], 1.0)
                nc.vector.memset(shf[:, :], 0.0)
                link.step(nc.vector.memset(we2[:, :, :], 0.0))
                v.wait_ge(s_x, 16 * ROWS)
                layer_norm(v, link, s_v0, s_a0, s_nt0, xres[:, :, :], bN)
                assert link.n == LN0 + 1
                v.wait_ge(s_ld, 16 * LOADS)
                link.step(nc.vector.tensor_copy(dloc[:, :], dsti[:, :]))
                nc.vector.tensor_copy(dmiss[:, :], dsti[:, :])
                v.wait_ge(s_t0, CH + 1)
                link.step(nc.vector.tensor_tensor(
                    dloc[:, :].rearrange("p (g j) -> p g j", j=J), dloc[:, :].rearrange("p (g j) -> p g j", j=J),
                    wps[0][:, 0:G].unsqueeze(2).to_broadcast([P, G, J]), ALU.subtract))
                inside = cap[:, 0:G * J]
                link.step(nc.vector.tensor_scalar(inside, dloc[:, :], 0.0, None, ALU.is_ge))
                link.step(nc.vector.scalar_tensor_tensor(inside, dloc[:, :], float(WIN), inside, ALU.is_lt, ALU.mult))
                link.step(nc.vector.scalar_tensor_tensor(dmiss[:, :], inside, float(NOWHERE), dmiss[:, :],
                                                         ALU.mult, ALU.add))
                link.step(nc.vector.tensor_scalar(inside, dmiss[:, :], 0.0, None, ALU.is_ge))
                link.step(nc.vector.tensor_reduce(bad[:, 0:1], inside, AX.X, ALU.add))
                v.wait_ge(s_de, 16 * 5)
                link.step(nc.vector.tensor_tensor(cap[:, :], dedge[:, 1:SF + 2], dedge[:, 0:SF + 1], ALU.is_lt))
                link.step(nc.vector.memset(cap[0:1, 0:1], 0.0))
                link.step(nc.vector.tensor_reduce(bad[:, 1:2], cap[:, :], AX.X, ALU.add))
                nc.vector.tensor_tensor(bad[:, 0:1], bad[:, 0:1], bad[:, 1:2], ALU.add).then_inc(s_c0, 1)
                v.wait_ge(s_t0, CH + 3)
                nc.vector.tensor_scalar(flagi[:, :], wps[0][0:1, 511:512], 1.0, None, ALU.min)
                nc.vector.tensor_copy(pcols[:, :], wps[1][:, 0:6 * L])
                nc.vector.tensor_copy(wnT[:, :], tps[0][:, 0:P])
                nc.vector.tensor_copy(we2[0:EF, 0, :], tps[0][0:EF, P:2 * P])
                nc.vector.tensor_copy(we2[EF:P, 1, :], tps[0][EF:P, P:2 * P])
                nc.vector.tensor_copy(woT[:, :], tps[0][:, 2 * P:3 * P]).then_inc(s_c0, 1)

            @block.scalar
            def _(a):
                a.wait_ge(s_v0, 1)
                nc.scalar.activation(var[:, :], var[:, :], ACT.Sqrt).then_inc(s_a0, 1)
                for c, (o, w) in enumerate(chunks):
                    a.wait_ge(s_t0, 1 + c)
                    nc.scalar.activation(acc[:, o:o + w], nps[:, c % NB, 0:w], ACT.Relu).then_inc(s_e0, 1)

            @block.tensor
            def _(pe):
                pe.wait_ge(s_c0, 1)
                for c, (o, w) in enumerate(chunks):
                    pe.wait_ge(s_nt0, (o + w) // P)
                    if c >= NB:
                        pe.wait_ge(s_e0, c - NB + 1)
                    for t in range(w // P):
                        last = nc.tensor.transpose(nps[:, c % NB, t * P:(t + 1) * P], bN[:, o // P + t, :],
                                                   ident[:, :])
                    last.then_inc(s_t0, 1)
                pe.wait_ge(s_io, 12)
                pe.wait_ge(s_l0, LN0 + 2)
                firsts = dloc[0:1, :].rearrange("p (g j) -> p g j", j=J)[:, :, 0]
                nc.tensor.matmul(wps[0][:, 0:G], ones[0:1, :], firsts, start=True, stop=True).then_inc(s_t0, 1)
                pe.wait_ge(s_ld, 16 * LOADS)
                nc.tensor.transpose(wps[1][:, 0:6 * L], params[:, :], ident[0:6 * L, 0:6 * L])
                nc.tensor.transpose(tps[0][:, 0:P], wp[:, 0:D], ident[:, :])
                nc.tensor.transpose(tps[0][:, P:2 * P], wp[:, D:D + 2 * EF], ident[:, :])
                nc.tensor.transpose(tps[0][:, 2 * P:3 * P], wo[:, :], ident[:, :]).then_inc(s_t0, 1)
                pe.wait_ge(s_c0, 2)
                nc.tensor.matmul(wps[0][0:1, 511:512], bad[:, 0:1], onec[:, :], start=True, stop=True).then_inc(s_t0, 1)

        s_w = sem("s_w")
        s_rl = sem("s_rl")
        s_tp = sem("s_tp")
        s_st = sem("s_st")
        s_tab = sem("s_tab")
        s_idx = [sem(f"s_idx{i}") for i in range(2)]
        s_gx = [[sem(f"s_gx{i}{h}") for h in range(2)] for i in range(2)]
        s_ea = [sem(f"s_ea{i}") for i in range(2)]
        s_rest = sem("s_rest")
        s_hot = [sem(f"s_hot{i}") for i in range(2)]
        s_add = [sem(f"s_add{i}") for i in range(2)]
        s_msg = [sem(f"s_msg{i}") for i in range(2)]
        s_win = [sem(f"s_win{i}") for i in range(2)]
        s_acc = [sem(f"s_acc{i}") for i in range(2)]
        s_z1 = sem("s_z1")
        s_z1e = sem("s_z1e")
        s_h1 = sem("s_h1")
        s_z2 = sem("s_z2")
        s_z2e = sem("s_z2e")
        s_bv = sem("s_bv")
        s_ba = sem("s_ba")
        s_l1 = sem("s_l1")
        s_pl = sem("s_pl")
        g_idx, g_row, g_edge, g_msg, g_relu = (sem(f"g_{x}") for x in ("idx", "row", "edge", "msg", "relu"))
        g_hot, g_win, g_acc, g_rest = (sem(f"g_{x}") for x in ("hot", "win", "acc", "rest"))
        LINKS = 8

        def general_window(v, q, w, s_hot_, s_win_, s_acc_, sums, credit=0):
            nc.vector.tensor_tensor(hot[:, 0, :, :], win[:, :].unsqueeze(1).to_broadcast([P, J, WIN]),
                                    dcur[:, :].unsqueeze(2).to_broadcast([P, J, WIN]),
                                    ALU.is_equal).then_inc(s_hot_, 1)
            v.wait_ge(s_win_, q + 1)
            for sums_, product, n in sums:
                nc.vector.tensor_tensor(sums_[0:n, bass.ds(w * WIN, WIN)], product[0:n, 0:WIN],
                                        sums_[0:n, bass.ds(w * WIN, WIN)], ALU.add)
            nc.vector.tensor_scalar(dcur[:, :], dcur[:, :], float(WIN), None, ALU.subtract).then_inc(s_acc_, 1)
            v.wait_ge(s_acc_, q + 1 + credit)

        with nc.Block() as block:
            @block.sync
            def _(sp):
                flag = flag_on(sp)
                with sp.Fori(0, L) as l:
                    sp.wait_ge(s_z2, l * CH + 1)
                    sp.dma_start(w1[:, :], W1[bass.ds(l, 1), :, :].rearrange("l i o -> (l i) o")).then_inc(s_w, 16)
                    sp.dma_start(w2[:, :], W2[bass.ds(l, 1), :, :].rearrange("l i o -> (l i) o")).then_inc(s_w, 16)
                    for c in range(CH):
                        sp.wait_ge(s_st, l * CH + c + 1)
                        for t, k, n, rows_ in node_rows(table, c):
                            sp.dma_start(rows_, zN[0:n, t:t + k, :]).then_inc(s_tab, 16)

                    def load(k, s):
                        sp.wait_ge(s_add[s], l * PAIRS + k + 1)
                        load_edges(sp, ea[:, s, :], ea128, 2 * k + s, s_ea[s], s_rest, (l + 1) * 16)

                    with sp.Fori(0, PAIRS - 1) as k:
                        load(k, 0)
                        load(k, 1)
                    load(PAIRS - 1, 0)
                    load(PAIRS - 1, 1)
                    sp.nop(nofuse=True)
                    with sp.If(flag > 0):
                        sp.wait_ge(s_acc[1], (l + 1) * PAIRS + 1)
                        sp.nop(nofuse=True)
                        with sp.Fori(0, G - 1) as g:
                            sp.wait_ge(g_idx, l * G + g + 1)
                            load_edges(sp, ea[:, 0, :], ea128, g, g_edge, g_rest, 0)
                        sp.wait_ge(g_idx, (l + 1) * G)
                        load_edges(sp, ea[:, 0, :], ea128, G - 1, g_edge, g_rest, (l + 1) * 16)
                    sp.nop(nofuse=True)
                sp.wait_ge(s_tab, L * ROWS * 16)

            @block.gpsimd
            def _(p):
                flag = flag_on(p)
                with p.Fori(0, L) as l:
                    p.wait_ge(s_tab, (l + 1) * (ROWS * 16))
                    p.nop(nofuse=True)
                    with p.Fori(0, PAIRS) as k:
                        for s in range(2):
                            p.wait_ge(s_idx[s], l * PAIRS + k + 1)
                            p.nop(nofuse=True)
                            for j in range(J):
                                nc.gpsimd.indirect_dma_start(
                                    gx[:, s, j * D:(j + 1) * D], None, table,
                                    bass.IndirectOffsetOnAxis(ap=idx[:, s, j:j + 1], axis=0),
                                ).then_inc(s_gx[s][j // (J // 2)], 16)
                    with p.If(flag > 0):
                        with p.Fori(0, G) as g:
                            p.wait_ge(g_idx, l * G + g + 1)
                            p.nop(nofuse=True)
                            for j in range(J):
                                nc.gpsimd.indirect_dma_start(
                                    gx[:, 0, j * D:(j + 1) * D], None, table,
                                    bass.IndirectOffsetOnAxis(ap=idg[:, j:j + 1], axis=0)).then_inc(g_row, 16)
                    p.nop(nofuse=True)

            @block.vector
            def _(v):
                flag = flag_on(v)
                for s in range(2):
                    v.sem_inc(s_add[s], 1)
                    v.sem_inc(s_acc[s], 1)
                v.sem_inc(s_bv, 1)
                for s in range(2):
                    nc.vector.tensor_copy(idx[:, s, :], srci[:, s * J:(s + 1) * J]).then_inc(s_idx[s], 1)
                with v.Fori(0, L) as l:
                    link = Link(v, s_l1, l * LINKS)
                    v.wait_ge(s_bv, l * 6 + 1)
                    v.nop(nofuse=True)
                    nc.vector.tensor_copy(pl[:, :].unsqueeze(1),
                                          pcols[:, :].rearrange("p (k l) -> p l k", l=L)[:, bass.ds(l, 1), :]
                                          ).then_inc(s_pl, 1)
                    for c, (o, w) in enumerate(chunks):
                        v.wait_ge(s_tp, l * CH + c + 1)
                        nc.vector.tensor_copy(zbuf[:, o:o + w], nps[:, c % NB, 0:w]).then_inc(s_st, 1)
                    with v.Fori(0, PAIRS) as k:
                        for s in range(2):
                            g = k * 2 + s
                            n = l * PAIRS + k
                            v.wait_ge(s_win[s], n + 1)
                            nc.vector.tensor_tensor(
                                hot[:, s, :, :], win[:, :].unsqueeze(1).to_broadcast([P, J, WIN]),
                                dloc[:, bass.ds(g * J, J)].unsqueeze(2).to_broadcast([P, J, WIN]),
                                ALU.is_equal).then_inc(s_hot[s], 1)
                            v.wait_ge(s_ea[s], (n + 1) * 16)
                            for h in range(2):
                                v.wait_ge(s_gx[s][h], (n + 1) * (8 * J))
                                i = nc.vector.tensor_tensor(
                                    msg[:, s, h * GE // 2:(h + 1) * GE // 2], gx[:, s, h * GE // 2:(h + 1) * GE // 2],
                                    ea[:, s, h * GE // 2:(h + 1) * GE // 2], ALU.add)
                            i.then_inc(s_add[s], 1)
                            v.wait_ge(s_add[s], n + 2)
                            nc.vector.tensor_copy(idx[:, s, :], srci[:, bass.ds((g + 2) * J, J)]
                                                  ).then_inc(s_idx[s], 1)
                            first = v.value_load(dsti[0:1, bass.ds(g * J, 1)], min_val=0, max_val=N - 1)
                            v.wait_ge(s_win[s], n + 2)
                            v.wait_ge(s_acc[1 - s], n + s + 1)
                            nc.vector.tensor_tensor(acc[:, bass.ds(first, WIN)], wps[s][:, 0:WIN],
                                                    acc[:, bass.ds(first, WIN)], ALU.add).then_inc(s_acc[s], 1)
                    v.nop(nofuse=True)
                    with v.If(flag > 0):
                        with v.Fori(0, G) as g:
                            m = l * G + g
                            v.wait_ge(s_acc[1], (l + 1) * PAIRS + 1)
                            nc.vector.tensor_copy(idg[:, :], srci[:, bass.ds(g * J, J)]).then_inc(g_idx, 1)
                            v.wait_ge(g_row, (m + 1) * (16 * J))
                            v.wait_ge(g_edge, (m + 1) * 16)
                            nc.vector.tensor_tensor(msg[:, 0, :], gx[:, 0, :], ea[:, 0, :], ALU.add).then_inc(g_msg, 1)
                            nc.vector.tensor_copy(dcur[:, :], dmiss[:, bass.ds(g * J, J)]).then_inc(g_msg, 1)
                            v.wait_ge(g_msg, (m + 1) * 2)
                            nc.vector.tensor_scalar(msg[:, 0, :], msg[:, 0, :], 0.0, None, ALU.max).then_inc(g_relu, 1)
                            with v.Fori(0, NW) as w:
                                q = m * NW + w
                                general_window(v, q, w, g_hot, g_win, g_acc, [(acc, wps[0], P)])
                    v.nop(nofuse=True)
                    for half in range(2):
                        for c, (o, w) in enumerate(chunks):
                            if half == 0:
                                v.wait_ge(s_z1e, l * CH + c + 1)
                                last = nc.vector.bn_stats(stats[:, c, :], zbuf[:, o:o + real[c]])
                            else:
                                v.wait_ge(s_z2, l * CH + c + 2)
                                nc.vector.tensor_scalar(acc[:, o:o + real[c]], nps[:, c % NB, 0:real[c]],
                                                        pl[:, 3:4], None, ALU.add).then_inc(s_z2e, 1)
                                v.wait_ge(s_z2e, l * CH + c + 1)
                                last = nc.vector.bn_stats(stats[:, c, :], acc[:, o:o + real[c]])
                        link.step(last)
                        v.nop(nofuse=True)
                        link.step(nc.vector.bn_aggr(mv[:, :], stats[:, :, :].rearrange("p c s -> p (c s)")))
                        nc.vector.tensor_scalar(std[:, :], mv[:, 1:2], EPS, None, ALU.add).then_inc(s_bv, 1)
                        v.wait_ge(s_ba, l * 2 + half + 1)
                        link.step(nc.vector.reciprocal(std[:, :], std[:, :]))
                        nc.vector.tensor_tensor(scl[:, :], std[:, :], pl[:, 3 * half + 1:3 * half + 2],
                                                ALU.mult).then_inc(s_bv, 1)
                        v.wait_ge(s_bv, l * 6 + half * 3 + 3)
                        link.step(nc.vector.scalar_tensor_tensor(shf[:, :], mv[:, 0:1], -1.0, scl[:, :],
                                                                 ALU.mult, ALU.mult))
                        nc.vector.tensor_tensor(shf[:, :], shf[:, :], pl[:, 3 * half + 2:3 * half + 3],
                                                ALU.add).then_inc(s_bv, 1)
                    assert link.n == LINKS

            @block.scalar
            def _(a):
                with a.Fori(0, L) as l:
                    a.wait_ge(s_bv, l * 6 + 1)
                    for c, (o, w) in enumerate(chunks):
                        nc.scalar.activation(acc[:, o:o + real[c]], acc[:, o:o + real[c]], ACT.Relu,
                                             bias=shf[:, 0:1], scale=scl[:, 0:1]).then_inc(s_rl, 1)
                    with a.Fori(0, PAIRS) as k:
                        for s in range(2):
                            a.wait_ge(s_add[s], l * PAIRS + k + 2)
                            nc.scalar.activation(msg[:, s, :], msg[:, s, :], ACT.Relu).then_inc(s_msg[s], 1)
                    a.wait_ge(s_pl, l + 1)
                    for c, (o, w) in enumerate(chunks):
                        a.wait_ge(s_z1, l * CH + c + 1)
                        nc.scalar.activation(zbuf[:, o:o + w], nps[:, c % NB, 0:w], ACT.Identity,
                                             bias=pl[:, 0:1]).then_inc(s_z1e, 1)
                    a.wait_ge(s_bv, l * 6 + 2)
                    nc.scalar.activation(std[:, :], std[:, :], ACT.Sqrt).then_inc(s_ba, 1)
                    a.wait_ge(s_bv, l * 6 + 4)
                    for c, (o, w) in enumerate(chunks):
                        nc.scalar.activation(zbuf[:, o:o + real[c]], zbuf[:, o:o + real[c]], ACT.Relu,
                                             bias=shf[:, 0:1], scale=scl[:, 0:1]).then_inc(s_h1, 1)
                    a.wait_ge(s_bv, l * 6 + 5)
                    nc.scalar.activation(std[:, :], std[:, :], ACT.Sqrt).then_inc(s_ba, 1)

            @block.tensor
            def _(pe):
                flag = flag_on(pe)
                for s in range(2):
                    pe.sem_inc(s_win[s], 1)
                pe.sem_inc(s_z2, 1)
                with pe.Fori(0, L) as l:
                    for c, (o, w) in enumerate(chunks):
                        pe.wait_ge(s_rl, l * CH + c + 1)
                        if c >= NB:
                            pe.wait_ge(s_st, l * CH + c - NB + 1)
                        for t in range(w // P):
                            last = nc.tensor.transpose(nps[:, c % NB, t * P:(t + 1) * P],
                                                       acc[:, o + t * P:o + (t + 1) * P], ident[:, :])
                        last.then_inc(s_tp, 1)
                    with pe.Fori(0, PAIRS) as k:
                        for s in range(2):
                            n = l * PAIRS + k
                            pe.wait_ge(s_hot[s], n + 1)
                            pe.wait_ge(s_msg[s], n + 1)
                            pe.wait_ge(s_acc[s], n + 1)
                            for j in range(J):
                                last = nc.tensor.matmul(wps[s][:, 0:WIN], msg[:, s, j * D:(j + 1) * D],
                                                        hot[:, s, j, :], start=(j == 0), stop=(j == J - 1))
                            last.then_inc(s_win[s], 1)
                    for s in range(2):
                        pe.wait_ge(s_acc[s], (l + 1) * PAIRS + 1)
                    pe.nop(nofuse=True)
                    with pe.If(flag > 0):
                        with pe.Fori(0, G) as g:
                            pe.wait_ge(g_relu, l * G + g + 1)
                            pe.nop(nofuse=True)
                            with pe.Fori(0, NW) as w:
                                pe.wait_ge(g_hot, (l * G + g) * NW + w + 1)
                                for j in range(J):
                                    last = nc.tensor.matmul(wps[0][:, 0:WIN], msg[:, 0, j * D:(j + 1) * D],
                                                            hot[:, 0, j, :], start=(j == 0), stop=(j == J - 1))
                                last.then_inc(g_win, 1)
                        pe.wait_ge(g_acc, (l + 1) * (G * NW))
                        pe.nop(nofuse=True)
                    pe.wait_ge(s_st, (l + 1) * CH)
                    pe.wait_ge(s_w, (l + 1) * 32)
                    for c, (o, w) in enumerate(chunks):
                        if c >= NB:
                            pe.wait_ge(s_z1e, l * CH + c - NB + 1)
                        nc.tensor.matmul(nps[:, c % NB, 0:w], w1[:, :], acc[:, o:o + w],
                                         start=True, stop=True).then_inc(s_z1, 1)
                    pe.wait_ge(s_z1e, (l + 1) * CH)
                    for c, (o, w) in enumerate(chunks):
                        pe.wait_ge(s_h1, l * CH + c + 1)
                        if c >= NB:
                            pe.wait_ge(s_z2e, l * CH + c - NB + 1)
                        nc.tensor.matmul(nps[:, c % NB, 0:real[c]], w2[:, :], zbuf[:, o:o + real[c]],
                                         start=True, stop=True).then_inc(s_z2, 1)
                    pe.wait_ge(s_z2e, (l + 1) * CH)

        s_b2 = sem("s_b2")
        s_t2 = sem("s_t2")
        s_r2 = sem("s_r2")
        s_l2 = sem("s_l2")
        s_v2 = sem("s_v2")
        s_a2 = sem("s_a2")
        s_n2 = sem("s_n2")
        s_u2 = sem("s_u2")
        s_e2 = sem("s_e2")
        s_p2 = sem("s_p2")
        s_q2 = sem("s_q2")
        s_d2 = sem("s_d2")
        with nc.Block() as block:
            @block.scalar
            def _(a):
                for c, (o, w) in enumerate(chunks):
                    nc.scalar.activation(acc[:, o:o + real[c]], acc[:, o:o + real[c]], ACT.Identity,
                                         bias=shf[:, 0:1], scale=scl[:, 0:1]).then_inc(s_b2, 1)
                a.wait_ge(s_v2, 1)
                nc.scalar.activation(var[:, :], var[:, :], ACT.Sqrt).then_inc(s_a2, 1)
                for c, (o, w) in enumerate(chunks):
                    a.wait_ge(s_u2, c + 1)
                    nc.scalar.activation(acc[:, o:o + w], nps[:, c % 2, 0:w], ACT.Relu).then_inc(s_e2, 1)

            def project2(pe, c):
                o, w = chunks[c]
                pe.wait_ge(s_e2, c + 1)
                if c >= 2:
                    pe.wait_ge(s_q2, c - 1)
                for t in range(w // P):
                    nc.tensor.matmul(nps[:, 2 + c % 2, t * P:(t + 1) * P], acc[:, o + t * P:o + (t + 1) * P],
                                     wnT[:, :], start=True, stop=False)
                    last = nc.tensor.matmul(nps[:, 2 + c % 2, t * P:(t + 1) * P], ones[:, :], bp[:, :],
                                            start=False, stop=True)
                last.then_inc(s_p2, 1)

            @block.tensor
            def _(pe):
                for c, (o, w) in enumerate(chunks):
                    pe.wait_ge(s_b2, c + 1)
                    if c >= NB:
                        pe.wait_ge(s_r2, c - NB + 1)
                    for t in range(w // P):
                        last = nc.tensor.transpose(nps[:, c % NB, t * P:(t + 1) * P],
                                                   acc[:, o + t * P:o + (t + 1) * P], ident[:, :])
                    last.then_inc(s_t2, 1)
                pe.wait_ge(s_r2, CH)
                for c, (o, w) in enumerate(chunks):
                    pe.wait_ge(s_n2, (o + w) // P)
                    if c >= 2:
                        pe.wait_ge(s_e2, c - 1)
                    for t in range(w // P):
                        last = nc.tensor.transpose(nps[:, c % 2, t * P:(t + 1) * P], bN[:, o // P + t, :],
                                                   ident[:, :])
                    last.then_inc(s_u2, 1)
                    if c >= 1:
                        project2(pe, c - 1)
                project2(pe, CH - 1)

            @block.vector
            def _(v):
                link = Link(v, s_l2)
                for c, (o, w) in enumerate(chunks):
                    v.wait_ge(s_t2, c + 1)
                    nc.vector.tensor_tensor(xres[:, o // P:(o + w) // P, :],
                                            nps[:, c % NB, 0:w].rearrange("p (t d) -> p t d", d=D),
                                            xres[:, o // P:(o + w) // P, :], ALU.add).then_inc(s_r2, 1)
                v.wait_ge(s_r2, CH)
                layer_norm(v, link, s_v2, s_a2, s_n2, xres[:, :, :], bN)
                for c, (o, w) in enumerate(chunks):
                    v.wait_ge(s_p2, c + 1)
                    nc.vector.tensor_copy(zbuf[:, o:o + w], nps[:, 2 + c % 2, 0:w]).then_inc(s_q2, 1)

            @block.sync
            def _(sp):
                for c in range(CH):
                    sp.wait_ge(s_q2, c + 1)
                    for t, k, n, rows_ in node_rows(table2, c):
                        sp.dma_start(rows_, zN[0:n, t:t + k, :]).then_inc(s_d2, 16)
                sp.wait_ge(s_d2, 16 * ROWS)

        s_ef = [sem(f"s_ef{i}") for i in range(2)]
        s_rest3 = sem("s_rest3")
        s_ft = [sem(f"s_ft{i}") for i in range(2)]
        s_fs = [sem(f"s_fs{i}") for i in range(2)]
        s_pe = [sem(f"s_pe{i}") for i in range(2)]
        s_xp = [sem(f"s_xp{i}") for i in range(2)]
        s_lg = [sem(f"s_lg{i}") for i in range(2)]
        s_pr = sem("s_pr")
        s_id3 = [sem(f"s_id3{i}") for i in range(2)]
        s_g3 = [sem(f"s_g3{i}") for i in range(2)]
        s_ox = [sem(f"s_ox{i}") for i in range(2)]
        s_ol = [sem(f"s_ol{i}") for i in range(2)]
        with nc.Block() as block:
            @block.sync
            def _(sp):
                def load(k, s):
                    sp.wait_ge(s_ft[s], k + 1)
                    load_edges(sp, ea[:, s, 0:J * EF], ea64, 2 * k + s, s_ef[s], s_rest3, 16)

                with sp.Fori(0, PAIRS - 1) as k:
                    load(k, 0)
                    load(k, 1)
                load(PAIRS - 1, 0)
                load(PAIRS - 1, 1)

            @block.gpsimd
            def _(p):
                with p.Fori(0, PAIRS) as k:
                    for s in range(2):
                        p.wait_ge(s_id3[s], k + 1)
                        p.nop(nofuse=True)
                        for j in range(J):
                            nc.gpsimd.indirect_dma_start(
                                gx[:, s, j * D:(j + 1) * D], None, table2,
                                bass.IndirectOffsetOnAxis(ap=idx[:, s, j:j + 1], axis=0)).then_inc(s_g3[s], 16)

            @block.tensor
            def _(pe):
                for s in range(2):
                    pe.sem_inc(s_ft[s], 1)
                    pe.sem_inc(s_pe[s], 1)
                with pe.Fori(0, PAIRS) as k:
                    for s in range(2):
                        pe.wait_ge(s_ef[s], (k + 1) * 16)
                        pe.wait_ge(s_fs[s], k + 1)
                        for q in range(J // 2):
                            last = nc.tensor.transpose(tps[s][:, q * P:(q + 1) * P],
                                                       ea[:, s, q * P:(q + 1) * P], ident[:, :])
                        last.then_inc(s_ft[s], 1)
                        pe.wait_ge(s_fs[s], k + 2)
                        pe.wait_ge(s_xp[s], k + 1)
                        for q in range(J // 2):
                            last = nc.tensor.matmul(
                                nps[:, 2 * s + q // 2, (q % 2) * 2 * D:(q % 2 + 1) * 2 * D],
                                eft[:, s, q * P:(q + 1) * P], we2[:, :, :].rearrange("p a d -> p (a d)"),
                                start=True, stop=True)
                        last.then_inc(s_pe[s], 1)

            @block.vector
            def _(v):
                for s in range(2):
                    v.sem_inc(s_xp[s], 1)
                    v.sem_inc(s_lg[s], 1)
                for s in range(2):
                    nc.vector.tensor_copy(idx[:, s, :], srci[:, s * J:(s + 1) * J]).then_inc(s_id3[s], 1)
                with v.Fori(0, PAIRS) as k:
                    for s in range(2):
                        g = k * 2 + s
                        v.wait_ge(s_pe[s], k + 2)
                        v.wait_ge(s_g3[s], (k + 1) * (16 * J))
                        v.wait_ge(s_ox[s], (k + 1) * 16)
                        nc.vector.tensor_tensor(msg[:, s, :].rearrange("p (b c) -> p b c", b=2),
                                                nps[:, 2 * s:2 * s + 2, :],
                                                gx[:, s, :].rearrange("p (b c) -> p b c", b=2),
                                                ALU.add).then_inc(s_xp[s], 1)
                        v.wait_ge(s_xp[s], k + 2)
                        nc.vector.tensor_copy(idx[:, s, :], srci[:, bass.ds((g + 2) * J, J)]).then_inc(s_id3[s], 1)
                        v.wait_ge(s_lg[1 - s], k + s + 1)
                        nc.vector.tensor_tensor(prod[:, :].rearrange("p (j d) -> p j d", d=D),
                                                msg[:, s, :].rearrange("p (j d) -> p j d", d=D),
                                                attnb[:, :].unsqueeze(1).to_broadcast([P, J, D]),
                                                ALU.mult).then_inc(s_pr, 1)
                        v.wait_ge(s_pr, 2 * k + s + 1)
                        v.wait_ge(s_ol[s], (k + 1) * 16)
                        nc.vector.tensor_reduce(lg[:, s, :, :].rearrange("p j h -> p (j h)"),
                                                prod[:, :].rearrange("p (q d) -> p q d", d=HD), AX.X,
                                                ALU.add).then_inc(s_lg[s], 1)

            @block.scalar
            def _(a):
                for s in range(2):
                    a.sem_inc(s_fs[s], 1)
                    a.sem_inc(s_ox[s], 16)
                    a.sem_inc(s_ol[s], 16)
                with a.Fori(0, PAIRS) as k:
                    for s in range(2):
                        g = 2 * k + s
                        a.wait_ge(s_ft[s], k + 2)
                        a.wait_ge(s_pe[s], k + 1)
                        nc.scalar.copy(eft[:, s, :], tps[s][:, :]).then_inc(s_fs[s], 1)
                        a.wait_ge(s_xp[s], k + 2)
                        a.dma_start(xp_d[bass.ds(g * P, P), :], msg[:, s, :]).then_inc(s_ox[s], 16)
                        a.wait_ge(s_lg[s], k + 2)
                        a.dma_start(by_group(lg_d, g),
                                    lg[:, s, :, :].rearrange("p j h -> p (j h)")).then_inc(s_ol[s], 16)
                for s in range(2):
                    a.wait_ge(s_ox[s], (PAIRS + 1) * 16)
                    a.wait_ge(s_ol[s], (PAIRS + 1) * 16)

        m_free = sem("m_free")
        m_load = sem("m_load")
        m_cast = sem("m_cast")
        m_step = sem("m_step")
        m_node = sem("m_node")
        m_idx = sem("m_idx")
        m_row = sem("m_row")
        m_out = sem("m_out")
        STEPS = 6
        nodemax = rec[:, :].rearrange("p (t h) -> p t h", h=H)
        with nc.Block() as block:
            @block.sync
            def _(sp):
                flag = flag_on(sp)
                with sp.If(flag > 0):
                    with sp.Fori(0, E // CB) as c:
                        sp.wait_ge(m_free, c + 1)
                        sp.dma_start(ea[:, 0, 0:CB].bitcast(I32),
                                     dst[bass.ds(c * CB, CB)].partition_broadcast(P)).then_inc(m_load, 16)
                        sp.dma_start(ea[:, 1, 0:CB * H],
                                     lg_d[bass.ds(c * CB, CB), :].rearrange("f h -> (f h)").partition_broadcast(P)
                                     ).then_inc(m_load, 16)
                    sp.wait_ge(m_free, E // CB + 1)
                    sp.dma_start(nm_d.rearrange("(t p) h -> p t h", p=P), nodemax).then_inc(m_node, 16)
                    sp.wait_ge(m_node, 16)
                    sp.nop(nofuse=True)
                    with sp.Fori(0, G) as g:
                        sp.wait_ge(m_row, (g + 1) * (16 * J))
                        sp.dma_start(by_group(mx_d, g), lg[:, 0, :, :].rearrange("p j h -> p (j h)")
                                     ).then_inc(m_out, 16)
                    sp.wait_ge(m_out, G * 16)
                sp.nop(nofuse=True)

            @block.gpsimd
            def _(p):
                flag = flag_on(p)
                with p.If(flag > 0):
                    p.wait_ge(m_node, 16)
                    p.nop(nofuse=True)
                    with p.Fori(0, G) as g:
                        p.wait_ge(m_idx, g + 1)
                        p.nop(nofuse=True)
                        for j in range(J):
                            nc.gpsimd.indirect_dma_start(
                                lg[:, 0, j, :], None, nm_d,
                                bass.IndirectOffsetOnAxis(ap=idg[:, j:j + 1], axis=0)).then_inc(m_row, 16)
                p.nop(nofuse=True)

            @block.vector
            def _(v):
                flag = flag_on(v)
                with v.If(flag > 0):
                    v.sem_inc(m_free, 1)
                    nc.vector.memset(rec[:, :], -BIG)
                    with v.Fori(0, E // CB) as c:
                        v.wait_ge(m_load, (c + 1) * 32)
                        nc.vector.tensor_copy(gx[:, 0, 0:CB], ea[:, 0, 0:CB].bitcast(I32)).then_inc(m_cast, 1)
                        v.wait_ge(m_cast, c + 1)
                        v.nop(nofuse=True)
                        with v.Fori(0, NT) as t:
                            n = [(c * NT + t) * STEPS]

                            def step(i):
                                i.then_inc(m_step, 1)
                                n[0] = n[0] + 1
                                v.wait_ge(m_step, n[0])

                            step(nc.vector.tensor_scalar(gx[:, 0, CB:2 * CB], gx[:, 0, 0:CB], nodeid[:, 0:1],
                                                         2.0 * BIG, ALU.is_equal, ALU.mult))
                            step(nc.vector.tensor_scalar(gx[:, 0, CB:2 * CB], gx[:, 0, CB:2 * CB], BIG, None,
                                                         ALU.subtract))
                            step(nc.vector.tensor_tensor(
                                gx[:, 1, 0:CB * H].rearrange("p (h f) -> p h f", h=H),
                                gx[:, 0, CB:2 * CB].unsqueeze(1).to_broadcast([P, H, CB]),
                                ea[:, 1, 0:CB * H].rearrange("p (f h) -> p h f", h=H), ALU.min))
                            step(nc.vector.tensor_reduce(blockmax[:, :], gx[:, 1, 0:CB * H].rearrange(
                                "p (h f) -> p h f", h=H), AX.X, ALU.max))
                            step(nc.vector.tensor_tensor(rec[:, bass.ds(t * H, H)], rec[:, bass.ds(t * H, H)],
                                                         blockmax[:, :], ALU.max))
                            step(nc.vector.tensor_scalar(gx[:, 0, 0:CB], gx[:, 0, 0:CB], float(P), None,
                                                         ALU.subtract))
                        v.drain().then_inc(m_free, 1)
                    with v.Fori(0, G) as g:
                        v.wait_ge(m_free, E // CB + 1)
                        nc.vector.tensor_scalar(idg[:, :], dsti[:, bass.ds(g * J, J)], 0.0, None,
                                                ALU.max).then_inc(m_idx, 1)
                        v.wait_ge(m_out, (g + 1) * 16)
                v.nop(nofuse=True)

        s_la = sem("s_la")
        s_mx = sem("s_mx")
        s_l4 = sem("s_l4")
        s_t4 = sem("s_t4")
        s_v4 = sem("s_v4")
        s_a4 = sem("s_a4")
        s_o4 = sem("s_o4")
        g_scan = sem("g_scan")
        g_fix = sem("g_fix")
        lgE = bbuf[:, 0:SF * H].rearrange("p (f h) -> p f h", h=H)
        mxE = zbuf[:, 0:SF * H].rearrange("p (f h) -> p f h", h=H)
        with nc.Block() as block:
            @block.sync
            def _(sp):
                flag = flag_on(sp)
                sp.dma_start(bbuf[:, 0:SF * H], lg_d.rearrange("(p f) h -> p (f h)", f=SF)).then_inc(s_la, 16)
                with sp.If(flag > 0):
                    sp.wait_ge(g_scan, 1)
                    sp.dma_start(zbuf[:, 0:SF * H], mx_d.rearrange("(p f) h -> p (f h)", f=SF)).then_inc(s_mx, 16)
                sp.nop(nofuse=True)
                sp.wait_ge(s_a4, 1)
                sp.dma_start(ex_d.rearrange("(p f) h -> p (f h)", f=SF), zbuf[:, 0:SF * H]).then_inc(s_o4, 16)
                sp.wait_ge(s_o4, 16)

            @block.vector
            def _(v):
                flag = flag_on(v)
                link = Link(v, s_l4)
                link.step(nc.vector.tensor_tensor(cap[:, :], dedge[:, 1:SF + 2], dedge[:, 0:SF + 1], ALU.not_equal))
                link.step(nc.vector.tensor_scalar(cap[:, :], cap[:, :], -2.0 * BIG, BIG, ALU.mult, ALU.add))
                v.wait_ge(s_la, 16)
                for turn in range(2):
                    back = turn == 1
                    caps = cap[:, 1:SF + 1][:, ::-1] if back else cap[:, 0:SF]
                    data = mxE if back else lgE

                    def scans(initial):
                        for h in range(H):
                            i, o = data[:, :, h], mxE[:, :, h]
                            if back:
                                i, o = i[:, ::-1], o[:, ::-1]
                            last = nc.vector.tensor_tensor_scan(o, caps, i, initial(h), ALU.min, ALU.max)
                        link.step(last)

                    scans(lambda h: -BIG)
                    end = 0 if back else SF - 1
                    nc.vector.tensor_copy(pair[:, 0, :], mxE[:, end, :])
                    link.step(nc.vector.tensor_reduce(pair[:, 1, 0:1], caps, AX.X, ALU.min))
                    for h in range(1, H):
                        last = nc.vector.tensor_copy(pair[:, 1, h:h + 1], pair[:, 1, 0:1])
                    last.then_inc(s_v4, 1)
                    v.wait_ge(s_t4, 2 * turn + 1)
                    link.step(nc.vector.tensor_copy(rows[:, :, :],
                                                    tps[0][0:H, 0:2 * P].rearrange("h (a p) -> h a p", a=2)))
                    link.step(nc.vector.memset(carry[:, :], -BIG))
                    d0, d1, o = rows[:, 1, :], rows[:, 0, :], carry[:, 1:P + 1]
                    if back:
                        d0, d1, o = d0[:, ::-1], d1[:, ::-1], o[:, ::-1]
                    nc.vector.tensor_tensor_scan(o, d0, d1, -BIG, ALU.min, ALU.max).then_inc(s_v4, 1)
                    v.wait_ge(s_t4, 2 * turn + 2)
                    link.step(nc.vector.tensor_copy(carried[:, :], tps[1][:, 0:H]))
                    scans(lambda h: carried[:, h:h + 1])
                with v.If(flag > 0):
                    v.sem_inc(g_scan, 1)
                    v.wait_ge(s_mx, 16)
                    nc.vector.tensor_tensor(mxE, mxE, lgE, ALU.max).then_inc(g_fix, 1)
                    v.wait_ge(g_fix, 1)
                v.nop(nofuse=True)
                nc.vector.tensor_tensor(mxE, lgE, mxE, ALU.subtract).then_inc(s_v4, 1)

            @block.tensor
            def _(pe):
                for turn in range(2):
                    pe.wait_ge(s_v4, 2 * turn + 1)
                    nc.tensor.transpose(tps[0][0:H, 0:P], pair[:, 0, :], ident[:, :])
                    nc.tensor.transpose(tps[0][0:H, P:2 * P], pair[:, 1, :], ident[:, :]).then_inc(s_t4, 1)
                    pe.wait_ge(s_v4, 2 * turn + 2)
                    o = 2 if turn == 1 else 0
                    nc.tensor.transpose(tps[1][:, 0:H], carry[:, o:o + P], ident[0:H, 0:H]).then_inc(s_t4, 1)

            @block.scalar
            def _(a):
                a.wait_ge(s_v4, 5)
                nc.scalar.activation(mxE, mxE, ACT.Exp).then_inc(s_a4, 1)

        RING = 4
        s_x5 = [sem(f"s_x5{i}") for i in range(RING)]
        s_e5 = [sem(f"s_e5{i}") for i in range(RING)]
        s_m5 = [sem(f"s_m5{i}") for i in range(RING)]
        s_h5 = [sem(f"s_h5{i}") for i in range(2)]
        s_w5 = [sem(f"s_w5{i}") for i in range(2)]
        s_v5 = [sem(f"s_v5{i}") for i in range(2)]
        s_s5 = [sem(f"s_s5{i}") for i in range(2)]
        s_z5 = sem("s_z5")
        h_load, h_msg, h_hot, h_win, h_acc = (sem(f"h_{x}") for x in ("load", "msg", "hot", "win", "acc"))
        num = zbuf
        den = bbuf
        slot5 = [gx[:, 0, :], gx[:, 1, :], ea[:, 0, :], ea[:, 1, :]]

        def groups5(engine, body):
            with engine.Fori(0, G // RING) as k:
                for q in range(RING):
                    body(k, q)
            for q in range(G % RING):
                body(G // RING, q)

        def weigh(q, s):
            return nc.vector.tensor_tensor(
                msg[:, s, :].rearrange("p (q d) -> p q d", d=HD), slot5[q].rearrange("p (q d) -> p q d", d=HD),
                lg[:, q, :, :].rearrange("p j h -> p (j h)").unsqueeze(2).to_broadcast([P, J * H, HD]), ALU.mult)

        def products5(q, s):
            for j in range(J):
                nc.tensor.matmul(wps[s][:, 0:WIN], msg[:, s, j * D:(j + 1) * D], hot[:, s, j, :],
                                 start=(j == 0), stop=(j == J - 1))
            for j in range(J):
                last = nc.tensor.matmul(tps[s][0:H, 0:WIN], lg[:, q, j, :], hot[:, s, j, :],
                                        start=(j == 0), stop=(j == J - 1))
            return last

        with nc.Block() as block:
            @block.sync
            def _(sp):
                flag = flag_on(sp)

                def load(k, q):
                    g = k * RING + q
                    sp.wait_ge(s_m5[q], k + 1)
                    sp.dma_start(slot5[q], xp_d[bass.ds(g * P, P), :]).then_inc(s_x5[q], 16)
                    sp.wait_ge(s_w5[q % 2], k * 2 + q // 2 + 1)
                    sp.dma_start(lg[:, q, :, :].rearrange("p j h -> p (j h)"), by_group(ex_d, g)
                                 ).then_inc(s_e5[q], 16)

                groups5(sp, load)
                sp.nop(nofuse=True)
                with sp.If(flag > 0):
                    sp.wait_ge(s_s5[0], PAIRS + 1)
                    sp.wait_ge(s_s5[1], PAIRS + 1)
                    sp.nop(nofuse=True)
                    with sp.Fori(0, G) as g:
                        sp.wait_ge(h_acc, g * NW + 1)
                        sp.dma_start(slot5[0], xp_d[bass.ds(g * P, P), :]).then_inc(h_load, 16)
                        sp.dma_start(lg[:, 0, :, :].rearrange("p j h -> p (j h)"), by_group(ex_d, g)
                                     ).then_inc(h_load, 16)
                sp.nop(nofuse=True)

            @block.vector
            def _(v):
                flag = flag_on(v)
                for q in range(RING):
                    v.sem_inc(s_m5[q], 1)
                nc.vector.memset(num[:, 0:NP + WIN], 0.0)
                nc.vector.memset(den[0:H, 0:NP + WIN], 0.0).then_inc(s_z5, 1)

                def group(k, q):
                    g, s, n = k * RING + q, q % 2, k * 2 + q // 2
                    v.wait_ge(s_w5[s], n + 2)
                    nc.vector.tensor_tensor(
                        hot[:, s, :, :], win[:, :].unsqueeze(1).to_broadcast([P, J, WIN]),
                        dloc[:, bass.ds(g * J, J)].unsqueeze(2).to_broadcast([P, J, WIN]),
                        ALU.is_equal).then_inc(s_h5[s], 1)
                    v.wait_ge(s_x5[q], (k + 1) * 16)
                    v.wait_ge(s_e5[q], (k + 1) * 16)
                    weigh(q, s).then_inc(s_m5[q], 1)

                groups5(v, group)
                v.nop(nofuse=True)
                with v.If(flag > 0):
                    v.sem_inc(h_acc, 1)
                    v.wait_ge(s_s5[0], PAIRS + 1)
                    v.wait_ge(s_s5[1], PAIRS + 1)
                    v.nop(nofuse=True)
                    with v.Fori(0, G) as g:
                        v.wait_ge(h_load, (g + 1) * 32)
                        weigh(0, 0).then_inc(h_msg, 1)
                        nc.vector.tensor_copy(dcur[:, :], dmiss[:, bass.ds(g * J, J)]).then_inc(h_msg, 1)
                        v.wait_ge(h_msg, (g + 1) * 2)
                        v.nop(nofuse=True)
                        with v.Fori(0, NW) as w:
                            general_window(v, g * NW + w, w, h_hot, h_win, h_acc,
                                           [(num, wps[0], P), (den, tps[0], H)], credit=1)
                v.nop(nofuse=True)

            @block.tensor
            def _(pe):
                flag = flag_on(pe)
                for s in range(2):
                    pe.sem_inc(s_w5[s], 2)

                def group(k, q):
                    s, n = q % 2, k * 2 + q // 2
                    pe.wait_ge(s_h5[s], n + 1)
                    pe.wait_ge(s_m5[q], k + 2)
                    pe.wait_ge(s_v5[s], n + 1)
                    products5(q, s).then_inc(s_w5[s], 1)

                groups5(pe, group)
                pe.nop(nofuse=True)
                with pe.If(flag > 0):
                    pe.wait_ge(s_v5[0], PAIRS + 1)
                    pe.nop(nofuse=True)
                    with pe.Fori(0, G) as g:
                        pe.wait_ge(h_msg, (g + 1) * 2)
                        pe.nop(nofuse=True)
                        with pe.Fori(0, NW) as w:
                            pe.wait_ge(h_hot, g * NW + w + 1)
                            products5(0, 0).then_inc(h_win, 1)
                pe.nop(nofuse=True)

            @block.scalar
            def _(a):
                for s in range(2):
                    a.sem_inc(s_v5[s], 1)

                def group(k, q):
                    s, n = q % 2, k * 2 + q // 2
                    a.wait_ge(s_w5[s], n + 3)
                    a.wait_ge(s_s5[s], n + 1)
                    nc.scalar.copy(ev[:, s, 0, :], wps[s][:, 0:WIN])
                    nc.scalar.copy(ev[0:H, s, 1, :], tps[s][0:H, 0:WIN]).then_inc(s_v5[s], 1)

                groups5(a, group)

            @block.gpsimd
            def _(p):
                for s in range(2):
                    p.sem_inc(s_s5[s], 1)
                p.wait_ge(s_z5, 1)
                p.nop(nofuse=True)

                def group(k, q):
                    g, s, n = k * RING + q, q % 2, k * 2 + q // 2
                    first = p.value_load(dsti[0:1, bass.ds(g * J, 1)], min_val=0, max_val=N - 1)
                    p.wait_ge(s_v5[s], n + 2)
                    p.wait_ge(s_s5[1 - s], n + s + 1)
                    p.nop(nofuse=True)
                    nc.gpsimd.tensor_tensor(num[:, bass.ds(first, WIN)], ev[:, s, 0, :],
                                            num[:, bass.ds(first, WIN)], ALU.add)
                    nc.gpsimd.tensor_tensor(den[0:H, bass.ds(first, WIN)], ev[0:H, s, 1, :],
                                            den[0:H, bass.ds(first, WIN)], ALU.add).then_inc(s_s5[s], 1)

                groups5(p, group)

        s_k6 = sem("s_k6")
        s_q6 = sem("s_q6")
        s_j6 = sem("s_j6")
        s_i6 = sem("s_i6")
        s_d6 = sem("s_d6")
        s_f6 = sem("s_f6")
        s_v6 = sem("s_v6")
        s_p6 = sem("s_p6")
        s_h6 = sem("s_h6")
        s_l6 = sem("s_l6")
        s_y6 = sem("s_y6")
        s_a6 = sem("s_a6")
        s_n6 = sem("s_n6")
        s_g6 = sem("s_g6")
        s_b6 = sem("s_b6")
        s_o6 = sem("s_o6")
        s_out = sem("s_out")
        with nc.Block() as block:
            def project(pe, c):
                o, w = chunks[c]
                pe.wait_ge(s_v6, c + 1)
                if c >= 2:
                    pe.wait_ge(s_h6, c - 1)
                for t in range(w // P):
                    nc.tensor.matmul(wps[c % 2][:, t * P:(t + 1) * P], num[:, o + t * P:o + (t + 1) * P],
                                     woT[:, :], start=True, stop=False)
                    last = nc.tensor.matmul(wps[c % 2][:, t * P:(t + 1) * P], ones[:, :], bo[:, :],
                                            start=False, stop=True)
                last.then_inc(s_p6, 1)

            def spread(pe, c):
                o, w = chunks[c]
                pe.wait_ge(s_i6, c + 1)
                if c >= 2:
                    pe.wait_ge(s_f6, c - 1)
                nc.tensor.matmul(nps[:, 2 + c % 2, 0:w], selh[:, :], den[0:H, o:o + w],
                                 start=True, stop=True).then_inc(s_d6, 1)

            @block.tensor
            def _(pe):
                for t in range(NT):
                    last = nc.tensor.transpose(tps[0][:, t * H:(t + 1) * H], den[0:H, t * P:(t + 1) * P],
                                               ident[0:H, 0:H])
                last.then_inc(s_k6, 1)
                pe.wait_ge(s_q6, 2)
                for c, (o, w) in enumerate(chunks):
                    if c >= 2:
                        pe.wait_ge(s_i6, c - 1)
                    for t in range(w // P):
                        last = nc.tensor.transpose(nps[0:H, c % 2, t * P:(t + 1) * P],
                                                   rec[:, (o // P + t) * H:(o // P + t + 1) * H], ident[:, :])
                    last.then_inc(s_j6, 1)
                    if c >= 1:
                        spread(pe, c - 1)
                    if c >= 2:
                        project(pe, c - 2)
                spread(pe, CH - 1)
                if CH >= 2:
                    project(pe, CH - 2)
                project(pe, CH - 1)

            @block.gpsimd
            def _(p):
                nc.gpsimd.tensor_tensor(xres[:, :, :], xres[:, :, :],
                                        betb[:, :].unsqueeze(1).to_broadcast([P, NT, D]), ALU.add).then_inc(s_b6, 1)

            @block.vector
            def _(v):
                link = Link(v, s_l6)
                v.wait_ge(s_k6, 1)
                nc.vector.tensor_scalar(rec[:, :], tps[0][:, 0:NT * H], 1.0e-30, None, ALU.max).then_inc(s_q6, 1)
                v.wait_ge(s_q6, 1)
                nc.vector.reciprocal(rec[:, :], rec[:, :]).then_inc(s_q6, 1)
                for c, (o, w) in enumerate(chunks):
                    v.wait_ge(s_d6, c + 1)
                    nc.vector.tensor_tensor(num[:, o:o + w], num[:, o:o + w], nps[:, 2 + c % 2, 0:w],
                                            ALU.mult).then_inc(s_f6, 1)
                    v.wait_ge(s_f6, c + 1)
                    nc.vector.tensor_tensor(num[:, o:o + w], num[:, o:o + w], acc[:, o:o + w],
                                            ALU.add).then_inc(s_v6, 1)
                v.wait_ge(s_h6, CH)
                layer_norm(v, link, s_y6, s_a6, s_n6, aN, bN)
                v.wait_ge(s_b6, 1)
                for c, (o, w) in enumerate(chunks):
                    t0, t1 = o // P, (o + w) // P
                    v.wait_ge(s_n6, t1)
                    nc.vector.tensor_tensor(bN[:, t0:t1, :], bN[:, t0:t1, :],
                                            gamb[:, :].unsqueeze(1).to_broadcast([P, t1 - t0, D]),
                                            ALU.mult).then_inc(s_g6, 1)
                    v.wait_ge(s_g6, c + 1)
                    nc.vector.tensor_tensor(bN[:, t0:t1, :], bN[:, t0:t1, :], xres[:, t0:t1, :],
                                            ALU.add).then_inc(s_o6, 1)

            @block.scalar
            def _(a):
                def rows6(c):
                    o, w = chunks[c]
                    a.wait_ge(s_p6, c + 1)
                    nc.scalar.activation(acc[:, o:o + w], wps[c % 2][:, 0:w], ACT.Relu).then_inc(s_h6, 1)

                for c, (o, w) in enumerate(chunks):
                    a.wait_ge(s_j6, c + 1)
                    nc.scalar.copy(den[0:H, o:o + w], nps[0:H, c % 2, 0:w]).then_inc(s_i6, 1)
                    if c >= 3:
                        rows6(c - 3)
                for c in range(max(0, CH - 3), CH):
                    rows6(c)
                a.wait_ge(s_y6, 1)
                nc.scalar.activation(var[:, :], var[:, :], ACT.Sqrt).then_inc(s_a6, 1)

            @block.sync
            def _(sp):
                for c in range(CH):
                    sp.wait_ge(s_o6, c + 1)
                    for t, k, n, rows_ in node_rows(out, c):
                        sp.dma_start(rows_, bN[0:n, t:t + k, :]).then_inc(s_out, 16)
                sp.wait_ge(s_out, 16 * ROWS)


_INS = ["x", "src", "dst", "edge_attr_128", "edge_attr_64", "L0_gnn_W1", "L0_gnn_b1", "L0_gnn_g_mlp",
        "L0_gnn_be_mlp", "L0_gnn_W2", "L0_gnn_b2", "L0_gnn_g_out", "L0_gnn_be_out", "L1_gnn_W_proj_w",
        "L1_gnn_W_proj_b", "L1_gnn_attn_vec", "L1_gnn_W_out_w", "L1_gnn_W_out_b", "L1_gnn_ln_gamma",
        "L1_gnn_ln_beta"]


def kernel(**inputs):
    import concourse.bacc as bacc
    from concourse.bass_utils import run_bass_kernel_spmd

    nc = bacc.Bacc("TRN2", target_bir_lowering=False, num_devices=1)
    arrays, args = {}, []
    for name in _INS:
        a = np.ascontiguousarray(inputs[name])
        arrays[f"in_{name}"] = a
        args.append(nc.dram_tensor(f"in_{name}", a.shape, mybir.dt.from_np(a.dtype), kind="ExternalInput").ap())
    shape = inputs["x"].shape
    args.append(nc.dram_tensor("out_0", shape, F32, kind="ExternalOutput").ap())
    gnn_program(nc, *args)
    r = run_bass_kernel_spmd(nc, [arrays], core_ids=[0])
    return r.results[0]["out_0"]
```

```python
import numpy as np
import concourse.bass as bass
from concourse import mybir
from contextlib import ExitStack

F32 = mybir.dt.float32
I32 = mybir.dt.int32
I16 = mybir.dt.int16
BF16 = mybir.dt.bfloat16
ALU = mybir.AluOpType
ACT = mybir.ActivationFunctionType
AX = mybir.AxisListType

P = 128
EPS = 1e-5
BIG = 1.0e38


class Link:

    def __init__(self, engine, sem, start=0):
        self.engine, self.sem, self.start, self.n = engine, sem, start, 0

    def step(self, instruction):
        instruction.then_inc(self.sem, 1)
        self.n += 1
        self.engine.wait_ge(self.sem, self.start + self.n)


def gnn_program(nc, x, src, dst, ea128, ea64, W1, b1, g_mlp, be_mlp, W2, b2, g_out, be_out,
                Wproj, bproj, attn, Wout, bout, gamma, beta, out):
    N, D = x.shape
    E = ea128.shape[0]
    EF = ea64.shape[1]
    L = W1.shape[0]
    H, HD = attn.shape
    assert D == P and H * HD == P and EF * 2 == P

    J = 8
    GE = J * P
    G = -(-E // GE)
    assert G % 2 == 0
    PAIRS = G // 2
    REM = E - (G - 1) * GE
    RP, RJ = REM // J, REM % J
    assert RP > 0
    EP = G * GE
    NOWHERE = -1000000
    JT = J - 1
    WIN = 64
    NT = -(-N // P)
    NP = NT * P
    NLAST = N - (NT - 1) * P
    chunks = [(c, min(512, NP - c)) for c in range(0, NP, 512)]
    CH = len(chunks)
    real = [min(w, N - c) for c, w in chunks]
    NB = 4
    SF = EP // P
    SLAST = E - (P - 1) * SF
    assert 0 < SLAST
    DH = D + H
    AW = max(NP + WIN, SF * H, NT * DH)
    K = 4
    B = G // K
    R = G % K
    assert B >= 3 and R > 0 and R % 2 == 0
    RING = 3
    NW = -(-NP // WIN)
    UN = max(d for d in range(1, 9) if NT % d == 0)
    CB = max(d for d in range(1, 257) if E % d == 0)

    def dram(name, shape):
        return nc.dram_tensor(name, shape, F32).ap()

    table = dram("table", (N, D))
    table2 = dram("table2", (N, DH))
    xres_d = dram("xres_d", (P, NT * D))
    cap_d = dram("cap_d", (EP + 1,))
    xp_d = dram("xp_d", (G * P, J * D))
    lg_d = dram("lg_d", (EP, H))
    ex_d = dram("ex_d", (EP, H))

    nm_d = dram("nm_d", (NP, H))
    mx_d = dram("mx_d", (EP, H))

    ctx = ExitStack()
    with ctx:
        def sb(name, shape, dt=F32):
            return ctx.enter_context(nc.sbuf_tensor(name, shape, dt))

        def pb(name, shape):
            return ctx.enter_context(nc.psum_tensor(name, shape, F32))

        def sem(name):
            return ctx.enter_context(nc.semaphore(name))

        acc = sb("acc", [P, AW])
        zbuf = sb("zbuf", [P, AW])
        ring = sb("ring", [P, max(2 * NP, RING * K * GE)])
        bbuf = ring[:, 0:AW]
        xden = sb("xden", [P, NP + WIN])
        xres = xden[:, 0:NP].rearrange("p (t d) -> p t d", d=D)
        srci = sb("srci", [P, (G + 2) * J], I32)
        dsti = sb("dsti", [P, G * J], I32)
        dloc = sb("dloc", [P, G * J])
        idx = sb("idx", [P, 2, J], I32)
        gx = sb("gx", [P, 2, J * DH])
        ea = sb("ea", [P, 2, GE])
        msg = sb("msg", [P, 2, GE])
        hot = sb("hot", [P, 2, J, WIN])
        lg = sb("lg", [P, J, H])
        lgc = sb("lgc", [P, RING, K * J * H])
        exc = sb("exc", [P, RING, K * J * H])
        eft = sb("eft", [P, 2, GE // 2])
        win = sb("win", [P, WIN])
        rampi = sb("rampi", [P, P], I32)
        ident = sb("ident", [P, P])
        ones = sb("ones", [1, P])
        dmiss = sb("dmiss", [P, G * J])
        dcur = sb("dcur", [P, J])
        idg = sb("idg", [P, J], I32)
        onec = sb("onec", [P, 1])
        nodeid = sb("nodeid", [P, 1])
        blockmax = sb("blockmax", [P, H])
        bad = sb("bad", [P, 2])
        flagi = sb("flagi", [1, 1], I32)
        params = sb("params", [6 * L, D])
        pcols = sb("pcols", [P, 6 * L])
        pl = sb("pl", [P, 6])
        w1 = sb("w1", [P, D])
        w2 = sb("w2", [P, D])
        stats = sb("stats", [P, CH, 6])
        mv = sb("mv", [P, 2])
        std = sb("std", [P, 1])
        scl = sb("scl", [P, 1])
        shf = sb("shf", [P, 1])
        lnst = sb("lnst", [P, NT, 6])
        dif = sb("dif", [P, NT])
        var = sb("var", [P, NT])
        nmr = sb("nmr", [P, NT])
        rec = sb("rec", [P, NT * H])
        wp = sb("wp", [P, D + 2 * EF])
        wo = sb("wo", [P, D])
        wnT = sb("wnT", [P, D])
        we2 = sb("we2", [P, 2, D])
        woT = sb("woT", [P, D])
        bp = sb("bp", [1, D])
        bo = sb("bo", [1, D])
        gamb = sb("gamb", [P, D])
        betb = sb("betb", [P, D])
        dedge = ring[:, AW:AW + SF + 2].bitcast(I32)
        assert SF + 1 <= 2 * GE
        cap = msg[:, :, :].rearrange("p s e -> p (s e)")[:, 0:SF + 1]
        lgs = sb("lgs", [P, K * J, H])
        mxs = sb("mxs", [P, K * J, H])
        caps = sb("caps", [P, K * J + 1])
        capf = sb("capf", [H, 1])
        pair = sb("pair", [P, 2, H])
        rows = sb("rows", [H, 2, P])
        carry = sb("carry", [H, P + 2])
        carried = sb("carried", [P, H])
        mlast = sb("mlast", [H, 1])
        top = sb("top", [H, 1])
        fac = sb("fac", [H, 1])
        facp = sb("facp", [P, 1])
        attnc = sb("attnc", [P, 1])
        bpc = sb("bpc", [P, 1])
        srcc = sb("srcc", [P, 1])
        dsrc = sb("dsrc", [P, P])
        asel = sb("asel", [P, H])
        wna = sb("wna", [P, H])
        wea = sb("wea", [P, 2, H])
        bpa = sb("bpa", [1, H])
        selh = sb("selh", [H, D])

        wps = [pb(f"wps{i}", [P, 512]) for i in range(2)]
        nps = pb("nps", [P, NB, 512])
        tps = [pb(f"tps{i}", [P, 512]) for i in range(2)]

        accT = acc[:, 0:NP]
        zN = zbuf[:, 0:NP].rearrange("p (t d) -> p t d", d=D)
        PART = NT * 3 * D // 2
        assert AW + SF + 2 <= PART
        assert PART + NT * P // 2 <= max(2 * NP, RING * K * GE) and NP < 2 ** 15 and NT * P <= AW
        zp = ring[:, 0:PART].bitcast(BF16).rearrange("p (t i d) -> p t i d", i=3, d=D)
        tile0 = ring[:, PART:PART + NT * P // 2].bitcast(I16).rearrange("p (t e) -> p t e", e=P)
        shot = [zbuf[:, i * NT * P // 2:(i + 1) * NT * P // 2].bitcast(BF16).rearrange("p (t e) -> p t e", e=P)
                for i in range(2)]
        part = eft[:, :, :].rearrange("p s e -> p (s e)")[:, 0:UN * D].rearrange("p (t d) -> p t d", d=D)
        assert UN * D <= GE and NT // UN < PAIRS
        zX = zbuf[:, 0:NT * DH].rearrange("p (t c) -> p t c", c=DH)
        bN = bbuf[:, 0:NP].rearrange("p (t d) -> p t d", d=D)
        aN = acc[:, 0:NP].rearrange("p (t d) -> p t d", d=D)

        def by_group(t, g):
            return t[bass.ds(g * GE, GE), :].rearrange("(p j) f -> p (j f)", j=J)

        def load_edges(sp, tile, t, g, s_done, s_rest, rest):
            F = t.shape[1]
            if isinstance(g, int) and g == G - 1:
                if RJ:
                    sp.dma_start(tile[RP:RP + 1, 0:RJ * F],
                                 t[E - RJ:E, :].rearrange("(p j) f -> p (j f)", p=1)).then_inc(s_rest, 16)
                    sp.wait_ge(s_rest, rest)
                sp.dma_start(tile[0:RP, :],
                             t[g * GE:g * GE + RP * J, :].rearrange("(p j) f -> p (j f)", j=J)).then_inc(s_done, 16)
            else:
                sp.dma_start(tile, by_group(t, g)).then_inc(s_done, 16)

        def node_rows(t, c):
            o, w = chunks[c]
            whole = min(w, N - o) // P
            parts = []
            if whole:
                parts.append((o // P, whole, P, t[o:o + whole * P, :].rearrange("(t p) d -> p t d", p=P)))
            if whole * P < min(w, N - o):
                o += whole * P
                parts.append((o // P, 1, N - o, t[o:N, :].rearrange("(t p) d -> p t d", t=1)))
            return parts

        ROWS = sum(len(node_rows(table, c)) for c in range(CH))

        def layer_norm(v, link, s_v, s_a, s_n, src3, dst3):
            with v.Fori(0, NT // UN) as b:
                for u in range(UN):
                    last = nc.vector.bn_stats(lnst[:, bass.ds(b * UN + u, 1), :].rearrange("p t s -> p (t s)"),
                                              src3[:, bass.ds(b * UN + u, 1), :].rearrange("p t d -> p (t d)"))
            link.step(v.drain())
            me, ve, mo, vo = (lnst[:, :, i] for i in (1, 2, 4, 5))
            link.step(nc.vector.tensor_tensor(dif[:, :], me, mo, ALU.subtract))
            link.step(nc.vector.tensor_tensor(dif[:, :], dif[:, :], dif[:, :], ALU.mult))
            link.step(nc.vector.tensor_tensor(var[:, :], ve, vo, ALU.add))
            link.step(nc.vector.tensor_scalar(var[:, :], var[:, :], 1.0 / D, EPS, ALU.mult, ALU.add))
            nc.vector.scalar_tensor_tensor(var[:, :], dif[:, :], 0.25, var[:, :], ALU.mult, ALU.add).then_inc(s_v, 1)
            link.step(nc.vector.tensor_tensor(nmr[:, :], me, mo, ALU.add))
            v.wait_ge(s_a, 1)
            link.step(nc.vector.reciprocal(var[:, :], var[:, :]))
            link.step(nc.vector.scalar_tensor_tensor(nmr[:, :], nmr[:, :], -0.5, var[:, :], ALU.mult, ALU.mult))
            with v.Fori(0, NT // UN) as b:
                for u in range(UN):
                    t = b * UN + u
                    nc.vector.tensor_scalar(dst3[:, bass.ds(t, 1), :].rearrange("p t d -> p (t d)"),
                                            src3[:, bass.ds(t, 1), :].rearrange("p t d -> p (t d)"),
                                            var[:, bass.ds(t, 1)], nmr[:, bass.ds(t, 1)],
                                            ALU.mult, ALU.add).then_inc(s_n, 1)

        def flag_on(engine):
            return engine.value_load(flagi[0:1, 0:1], min_val=0, max_val=1)

        s_x = sem("s_x")
        s_ld = sem("s_ld")
        s_io = sem("s_io")
        s_l0 = sem("s_l0")
        s_v0 = sem("s_v0")
        s_a0 = sem("s_a0")
        s_t0 = sem("s_t0")
        s_e0 = sem("s_e0")
        s_c0 = sem("s_c0")
        LOADS = 20 + 2 * (RJ > 0)
        LN0 = 8
        s_nt0 = sem("s_nt0")
        s_de = sem("s_de")
        with nc.Block() as block:
            @block.sync
            def _(sp):
                for c in range(CH):
                    for t, k, n, v in node_rows(x, c):
                        if n < P:
                            sp.wait_ge(s_io, 1)
                        sp.dma_start(xres[0:n, t:t + k, :], v).then_inc(s_x, 16)
                sp.wait_ge(s_io, 4)
                for tab, arr in ((srci, src), (dsti, dst)):
                    sp.dma_start(tab[:, 0:(G - 1) * J].rearrange("p (g j) -> p g j", j=J),
                                 arr[0:(G - 1) * GE].rearrange("(g p j) -> p g j", p=P, j=J)).then_inc(s_ld, 16)
                    last = tab[:, (G - 1) * J:G * J]
                    sp.dma_start(last[0:RP, :], arr[(G - 1) * GE:(G - 1) * GE + RP * J
                                                    ].rearrange("(p j) -> p j", j=J)).then_inc(s_ld, 16)
                    if RJ:
                        sp.dma_start(last[RP:RP + 1, 0:RJ], arr[E - RJ:E].unsqueeze(0)).then_inc(s_ld, 16)
                sp.dma_start(srci[:, G * J:(G + 2) * J].rearrange("p (g j) -> p g j", j=J),
                             src[0:2 * GE].rearrange("(g p j) -> p g j", p=P, j=J)).then_inc(s_ld, 16)
                for k, w in enumerate((b1, g_mlp, be_mlp, b2, g_out, be_out)):
                    sp.dma_start(params[k * L:(k + 1) * L, :], w).then_inc(s_ld, 16)
                sp.dma_start(wp[:, 0:D + EF], Wproj).then_inc(s_ld, 16)
                sp.dma_start(wp[:, D + EF:D + 2 * EF], Wproj[:, D:D + EF]).then_inc(s_ld, 16)
                sp.dma_start(wo[:, :], Wout).then_inc(s_ld, 16)
                sp.dma_start(bp[:, :], bproj.unsqueeze(0)).then_inc(s_ld, 16)
                sp.dma_start(bo[:, :], bout.unsqueeze(0)).then_inc(s_ld, 16)
                with nc.allow_non_contiguous_dma(reason="one word of each partition"):
                    sp.dma_start(attnc[:, :], attn.rearrange("h d -> (h d)").unsqueeze(1)).then_inc(s_ld, 16)
                    sp.dma_start(bpc[:, :], bproj.unsqueeze(1)).then_inc(s_ld, 16)
                sp.dma_start(gamb[:, :], gamma.partition_broadcast(P)).then_inc(s_ld, 16)
                sp.dma_start(betb[:, :], beta.partition_broadcast(P)).then_inc(s_ld, 16)
                sp.dma_start(dedge[0:P - 1, 1:SF + 1],
                             dst[0:(P - 1) * SF].rearrange("(p f) -> p f", f=SF)).then_inc(s_de, 16)
                sp.dma_start(dedge[P - 1:P, 1:SLAST + 1], dst[(P - 1) * SF:E].unsqueeze(0)).then_inc(s_de, 16)
                with nc.allow_non_contiguous_dma(reason="one word of each partition"):
                    sp.dma_start(dedge[1:P, 0:1], dst[0:(P - 1) * SF].rearrange("(p f) -> p f", f=SF)
                                 [:, SF - 1:SF]).then_inc(s_de, 16)
                    sp.dma_start(dedge[0:P - 2, SF + 1:SF + 2], dst[SF:(P - 1) * SF].rearrange("(p f) -> p f", f=SF)
                                 [:, 0:1]).then_inc(s_de, 16)
                    sp.dma_start(dedge[P - 2:P - 1, SF + 1:SF + 2],
                                 dst[(P - 1) * SF:(P - 1) * SF + 1].unsqueeze(0)).then_inc(s_de, 16)
                sp.wait_ge(s_ld, 16 * LOADS)
                sp.wait_ge(s_x, 16 * ROWS)
                sp.wait_ge(s_de, 16 * 5)

            @block.gpsimd
            def _(p):
                nc.gpsimd.memset(xres[:, NT - 1, :], 0.0).then_inc(s_io, 1)
                nc.gpsimd.memset(srci[:, (G - 1) * J:G * J], 0).then_inc(s_io, 1)
                nc.gpsimd.memset(dsti[:, (G - 1) * J:G * J], NOWHERE).then_inc(s_io, 1)
                nc.gpsimd.memset(dedge[:, :], N).then_inc(s_io, 1)
                nc.gpsimd.iota(rampi[:, :], [[1, P]], base=0, channel_multiplier=-1).then_inc(s_io, 1)
                nc.gpsimd.iota(win[:, :], [[1, WIN]], base=0, channel_multiplier=0,
                               allow_small_or_imprecise_dtypes=True).then_inc(s_io, 1)
                nc.gpsimd.memset(ones[:, :], 1.0).then_inc(s_io, 1)
                nc.gpsimd.memset(selh[:, :], 1.0).then_inc(s_io, 1)
                nc.gpsimd.memset(onec[:, :], 1.0).then_inc(s_io, 1)
                nc.gpsimd.iota(nodeid[:, :], [[0, 1]], base=0, channel_multiplier=1,
                               allow_small_or_imprecise_dtypes=True).then_inc(s_io, 1)
                p.wait_ge(s_io, 10)
                nc.gpsimd.affine_select(out=selh[:, :], in_=selh[:, :], compare_op=ALU.is_ge, fill=0.0, base=0,
                                        pattern=[[1, D]], channel_multiplier=-HD).then_inc(s_io, 1)
                p.wait_ge(s_io, 11)
                nc.gpsimd.affine_select(out=selh[:, :], in_=selh[:, :], compare_op=ALU.is_ge, fill=0.0,
                                        base=HD - 1, pattern=[[-1, D]], channel_multiplier=HD).then_inc(s_io, 1)
                nc.gpsimd.iota(tile0, [[P, NT], [0, P]], base=0, channel_multiplier=0).then_inc(s_io, 1)

            @block.vector
            def _(v):
                link = Link(v, s_l0)
                v.wait_ge(s_io, 12)
                nc.vector.tensor_scalar(ident[:, :], rampi[:, :], 0.0, None, ALU.is_equal).then_inc(s_c0, 1)
                nc.vector.memset(acc[:, NP:AW], 0.0)
                nc.vector.memset(wea[:, :, :], 0.0)
                nc.vector.memset(scl[:, :], 1.0)
                nc.vector.memset(shf[:, :], 0.0)
                link.step(nc.vector.memset(we2[:, :, :], 0.0))
                v.wait_ge(s_x, 16 * ROWS)
                layer_norm(v, link, s_v0, s_a0, s_nt0, xres[:, :, :], bN)
                assert link.n == LN0 + 1
                v.wait_ge(s_ld, 16 * LOADS)
                link.step(nc.vector.tensor_copy(dloc[:, :], dsti[:, :]))
                nc.vector.tensor_copy(dmiss[:, :], dsti[:, :])
                v.wait_ge(s_t0, CH + 1)
                link.step(nc.vector.tensor_tensor(
                    dloc[:, :].rearrange("p (g j) -> p g j", j=J), dloc[:, :].rearrange("p (g j) -> p g j", j=J),
                    wps[0][:, 0:G].unsqueeze(2).to_broadcast([P, G, J]), ALU.subtract))
                inside = cap[:, 0:G * J]
                link.step(nc.vector.tensor_scalar(inside, dloc[:, :], 0.0, None, ALU.is_ge))
                link.step(nc.vector.scalar_tensor_tensor(inside, dloc[:, :], float(WIN), inside, ALU.is_lt, ALU.mult))
                link.step(nc.vector.scalar_tensor_tensor(dmiss[:, :], inside, float(NOWHERE), dmiss[:, :],
                                                         ALU.mult, ALU.add))
                link.step(nc.vector.tensor_scalar(inside, dmiss[:, :], 0.0, None, ALU.is_ge))
                link.step(nc.vector.tensor_reduce(bad[:, 0:1], inside, AX.X, ALU.add))
                v.wait_ge(s_de, 16 * 5)
                link.step(nc.vector.tensor_tensor(cap[:, :], dedge[:, 1:SF + 2], dedge[:, 0:SF + 1], ALU.is_lt))
                link.step(nc.vector.memset(cap[0:1, 0:1], 0.0))
                link.step(nc.vector.tensor_reduce(bad[:, 1:2], cap[:, :], AX.X, ALU.add))
                nc.vector.tensor_tensor(bad[:, 0:1], bad[:, 0:1], bad[:, 1:2], ALU.add).then_inc(s_c0, 1)
                v.wait_ge(s_t0, CH + 3)
                nc.vector.tensor_scalar(flagi[:, :], wps[0][0:1, 511:512], 1.0, None, ALU.min)
                nc.vector.tensor_copy(pcols[:, :], wps[1][:, 0:6 * L])
                nc.vector.tensor_copy(wnT[:, :], tps[0][:, 0:P])
                nc.vector.tensor_copy(we2[0:EF, 0, :], tps[0][0:EF, P:2 * P])
                nc.vector.tensor_copy(we2[EF:P, 1, :], tps[0][EF:P, P:2 * P])
                nc.vector.tensor_copy(woT[:, :], tps[0][:, 2 * P:3 * P])
                nc.vector.tensor_scalar(asel[:, :], tps[1][:, 0:H], attnc[:, 0:1], None, ALU.mult).then_inc(s_c0, 1)
                v.wait_ge(s_t0, CH + 4)
                nc.vector.tensor_copy(wna[:, :], tps[1][:, 2 * H:3 * H])
                nc.vector.tensor_copy(wea[0:EF, 0, :], tps[1][0:EF, 3 * H:4 * H])
                nc.vector.tensor_copy(wea[EF:P, 1, :], tps[1][EF:P, 3 * H:4 * H])
                nc.vector.tensor_copy(bpa[:, :], tps[1][0:1, 4 * H:5 * H]).then_inc(s_c0, 1)

            @block.scalar
            def _(a):
                a.wait_ge(s_v0, 1)
                nc.scalar.activation(var[:, :], var[:, :], ACT.Sqrt).then_inc(s_a0, 1)
                for c, (o, w) in enumerate(chunks):
                    a.wait_ge(s_t0, 1 + c)
                    nc.scalar.activation(acc[:, o:o + w], nps[:, c % NB, 0:w], ACT.Relu).then_inc(s_e0, 1)

            @block.tensor
            def _(pe):
                pe.wait_ge(s_c0, 1)
                for c, (o, w) in enumerate(chunks):
                    pe.wait_ge(s_nt0, (o + w) // P)
                    if c >= NB:
                        pe.wait_ge(s_e0, c - NB + 1)
                    for t in range(w // P):
                        last = nc.tensor.transpose(nps[:, c % NB, t * P:(t + 1) * P], bN[:, o // P + t, :],
                                                   ident[:, :])
                    last.then_inc(s_t0, 1)
                pe.wait_ge(s_io, 12)
                pe.wait_ge(s_l0, LN0 + 2)
                firsts = dloc[0:1, :].rearrange("p (g j) -> p g j", j=J)[:, :, 0]
                nc.tensor.matmul(wps[0][:, 0:G], ones[0:1, :], firsts, start=True, stop=True).then_inc(s_t0, 1)
                pe.wait_ge(s_ld, 16 * LOADS)
                nc.tensor.transpose(wps[1][:, 0:6 * L], params[:, :], ident[0:6 * L, 0:6 * L])
                nc.tensor.transpose(tps[0][:, 0:P], wp[:, 0:D], ident[:, :])
                nc.tensor.transpose(tps[0][:, P:2 * P], wp[:, D:D + 2 * EF], ident[:, :])
                nc.tensor.transpose(tps[0][:, 2 * P:3 * P], wo[:, :], ident[:, :])
                nc.tensor.transpose(tps[1][:, 0:H], selh[:, :], ident[0:H, 0:H]).then_inc(s_t0, 1)
                pe.wait_ge(s_c0, 2)
                nc.tensor.matmul(wps[0][0:1, 511:512], bad[:, 0:1], onec[:, :], start=True, stop=True).then_inc(s_t0, 1)
                pe.wait_ge(s_c0, 3)
                nc.tensor.matmul(tps[1][:, 2 * H:3 * H], wp[:, 0:D], asel[:, :], start=True, stop=True)
                nc.tensor.matmul(tps[1][:, 3 * H:4 * H], wp[:, D:D + 2 * EF], asel[:, :], start=True, stop=True)
                nc.tensor.matmul(tps[1][0:1, 4 * H:5 * H], bpc[:, :], asel[:, :],
                                 start=True, stop=True).then_inc(s_t0, 1)

        s_w = sem("s_w")
        s_rl = sem("s_rl")
        s_tp = sem("s_tp")
        s_st = sem("s_st")
        s_tab = sem("s_tab")
        s_idx = [sem(f"s_idx{i}") for i in range(2)]
        s_gx = [[sem(f"s_gx{i}{h}") for h in range(2)] for i in range(2)]
        s_ea = [sem(f"s_ea{i}") for i in range(2)]
        s_rest = sem("s_rest")
        s_hot = [sem(f"s_hot{i}") for i in range(2)]
        s_add = [sem(f"s_add{i}") for i in range(2)]
        s_msg = [sem(f"s_msg{i}") for i in range(2)]
        s_win = [sem(f"s_win{i}") for i in range(2)]
        s_acc = [sem(f"s_acc{i}") for i in range(2)]
        s_z1 = sem("s_z1")
        s_z1e = sem("s_z1e")
        s_h1 = sem("s_h1")
        s_z2 = sem("s_z2")
        s_z2e = sem("s_z2e")
        s_bv = sem("s_bv")
        s_ba = sem("s_ba")
        s_l1 = sem("s_l1")
        s_pl = sem("s_pl")
        g_idx, g_row, g_edge, g_msg, g_relu = (sem(f"g_{x}") for x in ("idx", "row", "edge", "msg", "relu"))
        g_hot, g_win, g_acc, g_rest = (sem(f"g_{x}") for x in ("hot", "win", "acc", "rest"))
        s_cap = sem("s_cap")
        s_cd = sem("s_cd")
        s_hi = sem("s_hi")
        s_rr = sem("s_rr")
        s_mi = sem("s_mi")
        s_lo = sem("s_lo")
        SPLIT = NT // UN
        OWN = PAIRS - SPLIT
        assert OWN % 2 == 0 and OWN >= 4
        s_oc = sem("s_oc")
        s_ob = sem("s_ob")
        s_od = sem("s_od")
        s_oh = sem("s_oh")
        s_op = sem("s_op")
        s_os = sem("s_os")
        LINKS = 8

        def general_window(v, q, w, s_hot_, s_win_, s_acc_, sums, credit=0):
            nc.vector.tensor_tensor(hot[:, 0, :, :], win[:, :].unsqueeze(1).to_broadcast([P, J, WIN]),
                                    dcur[:, :].unsqueeze(2).to_broadcast([P, J, WIN]),
                                    ALU.is_equal).then_inc(s_hot_, 1)
            v.wait_ge(s_win_, q + 1)
            for sums_, product, n in sums:
                nc.vector.tensor_tensor(sums_[0:n, bass.ds(w * WIN, WIN)], product[0:n, 0:WIN],
                                        sums_[0:n, bass.ds(w * WIN, WIN)], ALU.add)
            nc.vector.tensor_scalar(dcur[:, :], dcur[:, :], float(WIN), None, ALU.subtract).then_inc(s_acc_, 1)
            v.wait_ge(s_acc_, q + 1 + credit)

        with nc.Block() as block:
            @block.sync
            def _(sp):
                flag = flag_on(sp)
                sp.wait_ge(s_cap, 2)
                sp.dma_start(cap_d[0:EP].rearrange("(p f) -> p f", f=SF), cap[:, 0:SF]).then_inc(s_cd, 16)
                sp.dma_start(cap_d[EP:EP + 1].unsqueeze(0), cap[P - 1:P, SF:SF + 1]).then_inc(s_cd, 16)
                with sp.Fori(0, L) as l:
                    sp.wait_ge(s_z2, l * CH + 1)
                    sp.dma_start(w1[:, :], W1[bass.ds(l, 1), :, :].rearrange("l i o -> (l i) o")).then_inc(s_w, 16)
                    sp.dma_start(w2[:, :], W2[bass.ds(l, 1), :, :].rearrange("l i o -> (l i) o")).then_inc(s_w, 16)
                    for c in range(CH):
                        sp.wait_ge(s_st, l * CH + c + 1)
                        for t, k, n, rows_ in node_rows(table, c):
                            sp.dma_start(rows_, zN[0:n, t:t + k, :]).then_inc(s_tab, 16)

                    def load(k, s):
                        sp.wait_ge(s_add[s], l * PAIRS + k + 1)
                        load_edges(sp, ea[:, s, :], ea128, 2 * k + s, s_ea[s], s_rest, (l + 1) * 16)

                    with sp.Fori(0, PAIRS - 1) as k:
                        load(k, 0)
                        load(k, 1)
                    load(PAIRS - 1, 0)
                    load(PAIRS - 1, 1)
                    sp.nop(nofuse=True)
                    with sp.If(flag > 0):
                        sp.wait_ge(s_acc[1], (l + 1) * PAIRS + 1)
                        sp.nop(nofuse=True)
                        with sp.Fori(0, G - 1) as g:
                            sp.wait_ge(g_idx, l * G + g + 1)
                            load_edges(sp, ea[:, 0, :], ea128, g, g_edge, g_rest, 0)
                        sp.wait_ge(g_idx, (l + 1) * G)
                        load_edges(sp, ea[:, 0, :], ea128, G - 1, g_edge, g_rest, (l + 1) * 16)
                    sp.nop(nofuse=True)
                sp.wait_ge(s_tab, L * ROWS * 16)
                sp.wait_ge(s_cd, 32)

            @block.gpsimd
            def _(p):
                flag = flag_on(p)

                def gathers(l, k, own):
                    for s in range(2):
                        p.wait_ge(s_idx[s], l * PAIRS + k + 1)
                        p.nop(nofuse=True)
                        for j in range(JT if own and s == 1 else J):
                            nc.gpsimd.indirect_dma_start(
                                gx[:, s, j * D:(j + 1) * D], None, table,
                                bass.IndirectOffsetOnAxis(ap=idx[:, s, j:j + 1], axis=0),
                            ).then_inc(s_gx[s][j // (J // 2)], 16)

                with p.Fori(0, L) as l:
                    p.wait_ge(s_tab, (l + 1) * (ROWS * 16))
                    p.nop(nofuse=True)
                    with p.Fori(0, SPLIT) as k:
                        gathers(l, k, False)
                    with p.Fori(0, OWN) as k:
                        gathers(l, k + SPLIT, True)
                    p.nop(nofuse=True)
                    with p.If(flag > 0):
                        with p.Fori(0, G) as g:
                            p.wait_ge(g_idx, l * G + g + 1)
                            p.nop(nofuse=True)
                            for j in range(J):
                                nc.gpsimd.indirect_dma_start(
                                    gx[:, 0, j * D:(j + 1) * D], None, table,
                                    bass.IndirectOffsetOnAxis(ap=idg[:, j:j + 1], axis=0)).then_inc(g_row, 16)
                    p.nop(nofuse=True)

            @block.vector
            def _(v):
                flag = flag_on(v)
                for s in range(2):
                    v.sem_inc(s_add[s], 1)
                    v.sem_inc(s_acc[s], 1)
                v.sem_inc(s_bv, 1)
                for s in range(2):
                    nc.vector.tensor_copy(idx[:, s, :], srci[:, s * J:(s + 1) * J]).then_inc(s_idx[s], 1)
                nc.vector.tensor_tensor(cap[:, :], dedge[:, 1:SF + 2], dedge[:, 0:SF + 1],
                                        ALU.not_equal).then_inc(s_cap, 1)
                v.wait_ge(s_cap, 1)
                nc.vector.tensor_scalar(cap[:, :], cap[:, :], -2.0 * BIG, BIG, ALU.mult, ALU.add).then_inc(s_cap, 1)

                def sources(k):
                    nc.vector.tensor_copy(srcc[:, :], srci[:, bass.ds((k * 2 + 1) * J + JT, 1)]).then_inc(s_oc, 1)

                def one_hot(l, k, u=0):
                    v.wait_ge(s_ob, l * (OWN + 1) + k + 1)
                    i = l * OWN + k + 1
                    nc.vector.tensor_scalar(dsrc[:, :], tps[0][:, 0:P], nodeid[:, 0:1], None,
                                            ALU.subtract).then_inc(s_od, 1)
                    v.wait_ge(s_od, i)
                    nc.vector.tensor_tensor(shot[u], dsrc[:, :].unsqueeze(1).to_broadcast([P, NT, P]), tile0,
                                            ALU.is_equal).then_inc(s_oh, 1)

                def messages(l, k, s, own, u=0):
                    g = k * 2 + s
                    n = l * PAIRS + k
                    v.wait_ge(s_win[s], n + 1)
                    nc.vector.tensor_tensor(
                        hot[:, s, :, :], win[:, :].unsqueeze(1).to_broadcast([P, J, WIN]),
                        dloc[:, bass.ds(g * J, J)].unsqueeze(2).to_broadcast([P, J, WIN]),
                        ALU.is_equal).then_inc(s_hot[s], 1)
                    v.wait_ge(s_ea[s], (n + 1) * 16)
                    if own and s == 1:
                        at = slice(JT * D, J * D)
                        i = l * OWN + k - SPLIT
                        v.wait_ge(s_op, i + 1)
                        nc.vector.tensor_copy(msg[:, s, at], nps[:, u, 2 * D:3 * D]).then_inc(s_os, 1)
                        for m, rows_ in enumerate((nps[:, u, D:2 * D], nps[:, u, 0:D], ea[:, s, at])):
                            v.wait_ge(s_os, i * 4 + m + 1)
                            nc.vector.tensor_tensor(msg[:, s, at], msg[:, s, at], rows_, ALU.add).then_inc(s_os, 1)
                    for h in range(2):
                        lo, hi = h * GE // 2, (JT * D if own and s == 1 and h == 1 else (h + 1) * GE // 2)
                        if s == 1 and h == 1:
                            each = 8 * J - 16 if own else 8 * J
                            before = 16 * SPLIT if own else 0
                            v.wait_ge(s_gx[s][h], l * (8 * J * PAIRS - 16 * OWN) + k * each + before + each)
                        else:
                            v.wait_ge(s_gx[s][h], (n + 1) * (8 * J))
                        i = nc.vector.tensor_tensor(msg[:, s, lo:hi], gx[:, s, lo:hi], ea[:, s, lo:hi], ALU.add)
                    i.then_inc(s_add[s], 1)
                    v.wait_ge(s_add[s], n + 2)
                    nc.vector.tensor_copy(idx[:, s, :], srci[:, bass.ds((g + 2) * J, J)]).then_inc(s_idx[s], 1)

                def add_up(l, k, s):
                    n = l * PAIRS + k
                    first = v.value_load(dsti[0:1, bass.ds((k * 2 + s) * J, 1)], min_val=0, max_val=N - 1)
                    v.wait_ge(s_win[s], n + 2)
                    v.wait_ge(s_acc[1 - s], n + s + 1)
                    nc.vector.tensor_tensor(acc[:, bass.ds(first, WIN)], wps[s][:, 0:WIN],
                                            acc[:, bass.ds(first, WIN)], ALU.add).then_inc(s_acc[s], 1)

                def own_pair(l, k, u, first=False, last=False):
                    messages(l, k + SPLIT, 0, True, u)
                    if not last:
                        one_hot(l, k + 1, 1 - u)
                        sources(k + SPLIT + 2)
                    if not first:
                        add_up(l, k + SPLIT - 1, 1)
                    messages(l, k + SPLIT, 1, True, u)
                    add_up(l, k + SPLIT, 0)

                with v.Fori(0, L) as l:
                    link = Link(v, s_l1, l * LINKS)
                    v.wait_ge(s_bv, l * 6 + 1)
                    v.nop(nofuse=True)
                    nc.vector.tensor_copy(pl[:, :].unsqueeze(1),
                                          pcols[:, :].rearrange("p (k l) -> p l k", l=L)[:, bass.ds(l, 1), :]
                                          ).then_inc(s_pl, 1)
                    for c, (o, w) in enumerate(chunks):
                        v.wait_ge(s_tp, l * CH + c + 1)
                        nc.vector.tensor_copy(zbuf[:, o:o + w], nps[:, c % NB, 0:w]).then_inc(s_st, 1)
                    v.wait_ge(s_cd, 32)
                    with v.Fori(0, SPLIT) as k:
                        messages(l, k, 0, False)
                        add_up(l, k, 0)
                        i = l * SPLIT + k
                        v.wait_ge(s_hi, i + 1)
                        nc.vector.tensor_tensor(part, zN[:, bass.ds(k * UN, UN), :], zp[:, bass.ds(k * UN, UN), 0, :],
                                                ALU.subtract).then_inc(s_rr, 1)
                        messages(l, k, 1, False)
                        add_up(l, k, 1)
                        v.wait_ge(s_mi, i + 1)
                        nc.vector.tensor_tensor(zp[:, bass.ds(k * UN, UN), 2, :], part,
                                                zp[:, bass.ds(k * UN, UN), 1, :], ALU.subtract).then_inc(s_lo, 1)
                    v.wait_ge(s_lo, (l + 1) * SPLIT)
                    sources(SPLIT)
                    one_hot(l, 0)
                    sources(SPLIT + 1)

                    own_pair(l, 0, 0, first=True)
                    with v.Fori(0, OWN // 2 - 1) as d:
                        own_pair(l, d * 2 + 1, 1)
                        own_pair(l, d * 2 + 2, 0)
                    own_pair(l, OWN - 1, 1, last=True)
                    add_up(l, PAIRS - 1, 1)
                    v.nop(nofuse=True)
                    with v.If(flag > 0):
                        with v.Fori(0, G) as g:
                            m = l * G + g
                            v.wait_ge(s_acc[1], (l + 1) * PAIRS + 1)
                            nc.vector.tensor_copy(idg[:, :], srci[:, bass.ds(g * J, J)]).then_inc(g_idx, 1)
                            v.wait_ge(g_row, (m + 1) * (16 * J))
                            v.wait_ge(g_edge, (m + 1) * 16)
                            nc.vector.tensor_tensor(msg[:, 0, :], gx[:, 0, 0:GE], ea[:, 0, :],
                                                    ALU.add).then_inc(g_msg, 1)
                            nc.vector.tensor_copy(dcur[:, :], dmiss[:, bass.ds(g * J, J)]).then_inc(g_msg, 1)
                            v.wait_ge(g_msg, (m + 1) * 2)
                            nc.vector.tensor_scalar(msg[:, 0, :], msg[:, 0, :], 0.0, None, ALU.max).then_inc(g_relu, 1)
                            with v.Fori(0, NW) as w:
                                q = m * NW + w
                                general_window(v, q, w, g_hot, g_win, g_acc, [(acc, wps[0], P)])
                    v.nop(nofuse=True)
                    for half in range(2):
                        for c, (o, w) in enumerate(chunks):
                            if half == 0:
                                v.wait_ge(s_z1e, l * CH + c + 1)
                                last = nc.vector.bn_stats(stats[:, c, :], zbuf[:, o:o + real[c]])
                            else:
                                v.wait_ge(s_z2, l * CH + c + 2)
                                nc.vector.tensor_scalar(acc[:, o:o + real[c]], nps[:, c % NB, 0:real[c]],
                                                        pl[:, 3:4], None, ALU.add).then_inc(s_z2e, 1)
                                v.wait_ge(s_z2e, l * CH + c + 1)
                                last = nc.vector.bn_stats(stats[:, c, :], acc[:, o:o + real[c]])
                        link.step(last)
                        v.nop(nofuse=True)
                        link.step(nc.vector.bn_aggr(mv[:, :], stats[:, :, :].rearrange("p c s -> p (c s)")))
                        nc.vector.tensor_scalar(std[:, :], mv[:, 1:2], EPS, None, ALU.add).then_inc(s_bv, 1)
                        v.wait_ge(s_ba, l * 2 + half + 1)
                        link.step(nc.vector.reciprocal(std[:, :], std[:, :]))
                        nc.vector.tensor_tensor(scl[:, :], std[:, :], pl[:, 3 * half + 1:3 * half + 2],
                                                ALU.mult).then_inc(s_bv, 1)
                        v.wait_ge(s_bv, l * 6 + half * 3 + 3)
                        link.step(nc.vector.scalar_tensor_tensor(shf[:, :], mv[:, 0:1], -1.0, scl[:, :],
                                                                 ALU.mult, ALU.mult))
                        nc.vector.tensor_tensor(shf[:, :], shf[:, :], pl[:, 3 * half + 2:3 * half + 3],
                                                ALU.add).then_inc(s_bv, 1)
                    assert link.n == LINKS

            @block.scalar
            def _(a):
                def relu(l, k, s):
                    a.wait_ge(s_add[s], l * PAIRS + k + 2)
                    nc.scalar.activation(msg[:, s, :], msg[:, s, :], ACT.Relu).then_inc(s_msg[s], 1)

                with a.Fori(0, L) as l:
                    a.wait_ge(s_bv, l * 6 + 1)
                    for c, (o, w) in enumerate(chunks):
                        nc.scalar.activation(acc[:, o:o + real[c]], acc[:, o:o + real[c]], ACT.Relu,
                                             bias=shf[:, 0:1], scale=scl[:, 0:1]).then_inc(s_rl, 1)
                    a.wait_ge(s_st, (l + 1) * CH)
                    a.wait_ge(s_cd, 32)
                    with a.Fori(0, SPLIT) as k:
                        nc.scalar.copy(zp[:, bass.ds(k * UN, UN), 0, :],
                                       zN[:, bass.ds(k * UN, UN), :]).then_inc(s_hi, 1)
                        relu(l, k, 0)
                        a.wait_ge(s_rr, l * SPLIT + k + 1)
                        a.nop(nofuse=True)
                        nc.scalar.copy(zp[:, bass.ds(k * UN, UN), 1, :], part).then_inc(s_mi, 1)
                        relu(l, k, 1)
                    with a.Fori(0, OWN) as k:
                        relu(l, k + SPLIT, 0)
                        relu(l, k + SPLIT, 1)
                    a.wait_ge(s_pl, l + 1)
                    for c, (o, w) in enumerate(chunks):
                        a.wait_ge(s_z1, l * CH + c + 1)
                        nc.scalar.activation(zbuf[:, o:o + w], nps[:, c % NB, 0:w], ACT.Identity,
                                             bias=pl[:, 0:1]).then_inc(s_z1e, 1)
                    a.wait_ge(s_bv, l * 6 + 2)
                    nc.scalar.activation(std[:, :], std[:, :], ACT.Sqrt).then_inc(s_ba, 1)
                    a.wait_ge(s_bv, l * 6 + 4)
                    for c, (o, w) in enumerate(chunks):
                        nc.scalar.activation(zbuf[:, o:o + real[c]], zbuf[:, o:o + real[c]], ACT.Relu,
                                             bias=shf[:, 0:1], scale=scl[:, 0:1]).then_inc(s_h1, 1)
                    a.wait_ge(s_bv, l * 6 + 5)
                    nc.scalar.activation(std[:, :], std[:, :], ACT.Sqrt).then_inc(s_ba, 1)

            @block.tensor
            def _(pe):
                flag = flag_on(pe)
                for s in range(2):
                    pe.sem_inc(s_win[s], 1)
                pe.sem_inc(s_z2, 1)

                def window(l, k, s):
                    n = l * PAIRS + k
                    pe.wait_ge(s_hot[s], n + 1)
                    pe.wait_ge(s_msg[s], n + 1)
                    pe.wait_ge(s_acc[s], n + 1)
                    for j in range(J):
                        last = nc.tensor.matmul(wps[s][:, 0:WIN], msg[:, s, j * D:(j + 1) * D], hot[:, s, j, :],
                                                start=(j == 0), stop=(j == J - 1))
                    last.then_inc(s_win[s], 1)

                def spread_sources(l, k):
                    pe.wait_ge(s_oc, l * (OWN + 1) + k + 1)
                    nc.tensor.matmul(tps[0][:, 0:P], srcc[:, :].to_broadcast([P, P]), ident[:, :],
                                     start=True, stop=True).then_inc(s_ob, 1)

                def gather_tile(l, k, u):
                    pe.wait_ge(s_oh, l * OWN + k + 1)
                    spread_sources(l, k + 1)
                    for t in range(NT):
                        last = nc.tensor.matmul(nps[:, u, 0:3 * D], shot[u][:, t, :],
                                                zp[:, t, :, :].rearrange("p i d -> p (i d)"),
                                                start=(t == 0), stop=(t == NT - 1))
                    last.then_inc(s_op, 1)

                with pe.Fori(0, L) as l:
                    for c, (o, w) in enumerate(chunks):
                        pe.wait_ge(s_rl, l * CH + c + 1)
                        if c >= NB:
                            pe.wait_ge(s_st, l * CH + c - NB + 1)
                        for t in range(w // P):
                            last = nc.tensor.transpose(nps[:, c % NB, t * P:(t + 1) * P],
                                                       acc[:, o + t * P:o + (t + 1) * P], ident[:, :])
                        last.then_inc(s_tp, 1)
                    with pe.Fori(0, SPLIT) as k:
                        window(l, k, 0)
                        window(l, k, 1)
                    spread_sources(l, 0)
                    gather_tile(l, 0, 0)

                    def own_pair(l, k, u):
                        window(l, k + SPLIT, 0)
                        gather_tile(l, k + 1, 1 - u)
                        window(l, k + SPLIT, 1)

                    own_pair(l, 0, 0)
                    with pe.Fori(0, OWN // 2 - 1) as d:
                        own_pair(l, d * 2 + 1, 1)
                        own_pair(l, d * 2 + 2, 0)
                    window(l, PAIRS - 1, 0)
                    window(l, PAIRS - 1, 1)
                    for s in range(2):
                        pe.wait_ge(s_acc[s], (l + 1) * PAIRS + 1)
                    pe.nop(nofuse=True)
                    with pe.If(flag > 0):
                        with pe.Fori(0, G) as g:
                            pe.wait_ge(g_relu, l * G + g + 1)
                            pe.nop(nofuse=True)
                            with pe.Fori(0, NW) as w:
                                pe.wait_ge(g_hot, (l * G + g) * NW + w + 1)
                                for j in range(J):
                                    last = nc.tensor.matmul(wps[0][:, 0:WIN], msg[:, 0, j * D:(j + 1) * D],
                                                            hot[:, 0, j, :], start=(j == 0), stop=(j == J - 1))
                                last.then_inc(g_win, 1)
                        pe.wait_ge(g_acc, (l + 1) * (G * NW))
                        pe.nop(nofuse=True)
                    pe.wait_ge(s_st, (l + 1) * CH)
                    pe.wait_ge(s_w, (l + 1) * 32)
                    for c, (o, w) in enumerate(chunks):
                        if c >= NB:
                            pe.wait_ge(s_z1e, l * CH + c - NB + 1)
                        nc.tensor.matmul(nps[:, c % NB, 0:w], w1[:, :], acc[:, o:o + w],
                                         start=True, stop=True).then_inc(s_z1, 1)
                    pe.wait_ge(s_z1e, (l + 1) * CH)
                    for c, (o, w) in enumerate(chunks):
                        pe.wait_ge(s_h1, l * CH + c + 1)
                        if c >= NB:
                            pe.wait_ge(s_z2e, l * CH + c - NB + 1)
                        nc.tensor.matmul(nps[:, c % NB, 0:real[c]], w2[:, :], zbuf[:, o:o + real[c]],
                                         start=True, stop=True).then_inc(s_z2, 1)
                    pe.wait_ge(s_z2e, (l + 1) * CH)

        s_b2 = sem("s_b2")
        s_t2 = sem("s_t2")
        s_r2 = sem("s_r2")
        s_l2 = sem("s_l2")
        s_v2 = sem("s_v2")
        s_a2 = sem("s_a2")
        s_n2 = sem("s_n2")
        s_u2 = sem("s_u2")
        s_e2 = sem("s_e2")
        s_p2 = sem("s_p2")
        s_q2 = sem("s_q2")
        s_d2 = sem("s_d2")
        with nc.Block() as block:
            @block.scalar
            def _(a):
                for c, (o, w) in enumerate(chunks):
                    nc.scalar.activation(acc[:, o:o + real[c]], acc[:, o:o + real[c]], ACT.Identity,
                                         bias=shf[:, 0:1], scale=scl[:, 0:1]).then_inc(s_b2, 1)
                a.wait_ge(s_v2, 1)
                nc.scalar.activation(var[:, :], var[:, :], ACT.Sqrt).then_inc(s_a2, 1)
                for c, (o, w) in enumerate(chunks):
                    a.wait_ge(s_u2, c + 1)
                    nc.scalar.activation(acc[:, o:o + w], nps[:, c % 2, 0:w], ACT.Relu).then_inc(s_e2, 1)

            def project2(pe, c):
                o, w = chunks[c]
                pe.wait_ge(s_e2, c + 1)
                if c >= 2:
                    pe.wait_ge(s_q2, c - 1)
                for t in range(w // P):
                    nc.tensor.matmul(nps[:, 2 + c % 2, t * P:(t + 1) * P], acc[:, o + t * P:o + (t + 1) * P],
                                     wnT[:, :], start=True, stop=False)
                    nc.tensor.matmul(nps[:, 2 + c % 2, t * P:(t + 1) * P], ones[:, :], bp[:, :],
                                     start=False, stop=True)
                    nc.tensor.matmul(wps[c % 2][:, t * H:(t + 1) * H], acc[:, o + t * P:o + (t + 1) * P],
                                     wna[:, :], start=True, stop=False)
                    last = nc.tensor.matmul(wps[c % 2][:, t * H:(t + 1) * H], ones[:, :], bpa[:, :],
                                            start=False, stop=True)
                last.then_inc(s_p2, 1)

            @block.tensor
            def _(pe):
                for c, (o, w) in enumerate(chunks):
                    pe.wait_ge(s_b2, c + 1)
                    if c >= NB:
                        pe.wait_ge(s_r2, c - NB + 1)
                    for t in range(w // P):
                        last = nc.tensor.transpose(nps[:, c % NB, t * P:(t + 1) * P],
                                                   acc[:, o + t * P:o + (t + 1) * P], ident[:, :])
                    last.then_inc(s_t2, 1)
                pe.wait_ge(s_r2, CH)
                for c, (o, w) in enumerate(chunks):
                    pe.wait_ge(s_n2, (o + w) // P)
                    if c >= 2:
                        pe.wait_ge(s_e2, c - 1)
                    for t in range(w // P):
                        last = nc.tensor.transpose(nps[:, c % 2, t * P:(t + 1) * P], bN[:, o // P + t, :],
                                                   ident[:, :])
                    last.then_inc(s_u2, 1)
                    if c >= 1:
                        project2(pe, c - 1)
                project2(pe, CH - 1)

            @block.vector
            def _(v):
                link = Link(v, s_l2)
                for c, (o, w) in enumerate(chunks):
                    v.wait_ge(s_t2, c + 1)
                    nc.vector.tensor_tensor(xres[:, o // P:(o + w) // P, :],
                                            nps[:, c % NB, 0:w].rearrange("p (t d) -> p t d", d=D),
                                            xres[:, o // P:(o + w) // P, :], ALU.add).then_inc(s_r2, 1)
                v.wait_ge(s_r2, CH)
                layer_norm(v, link, s_v2, s_a2, s_n2, xres[:, :, :], bN)
                for c, (o, w) in enumerate(chunks):
                    v.wait_ge(s_p2, c + 1)
                    t0, t1 = o // P, (o + w) // P
                    nc.vector.tensor_copy(zX[:, t0:t1, D:DH], wps[c % 2][:, 0:(t1 - t0) * H].rearrange(
                        "p (t h) -> p t h", h=H))
                    nc.vector.tensor_copy(zX[:, t0:t1, 0:D], nps[:, 2 + c % 2, 0:w].rearrange(
                        "p (t d) -> p t d", d=D)).then_inc(s_q2, 1)

            @block.sync
            def _(sp):
                sp.wait_ge(s_r2, CH)
                sp.dma_start(xres_d[:, :], xres[:, :, :].rearrange("p t d -> p (t d)")).then_inc(s_d2, 16)
                for c in range(CH):
                    sp.wait_ge(s_q2, c + 1)
                    for t, k, n, rows_ in node_rows(table2, c):
                        sp.dma_start(rows_, zX[0:n, t:t + k, :]).then_inc(s_d2, 16)
                sp.wait_ge(s_d2, 16 * (ROWS + 1))

        s_ef = [sem(f"s_ef{i}") for i in range(K)]
        s_ft = [sem(f"s_ft{i}") for i in range(2)]
        s_fs = [sem(f"s_fs{i}") for i in range(2)]
        s_pe = [sem(f"s_pe{i}") for i in range(2)]
        s_xp = [sem(f"s_xp{i}") for i in range(2)]
        s_id3 = [sem(f"s_id3{i}") for i in range(2)]
        s_g3 = [sem(f"s_g3{i}") for i in range(2)]
        s_keep = sem("s_keep")
        s_rest3 = sem("s_rest3")
        s_lgd = sem("s_lgd")
        s_lgs = sem("s_lgs")
        s_sub = sem("s_sub")
        s_exp = sem("s_exp")
        s_exd = sem("s_exd")
        s_exc = sem("s_exc")
        s_sr = sem("s_sr")
        s_sc = sem("s_sc")
        s_sl = sem("s_sl")
        s_fp = sem("s_fp")
        s_fc = sem("s_fc")
        s_f3 = sem("s_f3")
        s_h3 = [sem(f"s_h3{i}") for i in range(2)]
        s_m3 = [sem(f"s_m3{i}") for i in range(2)]
        s_w3 = [sem(f"s_w3{i}") for i in range(2)]
        s_a3 = [sem(f"s_a3{i}") for i in range(2)]
        s_z3 = sem("s_z3")
        num = zbuf
        den = xden[0:H, :]
        gx3 = gx[:, :, :].rearrange("p s (j c) -> p s j c", c=DH)
        LINKS3 = 12
        DENS, TURN, FACP = WIN, 2 * WIN, 2 * WIN + 2 * P

        assert RING == 3
        LOOPS = (B - 4) // RING

        def groups_of(b):
            return R if isinstance(b, int) and b == B else K

        def count(b, q):
            return b * (K // 2) + q // 2

        def ring_rows(m, q, n=1):
            return ring[:, (m * K + q) * GE:(m * K + q + n) * GE]

        def by_chunks(engine, rows, between, sums, after, ahead):
            def iteration(b, m):
                edge = isinstance(b, int)
                for q in range(K):
                    if not ahead:
                        if not (edge and b > B) and q < groups_of(b):
                            rows(b, m, q)
                    elif q + 1 < groups_of(b) and not (edge and b > B):
                        rows(b, m, q + 1)
                    elif q + 1 == K and not (edge and b >= B):
                        rows(b + 1, (m + 1) % RING, 0)
                    maxima = not (edge and (b < 1 or b > B + 1))
                    if maxima:
                        between(b - 1, q)
                    if not (edge and b < 2) and q < groups_of(b - 2 if edge else b):
                        sums(b - 2, (m - 2) % RING, q)
                    if maxima:
                        after(b - 1, q)

            if ahead:
                rows(0, 0, 0)
            for b in range(3):
                iteration(b, b)
            with engine.Fori(0, LOOPS) as k:
                for i in range(RING):
                    iteration(k * RING + 3 + i, i)
            for b in range(3 + LOOPS * RING, B + 3):
                iteration(b, b % RING)

        with nc.Block() as block:
            @block.sync
            def _(sp):
                flag = flag_on(sp)

                def features(b, q):
                    slot = ea[:, :, :].rearrange("p s e -> p (s e)")[:, q * J * EF:(q + 1) * J * EF]
                    if not (isinstance(b, int) and b == 0):
                        sp.wait_ge(s_ft[q % 2], count(b - 1, q) + 1)
                    load_edges(sp, slot, ea64, b * K + q, s_ef[q], s_rest3, 16)

                def logits(b, m):
                    n = groups_of(b)
                    for s in range(2):
                        sp.wait_ge(s_xp[s], count(b, n) + 1)
                    sp.dma_start(lg_d[bass.ds(b * (K * GE), n * GE), :].rearrange("(q p j) h -> p q (j h)", p=P, j=J),
                                 lgc[:, m, 0:n * J * H].rearrange("p (q c) -> p q c", q=n)).then_inc(s_lgd, 16)
                    sp.nop(nofuse=True)
                    with sp.If(flag > 0):
                        sp.dma_start(xp_d[bass.ds(b * (K * P), n * P), :].rearrange("(q p) c -> p q c", p=P),
                                     ring_rows(m, 0, n).rearrange("p (q c) -> p q c", q=n)).then_inc(s_keep, 16)
                        sp.wait_ge(s_keep, (b + 1) * 16)
                        sp.nop(nofuse=True)
                    sp.nop(nofuse=True)
                    f = n * J
                    sp.dma_start(caps[:, 0:f], cap_d[bass.ds(b * (K * GE), n * GE)].rearrange("(p f) -> p f", f=f)
                                 ).then_inc(s_lgs, 16)
                    with nc.allow_non_contiguous_dma(reason="one word of each partition"):
                        sp.dma_start(caps[:, f:f + 1], cap_d[bass.ds(b * (K * GE) + 1, n * GE)].rearrange(
                            "(p f) -> p f", f=f)[:, f - 1:f]).then_inc(s_lgs, 16)
                    sp.dma_start(capf[:, :], cap_d[bass.ds(b * (K * GE), 1)].partition_broadcast(H)
                                 ).then_inc(s_lgs, 16)
                    sp.wait_ge(s_lgd, (b + 1) * 16)
                    sp.dma_start(lgs[:, 0:f, :].rearrange("p f h -> p (f h)"),
                                 lg_d[bass.ds(b * (K * GE), n * GE), :].rearrange("(p f) h -> p (f h)", f=f)
                                 ).then_inc(s_lgs, 16)

                def exponentials(b, m):
                    n = groups_of(b)
                    sp.wait_ge(s_exd, (b + 1) * 16)
                    sp.dma_start(exc[:, m, 0:n * J * H].rearrange("p (q c) -> p q c", q=n),
                                 ex_d[bass.ds(b * (K * GE), n * GE), :].rearrange("(q p j) h -> p q (j h)", p=P, j=J)
                                 ).then_inc(s_exc, 16)

                def chunk(b, m):
                    edge = isinstance(b, int)
                    for q in range(2, groups_of(b)):
                        features(b, q)
                    if not (edge and b == 0):
                        logits(b - 1, (m - 1) % RING)
                    if not (edge and b == B):
                        for q in range(2):
                            features(b + 1, q)
                    if not (edge and b == 0):
                        exponentials(b - 1, (m - 1) % RING)

                features(0, 0)
                features(0, 1)
                for b in range(3):
                    chunk(b, b)
                with sp.Fori(0, LOOPS) as k:
                    for i in range(RING):
                        chunk(k * RING + 3 + i, i)
                for b in range(3 + LOOPS * RING, B + 1):
                    chunk(b, b % RING)
                logits(B, B % RING)
                exponentials(B, B % RING)
                sp.wait_ge(s_exc, (B + 1) * 16)

            @block.gpsimd
            def _(p):
                with p.Fori(0, PAIRS) as k:
                    for s in range(2):
                        p.wait_ge(s_id3[s], k + 1)
                        p.nop(nofuse=True)
                        for j in range(J):
                            nc.gpsimd.indirect_dma_start(
                                gx[:, s, j * DH:(j + 1) * DH], None, table2,
                                bass.IndirectOffsetOnAxis(ap=idx[:, s, j:j + 1], axis=0)).then_inc(s_g3[s], 16)

            @block.tensor
            def _(pe):
                for s in range(2):
                    pe.sem_inc(s_pe[s], 1)
                    pe.sem_inc(s_w3[s], 1)

                def rows_step(b, m, q):
                    s, n = q % 2, count(b, q)
                    pe.wait_ge(s_ef[q], (b + 1) * 16)
                    pe.wait_ge(s_xp[s], n + 1)
                    for t in range(J // 2):
                        last = nc.tensor.transpose(
                            tps[s][:, t * P:(t + 1) * P],
                            ea[:, :, :].rearrange("p s e -> p (s e)")[:, q * J * EF + t * P:q * J * EF + (t + 1) * P],
                            ident[:, :])
                    last.then_inc(s_ft[s], 1)
                    pe.wait_ge(s_fs[s], n + 1)
                    for t in range(J // 2):
                        nc.tensor.matmul(nps[:, 2 * s + t // 2, (t % 2) * 2 * D:(t % 2 + 1) * 2 * D],
                                         eft[:, s, t * P:(t + 1) * P], we2[:, :, :].rearrange("p a d -> p (a d)"),
                                         start=True, stop=True)
                        last = nc.tensor.matmul(tps[s][:, 2 * t * H:2 * (t + 1) * H],
                                                eft[:, s, t * P:(t + 1) * P],
                                                wea[:, :, :].rearrange("p a h -> p (a h)"), start=True, stop=True)
                    last.then_inc(s_pe[s], 1)

                def after_step(b, q):
                    if q < 2:
                        pe.wait_ge(s_sr, b * 4 + 2 * q + 1)
                        nc.tensor.transpose(wps[0][0:H, TURN:TURN + P], pair[:, 0, :], ident[:, :])
                        nc.tensor.transpose(wps[0][0:H, TURN + P:TURN + 2 * P], pair[:, 1, :],
                                            ident[:, :]).then_inc(s_sc, 1)

                def between_step(b, q):
                    turn = q - 1
                    if turn in (0, 1):
                        pe.wait_ge(s_sr, b * 4 + 2 * turn + 2)
                        pe.nop(nofuse=True)
                        nc.tensor.transpose(wps[turn][:, TURN:TURN + H], carry[:, 2 * turn:2 * turn + P],
                                            ident[0:H, 0:H]).then_inc(s_sc, 1)
                    if turn == 1:
                        pe.wait_ge(s_exp, b * 2 + 1)
                        pe.nop(nofuse=True)
                        nc.tensor.matmul(wps[0][:, FACP:FACP + 1], selh[:, :], fac[:, :],
                                         start=True, stop=True).then_inc(s_fp, 1)

                def sum_step(b, m, q):
                    s, n = q % 2, count(b, q)
                    pe.wait_ge(s_h3[s], n + 1)
                    pe.wait_ge(s_m3[s], n + 1)
                    pe.wait_ge(s_a3[s], n + 1)
                    for j in range(J):
                        nc.tensor.matmul(wps[s][:, 0:WIN], msg[:, s, j * D:(j + 1) * D], hot[:, s, j, :],
                                         start=(j == 0), stop=(j == J - 1))
                    for j in range(J):
                        last = nc.tensor.matmul(wps[s][0:H, DENS:DENS + WIN],
                                                exc[:, m, (q * J + j) * H:(q * J + j + 1) * H], hot[:, s, j, :],
                                                start=(j == 0), stop=(j == J - 1))
                    last.then_inc(s_w3[s], 1)

                by_chunks(pe, rows_step, between_step, sum_step, after_step, ahead=True)

            @block.vector
            def _(v):
                link = [Link(v, s_sl)]
                for s in range(2):
                    v.sem_inc(s_xp[s], 1)
                    v.sem_inc(s_a3[s], 1)
                for s in range(2):
                    nc.vector.tensor_copy(idx[:, s, :], srci[:, s * J:(s + 1) * J]).then_inc(s_id3[s], 1)
                nc.vector.memset(num[:, 0:NP + WIN], 0.0)
                nc.vector.memset(mlast[:, :], -BIG)
                nc.vector.memset(carry[:, :], -BIG)
                nc.vector.memset(den, 0.0).then_inc(s_z3, 1)
                v.wait_ge(s_z3, 1)

                def rows_step(b, m, q):
                    s, n = q % 2, count(b, q)
                    v.wait_ge(s_pe[s], n + 2)
                    v.wait_ge(s_g3[s], (n + 1) * (16 * J))
                    nc.vector.tensor_tensor(ring_rows(m, q).rearrange("p (j d) -> p j d", d=D),
                                            nps[:, 2 * s:2 * s + 2, :].rearrange("p b (j d) -> p (b j) d", d=D),
                                            gx3[:, s, :, 0:D], ALU.add)
                    nc.vector.tensor_tensor(
                        lgc[:, m, q * J * H:(q + 1) * J * H].rearrange("p (j h) -> p j h", h=H),
                        tps[s][:, 0:J * H].rearrange("p (j h) -> p j h", h=H),
                        gx3[:, s, :, D:DH], ALU.add).then_inc(s_xp[s], 1)
                    v.wait_ge(s_xp[s], n + 2)
                    nc.vector.tensor_copy(idx[:, s, :], srci[:, bass.ds((b * K + q + 2) * J, J)]).then_inc(s_id3[s], 1)

                def turn(b, back):
                    f = groups_of(b) * J
                    cp = caps[:, 1:f + 1][:, ::-1] if back else caps[:, 0:f]
                    data = mxs if back else lgs

                    def scans(initial):
                        for h in range(H):
                            i, o = data[:, 0:f, h], mxs[:, 0:f, h]
                            if back:
                                i, o = i[:, ::-1], o[:, ::-1]
                            last = nc.vector.tensor_tensor_scan(o, cp, i, initial(h), ALU.min, ALU.max)
                        return last
                    return f, cp, scans

                def maxima_ends(b, back):
                    f, cp, scans = turn(b, back)
                    link[0].step(scans(lambda h: -BIG))
                    end = 0 if back else f - 1
                    nc.vector.tensor_copy(pair[:, 0, :], mxs[:, end, :])
                    link[0].step(nc.vector.tensor_reduce(pair[:, 1, 0:1], cp, AX.X, ALU.min))
                    nc.vector.tensor_copy(pair[:, 1, 1:H], pair[:, 1, 0:1].to_broadcast([P, H - 1])).then_inc(s_sr, 1)

                def maxima_across(b, back):
                    v.wait_ge(s_sc, b * 4 + 2 * back + 1)
                    if not back:
                        nc.vector.tensor_copy(carry[:, 0:1], mlast[:, :])
                    link[0].step(nc.vector.tensor_copy(rows[:, :, :], wps[0][0:H, TURN:TURN + 2 * P].rearrange(
                        "h (a p) -> h a p", a=2)))
                    d0, d1, o = rows[:, 1, :], rows[:, 0, :], carry[:, 1:P + 1]
                    if back:
                        d0, d1, o = d0[:, ::-1], d1[:, ::-1], o[:, ::-1]
                    nc.vector.tensor_tensor_scan(o, d0, d1, -BIG if back else mlast[:, 0:1],
                                                 ALU.min, ALU.max).then_inc(s_sr, 1)
                    v.wait_ge(s_sr, b * 4 + 2 * back + 2)
                    if back:
                        link[0].step(nc.vector.scalar_tensor_tensor(top[:, :], carry[:, 1:2], capf[:, 0:1],
                                                                    carry[:, 0:1], ALU.min, ALU.max))
                        nc.vector.tensor_tensor(top[:, :], carry[:, 0:1], top[:, :], ALU.subtract).then_inc(s_sub, 1)
                    else:
                        link[0].step(nc.vector.tensor_copy(mlast[:, :], carry[:, P:P + 1]))

                def maxima_within(b, back):
                    f, cp, scans = turn(b, back)
                    v.wait_ge(s_sc, b * 4 + 2 * back + 2)
                    link[0].step(nc.vector.tensor_copy(carried[:, :], wps[int(back)][:, TURN:TURN + H]))
                    link[0].step(scans(lambda h: carried[:, h:h + 1]))
                    if back:
                        nc.vector.tensor_tensor(mxs[:, 0:f, :], lgs[:, 0:f, :], mxs[:, 0:f, :],
                                                ALU.subtract).then_inc(s_sub, 1)

                def between_step(b, q):
                    if q in (1, 2):
                        maxima_across(b, q == 2)

                def after_step(b, q):
                    if q == 0:
                        link[0] = Link(v, s_sl, b * LINKS3)
                        v.wait_ge(s_lgs, (b + 1) * 64)
                        maxima_ends(b, False)
                    if q == 1:
                        maxima_within(b, False)
                        maxima_ends(b, True)
                    if q == 2:
                        maxima_within(b, True)
                        assert link[0].n == LINKS3
                    if q == 3:
                        v.wait_ge(s_fp, b + 1)
                        nc.vector.tensor_copy(facp[:, :], wps[0][:, FACP:FACP + 1]).then_inc(s_fc, 1)

                def add_window(b, q):
                    s, n = q % 2, count(b, q)
                    first = v.value_load(dsti[0:1, bass.ds((b * K + q) * J, 1)], min_val=0, max_val=N - 1)
                    v.wait_ge(s_w3[s], n + 2)
                    v.wait_ge(s_a3[1 - s], n + s + 1)
                    nc.vector.tensor_tensor(num[:, bass.ds(first, WIN)], wps[s][:, 0:WIN],
                                            num[:, bass.ds(first, WIN)], ALU.add)
                    nc.vector.tensor_tensor(den[:, bass.ds(first, WIN)], wps[s][0:H, DENS:DENS + WIN],
                                            den[:, bass.ds(first, WIN)], ALU.add).then_inc(s_a3[s], 1)

                def sum_step(b, m, q):
                    s, n = q % 2, count(b, q)
                    start = isinstance(b, int) and b == 0
                    v.wait_ge(s_w3[s], n + 1)
                    nc.vector.tensor_tensor(
                        hot[:, s, :, :], win[:, :].unsqueeze(1).to_broadcast([P, J, WIN]),
                        dloc[:, bass.ds((b * K + q) * J, J)].unsqueeze(2).to_broadcast([P, J, WIN]),
                        ALU.is_equal).then_inc(s_h3[s], 1)
                    v.wait_ge(s_exc, (b + 1) * 16)
                    nc.vector.tensor_tensor(
                        msg[:, s, :].rearrange("p (q d) -> p q d", d=HD),
                        ring_rows(m, q).rearrange("p (q d) -> p q d", d=HD),
                        exc[:, m, q * J * H:(q + 1) * J * H].unsqueeze(2).to_broadcast([P, J * H, HD]),
                        ALU.mult).then_inc(s_m3[s], 1)
                    if q in (1, 2) and not (isinstance(b, int) and b == B):
                        v.wait_ge(s_sc, (b + 1) * 4 + 2 * q)
                    if q > 0:
                        add_window(b, q - 1)
                    elif not start:
                        add_window(b - 1, K - 1)
                        first = v.value_load(dsti[0:1, bass.ds(b * (K * J), 1)], min_val=0, max_val=N - 1)
                        v.wait_ge(s_fc, b + 1)
                        v.wait_ge(s_a3[(K - 1) % 2], count(b - 1, K - 1) + 2)
                        nc.vector.tensor_tensor(num[:, bass.ds(first, 1)], num[:, bass.ds(first, 1)],
                                                facp[:, 0:1], ALU.mult)
                        nc.vector.tensor_tensor(den[:, bass.ds(first, 1)], den[:, bass.ds(first, 1)],
                                                fac[:, :], ALU.mult).then_inc(s_f3, 1)
                        v.wait_ge(s_f3, b)

                by_chunks(v, rows_step, between_step, sum_step, after_step, ahead=False)
                add_window(B, R - 1)

            @block.scalar
            def _(a):
                def rows_step(b, m, q):
                    s, n = q % 2, count(b, q)
                    a.wait_ge(s_ft[s], n + 1)
                    a.wait_ge(s_pe[s], n + 1)
                    nc.scalar.copy(eft[:, s, :], tps[s][:, :]).then_inc(s_fs[s], 1)

                def between_step(b, q):
                    if q == 2:
                        f = groups_of(b) * J
                        a.wait_ge(s_sub, b * 2 + 1)
                        nc.scalar.activation(fac[:, :], top[:, :], ACT.Exp).then_inc(s_exp, 1)
                        a.wait_ge(s_sub, b * 2 + 2)
                        nc.scalar.activation(mxs[:, 0:f, :], mxs[:, 0:f, :], ACT.Exp).then_inc(s_exp, 1)
                        a.wait_ge(s_exp, b * 2 + 2)
                        a.dma_start(ex_d[bass.ds(b * (K * GE), f * P), :].rearrange("(p f) h -> p (f h)", f=f),
                                    mxs[:, 0:f, :].rearrange("p f h -> p (f h)")).then_inc(s_exd, 16)

                by_chunks(a, rows_step, between_step, lambda b, m, q: None, lambda b, q: None, ahead=True)

        m_free = sem("m_free")
        m_load = sem("m_load")
        m_cast = sem("m_cast")
        m_step = sem("m_step")
        m_node = sem("m_node")
        m_idx = sem("m_idx")
        m_row = sem("m_row")
        m_out = sem("m_out")
        STEPS = 6
        nodemax = rec[:, :].rearrange("p (t h) -> p t h", h=H)
        with nc.Block() as block:
            @block.sync
            def _(sp):
                flag = flag_on(sp)
                with sp.If(flag > 0):
                    with sp.Fori(0, E // CB) as c:
                        sp.wait_ge(m_free, c + 1)
                        sp.dma_start(ea[:, 0, 0:CB].bitcast(I32),
                                     dst[bass.ds(c * CB, CB)].partition_broadcast(P)).then_inc(m_load, 16)
                        sp.dma_start(ea[:, 1, 0:CB * H],
                                     lg_d[bass.ds(c * CB, CB), :].rearrange("f h -> (f h)").partition_broadcast(P)
                                     ).then_inc(m_load, 16)
                    sp.wait_ge(m_free, E // CB + 1)
                    sp.dma_start(nm_d.rearrange("(t p) h -> p t h", p=P), nodemax).then_inc(m_node, 16)
                    sp.wait_ge(m_node, 16)
                    sp.nop(nofuse=True)
                    with sp.Fori(0, G) as g:
                        sp.wait_ge(m_row, (g + 1) * (16 * J))
                        sp.dma_start(by_group(mx_d, g), lg[:, :, :].rearrange("p j h -> p (j h)")
                                     ).then_inc(m_out, 16)
                    sp.wait_ge(m_out, G * 16)
                sp.nop(nofuse=True)

            @block.gpsimd
            def _(p):
                flag = flag_on(p)
                with p.If(flag > 0):
                    p.wait_ge(m_node, 16)
                    p.nop(nofuse=True)
                    with p.Fori(0, G) as g:
                        p.wait_ge(m_idx, g + 1)
                        p.nop(nofuse=True)
                        for j in range(J):
                            nc.gpsimd.indirect_dma_start(
                                lg[:, j, :], None, nm_d,
                                bass.IndirectOffsetOnAxis(ap=idg[:, j:j + 1], axis=0)).then_inc(m_row, 16)
                p.nop(nofuse=True)

            @block.vector
            def _(v):
                flag = flag_on(v)
                with v.If(flag > 0):
                    v.sem_inc(m_free, 1)
                    nc.vector.memset(rec[:, :], -BIG)
                    with v.Fori(0, E // CB) as c:
                        v.wait_ge(m_load, (c + 1) * 32)
                        nc.vector.tensor_copy(gx[:, 0, 0:CB], ea[:, 0, 0:CB].bitcast(I32)).then_inc(m_cast, 1)
                        v.wait_ge(m_cast, c + 1)
                        v.nop(nofuse=True)
                        with v.Fori(0, NT) as t:
                            n = [(c * NT + t) * STEPS]

                            def step(i):
                                i.then_inc(m_step, 1)
                                n[0] = n[0] + 1
                                v.wait_ge(m_step, n[0])

                            step(nc.vector.tensor_scalar(gx[:, 0, CB:2 * CB], gx[:, 0, 0:CB], nodeid[:, 0:1],
                                                         2.0 * BIG, ALU.is_equal, ALU.mult))
                            step(nc.vector.tensor_scalar(gx[:, 0, CB:2 * CB], gx[:, 0, CB:2 * CB], BIG, None,
                                                         ALU.subtract))
                            step(nc.vector.tensor_tensor(
                                gx[:, 1, 0:CB * H].rearrange("p (h f) -> p h f", h=H),
                                gx[:, 0, CB:2 * CB].unsqueeze(1).to_broadcast([P, H, CB]),
                                ea[:, 1, 0:CB * H].rearrange("p (f h) -> p h f", h=H), ALU.min))
                            step(nc.vector.tensor_reduce(blockmax[:, :], gx[:, 1, 0:CB * H].rearrange(
                                "p (h f) -> p h f", h=H), AX.X, ALU.max))
                            step(nc.vector.tensor_tensor(rec[:, bass.ds(t * H, H)], rec[:, bass.ds(t * H, H)],
                                                         blockmax[:, :], ALU.max))
                            step(nc.vector.tensor_scalar(gx[:, 0, 0:CB], gx[:, 0, 0:CB], float(P), None,
                                                         ALU.subtract))
                        v.drain().then_inc(m_free, 1)
                    with v.Fori(0, G) as g:
                        v.wait_ge(m_free, E // CB + 1)
                        nc.vector.tensor_scalar(idg[:, :], dsti[:, bass.ds(g * J, J)], 0.0, None,
                                                ALU.max).then_inc(m_idx, 1)
                        v.wait_ge(m_out, (g + 1) * 16)
                v.nop(nofuse=True)

        s_la = sem("s_la")
        s_mx = sem("s_mx")
        g_sub = sem("g_sub")
        g_exp = sem("g_exp")
        g_exd = sem("g_exd")
        lgE = bbuf[:, 0:SF * H]
        mxE = zbuf[:, 0:SF * H]
        with nc.Block() as block:
            @block.sync
            def _(sp):
                flag = flag_on(sp)
                with sp.If(flag > 0):
                    sp.dma_start(lgE, lg_d.rearrange("(p f) h -> p (f h)", f=SF)).then_inc(s_la, 16)
                    sp.dma_start(mxE, mx_d.rearrange("(p f) h -> p (f h)", f=SF)).then_inc(s_mx, 16)
                    sp.wait_ge(g_exp, 1)
                    sp.dma_start(ex_d.rearrange("(p f) h -> p (f h)", f=SF), mxE).then_inc(g_exd, 16)
                    sp.wait_ge(g_exd, 16)
                sp.nop(nofuse=True)

            @block.vector
            def _(v):
                flag = flag_on(v)
                with v.If(flag > 0):
                    v.wait_ge(s_la, 16)
                    v.wait_ge(s_mx, 16)
                    nc.vector.tensor_tensor(mxE, mxE, lgE, ALU.max).then_inc(g_sub, 1)
                    v.wait_ge(g_sub, 1)
                    nc.vector.tensor_tensor(mxE, lgE, mxE, ALU.subtract).then_inc(g_sub, 1)
                v.nop(nofuse=True)

            @block.scalar
            def _(a):
                flag = flag_on(a)
                with a.If(flag > 0):
                    a.wait_ge(g_sub, 2)
                    nc.scalar.activation(mxE, mxE, ACT.Exp).then_inc(g_exp, 1)
                a.nop(nofuse=True)

        h_load, h_msg, h_hot, h_win, h_acc, h_zero = (
            sem(f"h_{x}") for x in ("load", "msg", "hot", "win", "acc", "zero"))
        with nc.Block() as block:
            @block.sync
            def _(sp):
                flag = flag_on(sp)
                with sp.If(flag > 0):
                    with sp.Fori(0, G) as g:
                        sp.wait_ge(h_acc, g * NW + 1)
                        sp.dma_start(ea[:, 0, :], xp_d[bass.ds(g * P, P), :]).then_inc(h_load, 16)
                        sp.dma_start(lg[:, :, :].rearrange("p j h -> p (j h)"), by_group(ex_d, g)
                                     ).then_inc(h_load, 16)
                sp.nop(nofuse=True)

            @block.vector
            def _(v):
                flag = flag_on(v)
                with v.If(flag > 0):
                    v.sem_inc(h_acc, 1)
                    nc.vector.memset(num[:, 0:NP + WIN], 0.0).then_inc(h_zero, 1)
                    nc.vector.memset(den, 0.0).then_inc(h_zero, 1)
                    v.wait_ge(h_zero, 2)
                    v.nop(nofuse=True)
                    with v.Fori(0, G) as g:
                        v.wait_ge(h_load, (g + 1) * 32)
                        nc.vector.tensor_tensor(
                            msg[:, 0, :].rearrange("p (q d) -> p q d", d=HD),
                            ea[:, 0, :].rearrange("p (q d) -> p q d", d=HD),
                            lg[:, :, :].rearrange("p j h -> p (j h)").unsqueeze(2).to_broadcast([P, J * H, HD]),
                            ALU.mult).then_inc(h_msg, 1)
                        nc.vector.tensor_copy(dcur[:, :], dsti[:, bass.ds(g * J, J)]).then_inc(h_msg, 1)
                        v.wait_ge(h_msg, (g + 1) * 2)
                        v.nop(nofuse=True)
                        with v.Fori(0, NW) as w:
                            general_window(v, g * NW + w, w, h_hot, h_win, h_acc,
                                           [(num, wps[0], P), (den, tps[0], H)], credit=1)
                v.nop(nofuse=True)

            @block.tensor
            def _(pe):
                flag = flag_on(pe)
                with pe.If(flag > 0):
                    with pe.Fori(0, G) as g:
                        pe.wait_ge(h_msg, (g + 1) * 2)
                        pe.nop(nofuse=True)
                        with pe.Fori(0, NW) as w:
                            pe.wait_ge(h_hot, g * NW + w + 1)
                            for j in range(J):
                                nc.tensor.matmul(wps[0][:, 0:WIN], msg[:, 0, j * D:(j + 1) * D], hot[:, 0, j, :],
                                                 start=(j == 0), stop=(j == J - 1))
                            for j in range(J):
                                last = nc.tensor.matmul(tps[0][0:H, 0:WIN], lg[:, j, :], hot[:, 0, j, :],
                                                        start=(j == 0), stop=(j == J - 1))
                            last.then_inc(h_win, 1)
                pe.nop(nofuse=True)

        s_k6 = sem("s_k6")
        s_q6 = sem("s_q6")
        s_j6 = sem("s_j6")
        s_i6 = sem("s_i6")
        s_d6 = sem("s_d6")
        s_f6 = sem("s_f6")
        s_v6 = sem("s_v6")
        s_p6 = sem("s_p6")
        s_h6 = sem("s_h6")
        s_l6 = sem("s_l6")
        s_y6 = sem("s_y6")
        s_a6 = sem("s_a6")
        s_n6 = sem("s_n6")
        s_g6 = sem("s_g6")
        s_b6 = sem("s_b6")
        s_o6 = sem("s_o6")
        s_out = sem("s_out")
        s_x6 = sem("s_x6")
        xback = ring[:, NP:2 * NP].rearrange("p (t d) -> p t d", d=D)
        with nc.Block() as block:
            def project(pe, c):
                o, w = chunks[c]
                pe.wait_ge(s_v6, c + 1)
                if c >= 2:
                    pe.wait_ge(s_h6, c - 1)
                for t in range(w // P):
                    nc.tensor.matmul(wps[c % 2][:, t * P:(t + 1) * P], num[:, o + t * P:o + (t + 1) * P],
                                     woT[:, :], start=True, stop=False)
                    last = nc.tensor.matmul(wps[c % 2][:, t * P:(t + 1) * P], ones[:, :], bo[:, :],
                                            start=False, stop=True)
                last.then_inc(s_p6, 1)

            def spread(pe, c):
                o, w = chunks[c]
                pe.wait_ge(s_i6, c + 1)
                if c >= 2:
                    pe.wait_ge(s_f6, c - 1)
                nc.tensor.matmul(nps[:, 2 + c % 2, 0:w], selh[:, :], den[0:H, o:o + w],
                                 start=True, stop=True).then_inc(s_d6, 1)

            @block.tensor
            def _(pe):
                for t in range(NT):
                    last = nc.tensor.transpose(tps[0][:, t * H:(t + 1) * H], den[0:H, t * P:(t + 1) * P],
                                               ident[0:H, 0:H])
                last.then_inc(s_k6, 1)
                pe.wait_ge(s_q6, 2)
                for c, (o, w) in enumerate(chunks):
                    if c >= 2:
                        pe.wait_ge(s_i6, c - 1)
                    for t in range(w // P):
                        last = nc.tensor.transpose(nps[0:H, c % 2, t * P:(t + 1) * P],
                                                   rec[:, (o // P + t) * H:(o // P + t + 1) * H], ident[:, :])
                    last.then_inc(s_j6, 1)
                    if c >= 1:
                        spread(pe, c - 1)
                    if c >= 2:
                        project(pe, c - 2)
                spread(pe, CH - 1)
                if CH >= 2:
                    project(pe, CH - 2)
                project(pe, CH - 1)

            @block.gpsimd
            def _(p):
                p.wait_ge(s_x6, 16)
                nc.gpsimd.tensor_tensor(xback, xback,
                                        betb[:, :].unsqueeze(1).to_broadcast([P, NT, D]), ALU.add).then_inc(s_b6, 1)

            @block.vector
            def _(v):
                link = Link(v, s_l6)
                v.wait_ge(s_k6, 1)
                nc.vector.tensor_scalar(rec[:, :], tps[0][:, 0:NT * H], 1.0e-30, None, ALU.max).then_inc(s_q6, 1)
                v.wait_ge(s_q6, 1)
                nc.vector.reciprocal(rec[:, :], rec[:, :]).then_inc(s_q6, 1)
                for c, (o, w) in enumerate(chunks):
                    v.wait_ge(s_d6, c + 1)
                    nc.vector.tensor_tensor(num[:, o:o + w], num[:, o:o + w], nps[:, 2 + c % 2, 0:w],
                                            ALU.mult).then_inc(s_f6, 1)
                    v.wait_ge(s_f6, c + 1)
                    nc.vector.tensor_tensor(num[:, o:o + w], num[:, o:o + w], acc[:, o:o + w],
                                            ALU.add).then_inc(s_v6, 1)
                v.wait_ge(s_h6, CH)
                layer_norm(v, link, s_y6, s_a6, s_n6, aN, bN)
                v.wait_ge(s_b6, 1)
                for c, (o, w) in enumerate(chunks):
                    t0, t1 = o // P, (o + w) // P
                    v.wait_ge(s_n6, t1)
                    nc.vector.tensor_tensor(bN[:, t0:t1, :], bN[:, t0:t1, :],
                                            gamb[:, :].unsqueeze(1).to_broadcast([P, t1 - t0, D]),
                                            ALU.mult).then_inc(s_g6, 1)
                    v.wait_ge(s_g6, c + 1)
                    nc.vector.tensor_tensor(bN[:, t0:t1, :], bN[:, t0:t1, :], xback[:, t0:t1, :],
                                            ALU.add).then_inc(s_o6, 1)

            @block.scalar
            def _(a):
                def rows6(c):
                    o, w = chunks[c]
                    a.wait_ge(s_p6, c + 1)
                    nc.scalar.activation(acc[:, o:o + w], wps[c % 2][:, 0:w], ACT.Relu).then_inc(s_h6, 1)

                for c, (o, w) in enumerate(chunks):
                    a.wait_ge(s_j6, c + 1)
                    nc.scalar.copy(den[0:H, o:o + w], nps[0:H, c % 2, 0:w]).then_inc(s_i6, 1)
                    if c >= 3:
                        rows6(c - 3)
                for c in range(max(0, CH - 3), CH):
                    rows6(c)
                a.wait_ge(s_y6, 1)
                nc.scalar.activation(var[:, :], var[:, :], ACT.Sqrt).then_inc(s_a6, 1)

            @block.sync
            def _(sp):
                sp.dma_start(ring[:, NP:2 * NP], xres_d[:, :]).then_inc(s_x6, 16)
                for c in range(CH):
                    sp.wait_ge(s_o6, c + 1)
                    for t, k, n, rows_ in node_rows(out, c):
                        sp.dma_start(rows_, bN[0:n, t:t + k, :]).then_inc(s_out, 16)
                sp.wait_ge(s_out, 16 * ROWS)


_INS = ["x", "src", "dst", "edge_attr_128", "edge_attr_64", "L0_gnn_W1", "L0_gnn_b1", "L0_gnn_g_mlp",
        "L0_gnn_be_mlp", "L0_gnn_W2", "L0_gnn_b2", "L0_gnn_g_out", "L0_gnn_be_out", "L1_gnn_W_proj_w",
        "L1_gnn_W_proj_b", "L1_gnn_attn_vec", "L1_gnn_W_out_w", "L1_gnn_W_out_b", "L1_gnn_ln_gamma",
        "L1_gnn_ln_beta"]


def kernel(**inputs):
    import concourse.bacc as bacc
    from concourse.bass_utils import run_bass_kernel_spmd

    nc = bacc.Bacc("TRN2", target_bir_lowering=False, num_devices=1)
    arrays, args = {}, []
    for name in _INS:
        a = np.ascontiguousarray(inputs[name])
        arrays[f"in_{name}"] = a
        args.append(nc.dram_tensor(f"in_{name}", a.shape, mybir.dt.from_np(a.dtype), kind="ExternalInput").ap())
    shape = inputs["x"].shape
    args.append(nc.dram_tensor("out_0", shape, F32, kind="ExternalOutput").ap())
    gnn_program(nc, *args)
    r = run_bass_kernel_spmd(nc, [arrays], core_ids=[0])
    return r.results[0]["out_0"]
```
